# Optimizing a Trainium2 kernel written in Bass

```python
import numpy as np
import jax
import jax.numpy as jnp

def _softmax(x, axis=-1):
    return jax.nn.softmax(x, axis=axis)

def _gelu(x):
    return jax.nn.gelu(x, approximate=True)

def _silu(x):
    return jax.nn.silu(x)

def _sigmoid(x):
    return jax.nn.sigmoid(x)

def _layernorm(x, axis=-1, eps=1e-05):
    m = jnp.mean(x, axis=axis, keepdims=True)
    v = jnp.var(x, axis=axis, keepdims=True)
    return (x - m) / jnp.sqrt(v + eps)

def _scatter_add(tgt, idx, src, axis=0):
    return tgt.at[idx].add(src)

def _segment_sum(src, seg, n):
    return jax.ops.segment_sum(src, seg, n)
kernel_name = 'mk_gnn_ffn_d1_gnn_r8_47f282'

def setup_inputs(seed: int=0):
    np.random.seed(seed)
    _w = jnp.asarray

    def _rec_inputs():
        import jax
        import jax.numpy as jnp
        _gk = jax.random.key(seed)
        x = -0.0003713 + 1 * jax.random.normal(jax.random.fold_in(_gk, 1), (6250, 256), jnp.float32)
        src = jax.random.randint(jax.random.fold_in(_gk, 2), (100000,), 0, 6250, jnp.int32)
        dst = jnp.minimum((6250 * jax.random.uniform(jax.random.fold_in(_gk, 3), (100000,)) ** 2.0).astype(jnp.int32), 49999)
        _o = jnp.argsort(dst, stable=True)
        src = src[_o]
        dst = dst[_o]
        edge_type_16 = jax.random.randint(jax.random.fold_in(_gk, 12), (100000,), 0, 16, jnp.int32)
        edge_weight = jax.random.uniform(jax.random.fold_in(_gk, 13), (100000,), jnp.float32, 0.0, 0.999999)
        return (x, src, dst, edge_type_16, edge_weight)
    x, src, dst, edge_type_16, edge_weight = _rec_inputs()

    def _L0_gnn_setup():
        import jax, jax.numpy as jnp
        import numpy as np
        N = 6250
        E = 100000
        D = 256
        R = 16
        B = 8
        LN_EPS = 1e-05

        def _layer_norm(x, g, b):
            mu = jnp.mean(x, axis=-1, keepdims=True)
            var = jnp.mean(jnp.square(x - mu), axis=-1, keepdims=True)
            return (x - mu) * jax.lax.rsqrt(var + LN_EPS) * g + b

        def _rgcn_layer(x, edge_index, edge_type, edge_attr, basis, att, root, bias):
            n = x.shape[0]
            r = att.shape[0]
            weight = jnp.einsum('rb,bio->rio', att, basis)
            H = jnp.einsum('ni,rio->nro', x, weight)
            loop = jnp.arange(n, dtype=edge_index.dtype)
            src = jnp.concatenate([edge_index[0], loop])
            dst = jnp.concatenate([edge_index[1], loop])
            et = jnp.concatenate([edge_type, jnp.full((n,), r - 1, dtype=edge_type.dtype)])
            ea = jnp.concatenate([edge_attr, jnp.ones((n,), dtype=x.dtype)])
            msg = H[src, et] * ea[:, None]
            summ = jax.ops.segment_sum(msg, dst, num_segments=n)
            cnt = jax.ops.segment_sum(jnp.ones_like(ea), dst, num_segments=n)
            agg = summ / cnt[:, None]
            return agg + x @ root + bias
        key = jax.random.key(seed)
        ks = jax.random.split(key, 20)
        s_basis = np.sqrt(2.0 / (D + D)).astype(np.float32)
        s_att = np.sqrt(2.0 / (R + B)).astype(np.float32)
        inp = {'x': jax.random.normal(ks[0], (N, D), dtype=jnp.float32), 'edge_index': jax.random.randint(ks[1], (2, E), 0, N), 'edge_type': jax.random.randint(ks[2], (E,), 0, R), 'edge_attr': jax.random.uniform(ks[3], (E,), dtype=jnp.float32), 'basis1': jax.random.normal(ks[4], (B, D, D), dtype=jnp.float32) * s_basis, 'att1': jax.random.normal(ks[5], (R, B), dtype=jnp.float32) * s_att, 'root1': jax.random.normal(ks[6], (D, D), dtype=jnp.float32) * s_basis, 'bias1': jnp.zeros((D,), dtype=jnp.float32), 'ln1_g': jnp.ones((D,), dtype=jnp.float32), 'ln1_b': jnp.zeros((D,), dtype=jnp.float32), 'basis2': jax.random.normal(ks[7], (B, D, D), dtype=jnp.float32) * s_basis, 'att2': jax.random.normal(ks[8], (R, B), dtype=jnp.float32) * s_att, 'root2': jax.random.normal(ks[9], (D, D), dtype=jnp.float32) * s_basis, 'bias2': jnp.zeros((D,), dtype=jnp.float32), 'ln2_g': jnp.ones((D,), dtype=jnp.float32), 'ln2_b': jnp.zeros((D,), dtype=jnp.float32)}
        return inp
    _L0_gnn_all = _L0_gnn_setup()
    _L0_gnn_in = {k: v for k, v in _L0_gnn_all.items() if k in ('basis1', 'att1', 'root1', 'bias1', 'ln1_g', 'ln1_b', 'basis2', 'att2', 'root2', 'bias2', 'ln2_g', 'ln2_b')}
    del _L0_gnn_all

    def _L0_ffn_setup():
        import jax, jax.numpy as jnp
        import numpy as np
        B, N, D = (16, 512, 256)
        NUM_EXPERTS, TOP_K, HEADS = (4, 2, 4)
        N_EDGES = 131072
        LN_EPS = 1e-05

        def _layernorm(x, g, b):
            mu = x.mean(-1, keepdims=True)
            var = ((x - mu) ** 2).mean(-1, keepdims=True)
            return (x - mu) * jax.lax.rsqrt(var + LN_EPS) * g + b

        def _forward(x, edge_index, W_gat, att_src, att_dst, b_gat, ln_gamma, ln_beta, W1, b1, W2, b2):
            Bc, Nc, Dc = x.shape
            M = Bc * Nc
            x_flat = x.reshape(M, Dc)
            h = (x_flat @ W_gat).reshape(M, HEADS, NUM_EXPERTS)
            loops = jnp.arange(M, dtype=edge_index.dtype)
            src = jnp.concatenate([edge_index[0], loops])
            dst = jnp.concatenate([edge_index[1], loops])
            a_src = (h * att_src).sum(-1)
            a_dst = (h * att_dst).sum(-1)
            e = jax.nn.leaky_relu(a_src[src] + a_dst[dst], negative_slope=0.2)
            e_max = jax.ops.segment_max(e, dst, num_segments=M)
            ee = jnp.exp(e - e_max[dst])
            denom = jax.ops.segment_sum(ee, dst, num_segments=M)
            alpha = ee / (denom[dst] + 1e-16)
            msg = h[src] * alpha[:, :, None]
            agg = jax.ops.segment_sum(msg, dst, num_segments=M).reshape(M, HEADS * NUM_EXPERTS) + b_gat
            scores = _layernorm(agg, ln_gamma, ln_beta).reshape(M, HEADS, NUM_EXPERTS).mean(1)
            scores = scores.reshape(Bc, Nc, NUM_EXPERTS)
            topk_s, topk_i = jax.lax.top_k(scores, TOP_K)
            w = jax.nn.softmax(topk_s, axis=-1)
            out = jnp.zeros_like(x)
            for ei in range(NUM_EXPERTS):
                g = jnp.where(topk_i == ei, w, 0.0).sum(-1)
                hh = jax.nn.gelu(x @ W1[ei] + b1[ei], approximate=False)
                out = out + g[..., None] * (hh @ W2[ei] + b2[ei])
            return out
        key = jax.random.key(seed)
        ks = jax.random.split(key, 8)
        s = 0.05
        return {'x': jax.random.normal(ks[0], (B, N, D), jnp.float32), 'W_gat': jax.random.normal(ks[1], (D, HEADS * NUM_EXPERTS), jnp.float32) * s, 'att_src': jax.random.normal(ks[2], (HEADS, NUM_EXPERTS), jnp.float32) * s, 'att_dst': jax.random.normal(ks[3], (HEADS, NUM_EXPERTS), jnp.float32) * s, 'b_gat': jnp.zeros((HEADS * NUM_EXPERTS,), jnp.float32), 'ln_gamma': jnp.ones((HEADS * NUM_EXPERTS,), jnp.float32), 'ln_beta': jnp.zeros((HEADS * NUM_EXPERTS,), jnp.float32), 'W1': jax.random.normal(ks[4], (NUM_EXPERTS, D, 2 * D), jnp.float32) * s, 'b1': jnp.zeros((NUM_EXPERTS, 2 * D), jnp.float32), 'W2': jax.random.normal(ks[5], (NUM_EXPERTS, 2 * D, D), jnp.float32) * s, 'b2': jnp.zeros((NUM_EXPERTS, D), jnp.float32), 'edge_index': jax.random.randint(ks[6], (2, N_EDGES), 0, B * N, jnp.int32)}
    _L0_ffn_all = _L0_ffn_setup()
    _L0_ffn_in = {k: v for k, v in _L0_ffn_all.items() if k in ('W_gat', 'att_src', 'att_dst', 'b_gat', 'ln_gamma', 'ln_beta', 'W1', 'b1', 'W2', 'b2', 'edge_index')}
    del _L0_ffn_all
    return {'x': x, 'src': src, 'dst': dst, 'edge_type_16': edge_type_16, 'edge_weight': edge_weight, 'L0_gnn_basis1': _L0_gnn_in['basis1'], 'L0_gnn_att1': _L0_gnn_in['att1'], 'L0_gnn_root1': _L0_gnn_in['root1'], 'L0_gnn_bias1': _L0_gnn_in['bias1'], 'L0_gnn_ln1_g': _L0_gnn_in['ln1_g'], 'L0_gnn_ln1_b': _L0_gnn_in['ln1_b'], 'L0_gnn_basis2': _L0_gnn_in['basis2'], 'L0_gnn_att2': _L0_gnn_in['att2'], 'L0_gnn_root2': _L0_gnn_in['root2'], 'L0_gnn_bias2': _L0_gnn_in['bias2'], 'L0_gnn_ln2_g': _L0_gnn_in['ln2_g'], 'L0_gnn_ln2_b': _L0_gnn_in['ln2_b'], 'L0_ffn_W_gat': _L0_ffn_in['W_gat'], 'L0_ffn_att_src': _L0_ffn_in['att_src'], 'L0_ffn_att_dst': _L0_ffn_in['att_dst'], 'L0_ffn_b_gat': _L0_ffn_in['b_gat'], 'L0_ffn_ln_gamma': _L0_ffn_in['ln_gamma'], 'L0_ffn_ln_beta': _L0_ffn_in['ln_beta'], 'L0_ffn_W1': _L0_ffn_in['W1'], 'L0_ffn_b1': _L0_ffn_in['b1'], 'L0_ffn_W2': _L0_ffn_in['W2'], 'L0_ffn_b2': _L0_ffn_in['b2'], 'L0_ffn_edge_index': _L0_ffn_in['edge_index']}

def reference(x, src, dst, edge_type_16, edge_weight, L0_gnn_basis1, L0_gnn_att1, L0_gnn_root1, L0_gnn_bias1, L0_gnn_ln1_g, L0_gnn_ln1_b, L0_gnn_basis2, L0_gnn_att2, L0_gnn_root2, L0_gnn_bias2, L0_gnn_ln2_g, L0_gnn_ln2_b, L0_ffn_W_gat, L0_ffn_att_src, L0_ffn_att_dst, L0_ffn_b_gat, L0_ffn_ln_gamma, L0_ffn_ln_beta, L0_ffn_W1, L0_ffn_b1, L0_ffn_W2, L0_ffn_b2, L0_ffn_edge_index):
    import jax
    import jax.numpy as jnp

    def _L0_gnn_ref(x, edge_index, edge_type, edge_attr, basis1, att1, root1, bias1, ln1_g, ln1_b, basis2, att2, root2, bias2, ln2_g, ln2_b):
        import jax, jax.numpy as jnp
        import numpy as np
        N = 6250
        E = 100000
        D = 256
        R = 16
        B = 8
        LN_EPS = 1e-05

        def _layer_norm(x, g, b):
            mu = jnp.mean(x, axis=-1, keepdims=True)
            var = jnp.mean(jnp.square(x - mu), axis=-1, keepdims=True)
            return (x - mu) * jax.lax.rsqrt(var + LN_EPS) * g + b

        def _rgcn_layer(x, edge_index, edge_type, edge_attr, basis, att, root, bias):
            n = x.shape[0]
            r = att.shape[0]
            weight = jnp.einsum('rb,bio->rio', att, basis)
            H = jnp.einsum('ni,rio->nro', x, weight)
            loop = jnp.arange(n, dtype=edge_index.dtype)
            src = jnp.concatenate([edge_index[0], loop])
            dst = jnp.concatenate([edge_index[1], loop])
            et = jnp.concatenate([edge_type, jnp.full((n,), r - 1, dtype=edge_type.dtype)])
            ea = jnp.concatenate([edge_attr, jnp.ones((n,), dtype=x.dtype)])
            msg = H[src, et] * ea[:, None]
            summ = jax.ops.segment_sum(msg, dst, num_segments=n)
            cnt = jax.ops.segment_sum(jnp.ones_like(ea), dst, num_segments=n)
            agg = summ / cnt[:, None]
            return agg + x @ root + bias
        h = x
        h_out = _rgcn_layer(h, edge_index, edge_type, edge_attr, basis1, att1, root1, bias1)
        h = jax.nn.relu(_layer_norm(h + h_out, ln1_g, ln1_b))
        h_out = _rgcn_layer(h, edge_index, edge_type, edge_attr, basis2, att2, root2, bias2)
        h = jax.nn.relu(_layer_norm(h + h_out, ln2_g, ln2_b))
        return h

    def _L0_ffn_ref(x, W_gat, att_src, att_dst, b_gat, ln_gamma, ln_beta, W1, b1, W2, b2, edge_index):
        import jax, jax.numpy as jnp
        import numpy as np
        B, N, D = (16, 512, 256)
        NUM_EXPERTS, TOP_K, HEADS = (4, 2, 4)
        N_EDGES = 131072
        LN_EPS = 1e-05

        def _layernorm(x, g, b):
            mu = x.mean(-1, keepdims=True)
            var = ((x - mu) ** 2).mean(-1, keepdims=True)
            return (x - mu) * jax.lax.rsqrt(var + LN_EPS) * g + b

        def _forward(x, edge_index, W_gat, att_src, att_dst, b_gat, ln_gamma, ln_beta, W1, b1, W2, b2):
            Bc, Nc, Dc = x.shape
            M = Bc * Nc
            x_flat = x.reshape(M, Dc)
            h = (x_flat @ W_gat).reshape(M, HEADS, NUM_EXPERTS)
            loops = jnp.arange(M, dtype=edge_index.dtype)
            src = jnp.concatenate([edge_index[0], loops])
            dst = jnp.concatenate([edge_index[1], loops])
            a_src = (h * att_src).sum(-1)
            a_dst = (h * att_dst).sum(-1)
            e = jax.nn.leaky_relu(a_src[src] + a_dst[dst], negative_slope=0.2)
            e_max = jax.ops.segment_max(e, dst, num_segments=M)
            ee = jnp.exp(e - e_max[dst])
            denom = jax.ops.segment_sum(ee, dst, num_segments=M)
            alpha = ee / (denom[dst] + 1e-16)
            msg = h[src] * alpha[:, :, None]
            agg = jax.ops.segment_sum(msg, dst, num_segments=M).reshape(M, HEADS * NUM_EXPERTS) + b_gat
            scores = _layernorm(agg, ln_gamma, ln_beta).reshape(M, HEADS, NUM_EXPERTS).mean(1)
            scores = scores.reshape(Bc, Nc, NUM_EXPERTS)
            topk_s, topk_i = jax.lax.top_k(scores, TOP_K)
            w = jax.nn.softmax(topk_s, axis=-1)
            out = jnp.zeros_like(x)
            for ei in range(NUM_EXPERTS):
                g = jnp.where(topk_i == ei, w, 0.0).sum(-1)
                hh = jax.nn.gelu(x @ W1[ei] + b1[ei], approximate=False)
                out = out + g[..., None] * (hh @ W2[ei] + b2[ei])
            return out
        return _forward(x, edge_index, W_gat, att_src, att_dst, b_gat, ln_gamma, ln_beta, W1, b1, W2, b2)
    edge_index = jnp.stack([src, dst])
    x = x + _L0_gnn_ref(_layernorm(x, axis=-1), edge_index, edge_type_16, edge_weight, L0_gnn_basis1, L0_gnn_att1, L0_gnn_root1, L0_gnn_bias1, L0_gnn_ln1_g, L0_gnn_ln1_b, L0_gnn_basis2, L0_gnn_att2, L0_gnn_root2, L0_gnn_bias2, L0_gnn_ln2_g, L0_gnn_ln2_b)
    x = x + _L0_ffn_ref(_layernorm(x, axis=-1)[None], L0_ffn_W_gat, L0_ffn_att_src, L0_ffn_att_dst, L0_ffn_b_gat, L0_ffn_ln_gamma, L0_ffn_ln_beta, L0_ffn_W1, L0_ffn_b1, L0_ffn_W2, L0_ffn_b2, L0_ffn_edge_index)[0]
    return x

_drawn_inputs = setup_inputs


def setup_inputs(seed=0):
    import zlib

    import numpy as np

    out = dict(_drawn_inputs(seed))
    spreads = {'L0_gnn_bias1': (0.0, 0.1),
     'L0_gnn_ln1_g': (1.0, 0.2),
     'L0_gnn_ln1_b': (0.0, 0.1),
     'L0_gnn_bias2': (0.0, 0.1),
     'L0_gnn_ln2_g': (1.0, 0.2),
     'L0_gnn_ln2_b': (0.0, 0.1),
     'L0_ffn_b_gat': (0.0, 0.1),
     'L0_ffn_ln_gamma': (1.0, 0.2),
     'L0_ffn_ln_beta': (0.0, 0.1),
     'L0_ffn_b1': (0.0, 0.1),
     'L0_ffn_b2': (0.0, 0.1)}
    factors = {'L0_ffn_att_dst': 2.74}
    for name, (base, spread) in spreads.items():
        noise = np.random.default_rng([zlib.crc32(name.encode()), seed]).standard_normal(out[name].shape)
        drawn = base * np.exp(spread * noise) if base else spread * noise
        out[name] = jnp.asarray(drawn.astype(out[name].dtype))
    for name, factor in factors.items():
        out[name] = (out[name] * factor).astype(out[name].dtype)
    return out
```

```python
import numpy as np
import concourse.bass as bass
from concourse import mybir
from contextlib import ExitStack, contextmanager

F32 = mybir.dt.float32
BF16 = mybir.dt.bfloat16
I32 = mybir.dt.int32
ALU = mybir.AluOpType
ACT = mybir.ActivationFunctionType
AX = mybir.AxisListType

P = 128
N, D = 6250, 256
NT = -(-N // P)
NP = NT * P
RELS, BASES = 16, 8
E_GNN, E_GAT = 100000, 131072
U = 16
T_GNN = -(-E_GNN // (P * U)) * U
T_GAT = E_GAT // P
KEYS = 8192
KH = KEYS // P
PAD = KEYS - 1
HEADS, EXPERTS, FF = 4, 4, 512
REC = HEADS + HEADS * EXPERTS
EPS = 1e-5


def over_tiles(eng, body):
    for k in range(2):
        body(0, k)
    with eng.Fori(1, NT // 2) as i:
        for k in range(2):
            body(i, k)
    if NT % 2:
        body(NT // 2, 0)


def later(i):
    return not isinstance(i, int) or i > 0


class Steps:

    def __init__(self, eng, sem, turn, per_turn):
        self.eng, self.sem, self.turn, self.per, self.k = eng, sem, turn, per_turn, 0

    def wait(self):
        if self.k or not isinstance(self.turn, int) or self.turn:
            if self.k:
                self.eng.wait_ge(self.sem, self.turn * self.per + self.k)

    def __call__(self, instruction):
        instruction.then_inc(self.sem, 1)
        self.k += 1


def build(nc, a, out):
    ctx = ExitStack()
    with ctx:
        top = ctx

        def sb(name, shape, dt=F32, scope=None):
            return (scope or top).enter_context(nc.sbuf_tensor(name, shape, dt))

        open_phases = []

        def sem(name):
            handle = nc.alloc_semaphore(name)
            open_phases[-1].append(handle)
            return handle

        @contextmanager
        def phase():
            with ExitStack() as scope:
                open_phases.append([])
                yield scope
                mine = open_phases.pop()
                if mine:
                    nc.clear_and_free_semaphores(mine)
                    nc.all_engine_barrier()


        def dram(name, shape, dt=F32):
            return nc.dram_tensor(name, shape, dt)

        x_pad = dram("x_pad", (NP, D))
        h0_d = dram("h0_d", (NP, D))
        h1_d = dram("h1_d", (NP, D))
        y_d = dram("y_d", (NP, D))
        table = [dram(f"table{l}", (NP, RELS * D)) for l in range(2)]
        rooted = [dram(f"rooted{l}", (NP, D)) for l in range(2)]
        run_d = dram("run_d", (P * T_GNN, D))
        bounds_gnn = dram("bounds_gnn", (2, KEYS))

        ident = sb("ident", [P, P])
        upper = sb("upper", [P, P])
        ones = sb("ones", [P, P])
        iota_row = sb("iota_row", [P, P])
        iota_i = sb("iota_i", [P, P], I32)
        split_gnn = sb("split_gnn", [P, 1])
        split_i = sb("split_i", [P, 1], I32)
        hidx = sb("hidx", [P, T_GNN], I32)
        ea = sb("ea", [P, T_GNN])
        keep = sb("keep", [P, T_GNN])
        lo_gnn = sb("lo_gnn", [P, T_GNN])
        hi_gnn = sb("hi_gnn", [P, T_GNN])
        first_gnn = sb("first_gnn", [P, KH])
        after_gnn = sb("after_gnn", [P, KH])
        last_gnn_i = sb("last_gnn_i", [P, KH], I32)
        has_gnn = sb("has_gnn", [P, KH])
        inv_gnn = sb("inv_gnn", [P, KH])
        carry = sb("carry", [P, D])
        minus_half = sb("minus_half", [P, 1])

        with phase() as sc:
            dst_i = sb("dst_i", [P, T_GNN], I32, sc)
            src_i = sb("src_i", [P, T_GNN], I32, sc)
            typ_i = sb("typ_i", [P, T_GNN], I32, sc)
            part_i = sb("part_i", [P, T_GNN], I32, sc)
            zero_rows = sb("zero_rows", [NP - N, D], F32, sc)
            set_done, edges_in, iota_done, key_step, xpad_done = (
                sem(n) for n in ("set_done", "edges_in", "iota_done", "key_step", "xpad_done"))
            full, rest = E_GNN // T_GNN, E_GNN % T_GNN
            with nc.Block() as block:
                @block.gpsimd
                def _(e):
                    e.memset(dst_i[:, :], PAD).then_inc(set_done, 1)
                    e.memset(src_i[:, :], 0).then_inc(set_done, 1)
                    e.memset(typ_i[:, :], 0).then_inc(set_done, 1)
                    e.memset(ea[:, :], 0.0).then_inc(set_done, 1)
                    e.memset(zero_rows[:, :], 0.0).then_inc(set_done, 1)
                    e.memset(ident[:, :], 0.0).then_inc(iota_done, 1)
                    e.memset(ones[:, :], 1.0).then_inc(iota_done, 1)
                    e.memset(minus_half[:, :], -0.5).then_inc(iota_done, 1)
                    e.iota(iota_i[:, :], pattern=[[1, P]], base=0, channel_multiplier=0).then_inc(iota_done, 1)
                    e.iota(split_i[:, :], pattern=[[0, 1]], base=T_GNN, channel_multiplier=T_GNN).then_inc(iota_done, 1)
                    e.wait_ge(iota_done, 5)
                    e.affine_select(out=ident[:, :], in_=ident[:, :], compare_op=ALU.not_equal, fill=1.0, base=0,
                                    pattern=[[-1, P]], channel_multiplier=1).then_inc(iota_done, 1)
                    e.affine_select(out=upper[:, :], in_=ones[:, :], compare_op=ALU.is_ge, fill=0.0, base=0,
                                    pattern=[[1, P]], channel_multiplier=-1).then_inc(iota_done, 1)
                    e.wait_ge(iota_done, 7)

                @block.sync
                def _(e):
                    e.wait_ge(set_done, 5)
                    for buf, arr in ((dst_i, a["dst"]), (src_i, a["src"]), (typ_i, a["edge_type_16"]), (ea, a["edge_weight"])):
                        e.dma_start(buf[0:full, :], arr[0:full * T_GNN].rearrange("(p t) -> p t", t=T_GNN)).then_inc(edges_in, 16)
                        e.dma_start(buf[full:full + 1, 0:rest], arr[full * T_GNN:E_GNN].rearrange("(p t) -> p t", p=1)).then_inc(edges_in, 16)
                    e.dma_start(x_pad[0:N, :], a["x"][:, :]).then_inc(xpad_done, 16)
                    e.dma_start(x_pad[N:NP, :], zero_rows[:, :]).then_inc(xpad_done, 16)
                    e.wait_ge(edges_in, 8 * 16)
                    e.wait_ge(xpad_done, 32)

                @block.vector
                def _(e):
                    st = Steps(e, key_step, 0, 99)
                    e.wait_ge(edges_in, 8 * 16)
                    e.wait_ge(iota_done, 5)
                    v = nc.vector
                    st(v.tensor_copy(iota_row[:, :], iota_i[:, :]))
                    st(v.tensor_copy(split_gnn[:, :], split_i[:, :]))
                    st(v.scalar_tensor_tensor(out=hidx[:, :], in0=src_i[:, :], scalar=float(RELS), in1=typ_i[:, :],
                                              op0=ALU.mult, op1=ALU.add))
                    st(v.memset(keep[:, 0:1], 0.0))
                    st(v.tensor_tensor(keep[:, 1:T_GNN], dst_i[:, 1:T_GNN], dst_i[:, 0:T_GNN - 1], ALU.is_equal))
                    st(v.tensor_single_scalar(part_i[:, :], dst_i[:, :], P - 1, ALU.bitwise_and))
                    st.wait()
                    st(v.tensor_copy(lo_gnn[:, :], part_i[:, :]))
                    st.wait()
                    st(v.tensor_single_scalar(part_i[:, :], dst_i[:, :], 7, ALU.logical_shift_right))
                    st.wait()
                    st(v.tensor_copy(hi_gnn[:, :], part_i[:, :]))

        def count(tag, lo, hi, T, first, after, bounds, finish):
            G = 8
            with phase() as sc:
                eq_lo = [sb(f"{tag}_eq_lo{j}", [P, G, P], BF16, sc) for j in range(2)]
                eq_hi = [sb(f"{tag}_eq_hi{j}", [P, G, KH], BF16, sc) for j in range(2)]
                cnt = sb(f"{tag}_cnt", [P, KH], F32, sc)
                before = sb(f"{tag}_before", [P, KH], F32, sc)
                zb = sb(f"{tag}_zb", [P, P], BF16, sc)
                ps = sc.enter_context(nc.psum_tensor(f"{tag}_ps", [P, 512], F32))
                ps2 = sc.enter_context(nc.psum_tensor(f"{tag}_ps2", [P, 512], F32))
                eq_ready, eq_used, zero_set, counted, tail, ranked, stored = (
                    sem(f"{tag}_{n}") for n in ("eq_ready", "eq_used", "zero_set", "counted", "tail", "ranked", "stored"))
                turns = T // (2 * G)
                with nc.Block() as block:
                    @block.vector
                    def _(e):
                        v = nc.vector
                        v.memset(zb[:, :], 0.0).then_inc(zero_set, 1)
                        with e.Fori(0, turns) as i:
                            for j in range(2):
                                e.wait_ge(eq_used, 2 * i + j + 1)
                                at = bass.ds((2 * i + j) * G, G)
                                v.tensor_tensor(eq_lo[j][:, :, :], lo[:, at].unsqueeze(2).to_broadcast([P, G, P]),
                                                iota_row[:, :].unsqueeze(1).to_broadcast([P, G, P]), ALU.is_equal).then_inc(eq_ready, 1)
                                v.tensor_tensor(eq_hi[j][:, :, :], hi[:, at].unsqueeze(2).to_broadcast([P, G, KH]),
                                                iota_row[:, 0:KH].unsqueeze(1).to_broadcast([P, G, KH]), ALU.is_equal).then_inc(eq_ready, 1)
                        e.wait_ge(counted, 1)
                        st = Steps(e, tail, 0, 99)
                        st(v.tensor_copy(cnt[:, :], ps[:, 0:KH]))
                        st.wait()
                        st(v.tensor_tensor_scan(before[:, :], ones[:, 0:KH], cnt[:, :], 0.0, ALU.mult, ALU.add))
                        st.wait()
                        st(v.tensor_tensor(before[:, :], before[:, :], cnt[:, :], ALU.subtract))
                        e.wait_ge(ranked, 1)
                        st(v.tensor_copy(after[:, :], ps2[:, 0:KH]))
                        st.wait()
                        st(v.tensor_tensor(first[:, :], after[:, :], cnt[:, :], ALU.subtract))
                        finish(v, st, cnt)

                    @block.tensor
                    def _(e):
                        e.wait_ge(zero_set, 1)
                        nc.tensor.matmul(ps[:, 0:KH], zb[:, :], zb[:, 0:KH], start=True, stop=False)
                        e.sem_inc(eq_used, 2)
                        with e.Fori(0, turns) as i:
                            for j in range(2):
                                e.wait_ge(eq_ready, 4 * i + 2 * j + 2)
                                for g in range(G):
                                    m = nc.tensor.matmul(ps[:, 0:KH], eq_lo[j][:, g, :], eq_hi[j][:, g, :], start=False, stop=False)
                                m.then_inc(eq_used, 1)
                        nc.tensor.matmul(ps[:, 0:KH], zb[:, :], zb[:, 0:KH], start=False, stop=True).then_inc(counted, 1)
                        e.wait_ge(tail, 3)
                        nc.tensor.matmul(ps2[:, 0:KH], upper[:, :], cnt[:, :], start=True, stop=False)
                        nc.tensor.matmul(ps2[:, 0:KH], ones[:, :], before[:, :], start=False, stop=True).then_inc(ranked, 1)

                    @block.sync
                    def _(e):
                        e.wait_ge(tail, 5)
                        with nc.allow_non_contiguous_dma(reason="8192 words, once"):
                            e.dma_start(bounds[0, :].rearrange("(h l) -> l h", l=P), first[:, :]).then_inc(stored, 16)
                            e.dma_start(bounds[1, :].rearrange("(h l) -> l h", l=P), after[:, :]).then_inc(stored, 16)
                        e.wait_ge(stored, 32)

        def finish_gnn(v, st, cnt):
            st(v.tensor_scalar(has_gnn[:, :], cnt[:, :], 1.0, None, ALU.min))
            st(v.tensor_scalar(inv_gnn[:, :], cnt[:, :], 1.0, None, ALU.add))
            st.wait()
            st(v.reciprocal(inv_gnn[:, :], inv_gnn[:, :]))
            st(v.tensor_scalar(last_gnn_i[:, :], after_gnn[:, :], -1.0, 0.0, ALU.add, ALU.max))
            st.wait()

        count("gnn", lo_gnn, hi_gnn, T_GNN, first_gnn, after_gnn, bounds_gnn, finish_gnn)

        def make_weights(l, weights, sc):
            basis, att, root = (a[f"L0_gnn_{n}{l + 1}"] for n in ("basis", "att", "root"))
            with phase() as s2:
                bs = [sb(f"basis{l}_{c}", [P, BASES, D], F32, s2) for c in range(2)]
                att_bc = sb(f"att_bc{l}", [P, RELS * BASES], F32, s2)
                loaded, mixed = sem(f"basis_in{l}"), sem(f"mixed{l}")
                with nc.Block() as block:
                    @block.sync
                    def _(e):
                        for c in range(2):
                            e.dma_start(bs[c][:, :, :], basis[:, c * P:(c + 1) * P, :].rearrange("b p o -> p b o")).then_inc(loaded, 16)
                            e.dma_start(weights[c][:, RELS, :], root[c * P:(c + 1) * P, :]).then_inc(loaded, 16)
                        e.dma_start(att_bc[:, :], att.rearrange("r b -> (r b)").unsqueeze(0).to_broadcast([P, RELS * BASES])).then_inc(loaded, 16)
                        e.wait_ge(loaded, 5 * 16)

                    @block.vector
                    def _(e):
                        v = nc.vector
                        e.wait_ge(loaded, 5 * 16)
                        n = 0
                        for b in range(BASES):
                            for r in range(RELS):
                                for c in range(2):
                                    w = weights[c][:, r, :]
                                    s = att_bc[:, r * BASES + b:r * BASES + b + 1]
                                    if b == 0:
                                        v.tensor_scalar(w, bs[c][:, b, :], s, None, ALU.mult).then_inc(mixed, 1)
                                    else:
                                        e.wait_ge(mixed, n - 2 * RELS + 1)
                                        v.scalar_tensor_tensor(out=w, in0=bs[c][:, b, :], scalar=s, in1=w,
                                                               op0=ALU.mult, op1=ALU.add).then_inc(mixed, 1)
                                    n += 1

        def node_loop(l):
            with phase() as sc:
                tag = f"n{l}"
                weights = [sb(f"{tag}_weights{c}", [P, RELS + 1, D], F32, sc) for c in range(2)]
                make_weights(l, weights, sc)
                h_in = [sb(f"{tag}_h_in{k}", [P, D], F32, sc) for k in range(2)]
                h_new = [sb(f"{tag}_h_new{k}", [P, D], F32, sc) for k in range(2)]
                hT = [sb(f"{tag}_hT{k}", [P, 2, P], F32, sc) for k in range(2)]
                prod = [sb(f"{tag}_prod{k}", [P, RELS + 1, D], F32, sc) for k in range(2)]
                psT = [sc.enter_context(nc.psum_tensor(f"{tag}_psT{k}", [P, 512], F32)) for k in range(2)]
                psP = [sc.enter_context(nc.psum_tensor(f"{tag}_psP{j}", [P, 512], F32)) for j in range(3)]
                psC = sc.enter_context(nc.psum_tensor(f"{tag}_psC", [P, 512], F32))
                S = {n: sem(f"{tag}_{n}") for n in (
                    "step", "h_taken", "turned", "hT_ready", "product", "evacuated", "held", "w_used", "carried", "idx_set", "vec_in", "rooted")}
                h_full = [sem(f"{tag}_h_full{k}") for k in range(2)]
                h_kept = [sem(f"{tag}_h_kept{k}") for k in range(2)]
                t_kept = [sem(f"{tag}_t_kept{k}") for k in range(2)]
                end_in = [sem(f"{tag}_end_in{k}") for k in range(2)]
                src_d, keep_d = (x_pad, h0_d) if l == 0 else (h0_d, h1_d)
                tail = tail_buffers(tag, sc) if l else None
                PER = 4 if l == 0 else TAIL_STEPS
                CH = 9
                with nc.Block() as block:
                    @block.sync
                    def _(e):
                        if l:
                            load_vectors(e, tail, l, S["vec_in"])
                        def body(i, k):
                            n = 2 * i + k
                            e.wait_ge(S["h_taken"], n + 1)
                            e.dma_start(h_in[k][:, :], src_d[bass.ds(n * P, P), :]).then_inc(h_full[k], 16)
                            if l:
                                tail_loads(e, tail, l, n, k, h_full[k])
                        over_tiles(e, body)

                    @block.vector
                    def _(e):
                        v = nc.vector
                        e.sem_inc(S["h_taken"], 2)
                        if l:
                            e.wait_ge(S["vec_in"], VECS * 16)

                        def body(i, k):
                            n = 2 * i + k
                            st = Steps(e, S["step"], n, PER)
                            e.wait_ge(h_full[k], (i + 1) * (16 if l == 0 else 16 * TAIL_LOADS))
                            if l == 0:
                                if later(i):
                                    e.wait_ge(h_kept[k], 16 * i)
                                    e.wait_ge(S["turned"], n - 1)
                                layer_norm(e, st, h_new[k], h_in[k], k, n + 1, S)
                                st.wait()
                                assert st.k == PER
                                e.sem_inc(S["h_taken"], 1)
                            else:
                                def free():
                                    if later(i):
                                        e.wait_ge(h_kept[k], 16 * i)
                                        e.wait_ge(S["turned"], n - 1)
                                tail_steps(e, st, tail, l, n, i, k, h_in[k], h_new[k], psC, S, end_in, n + 1, free)
                                e.sem_inc(S["h_taken"], 1)
                        over_tiles(e, body)

                    @block.tensor
                    def _(e):
                        def body(i, k):
                            n = 2 * i + k
                            if l:
                                cross_product(e, tail, n, k, psC, S, PER)
                            e.wait_ge(S["step"], n * PER + PER)
                            for c in range(2):
                                m = nc.tensor.transpose(psT[k][:, c * P:(c + 1) * P], h_new[k][:, c * P:(c + 1) * P], ident[:, :])
                            m.then_inc(S["turned"], 1)
                            e.wait_ge(S["hT_ready"], n + 1)
                            for q in range(CH):
                                e.wait_ge(S["evacuated"], n * CH + q + 1)
                                w = 512 if q < CH - 1 else D
                                for c in range(2):
                                    m = nc.tensor.matmul(psP[q % 3][:, 0:w], hT[k][:, c, :],
                                                         weights[c][:, 2 * q:2 * q + w // D, :].rearrange("p r o -> p (r o)"),
                                                         start=(c == 0), stop=(c == 1))
                                m.then_inc(S["product"], 1)
                        over_tiles(e, body)

                    @block.scalar
                    def _(e):
                        e.sem_inc(S["evacuated"], 3)

                        def body(i, k):
                            n = 2 * i + k
                            e.wait_ge(S["turned"], n + 1)
                            nc.scalar.activation(hT[k][:, :, :].rearrange("p c n -> p (c n)"), psT[k][:, 0:2 * P], ACT.Copy).then_inc(S["hT_ready"], 1)
                            if later(i):
                                e.wait_ge(t_kept[k], 32 * i)
                            for q in range(CH):
                                e.wait_ge(S["product"], n * CH + q + 1)
                                w = 512 if q < CH - 1 else D
                                nc.scalar.activation(prod[k][:, 2 * q:2 * q + w // D, :].rearrange("p r o -> p (r o)"),
                                                     psP[q % 3][:, 0:w], ACT.Copy).then_inc(S["evacuated"], 1)
                            e.wait_ge(S["evacuated"], 3 + (n + 1) * CH)
                            e.dma_start(table[l][bass.ds(n * P, P), :], prod[k][:, 0:RELS, :].rearrange("p r o -> p (r o)")).then_inc(t_kept[k], 16)
                            e.dma_start(rooted[l][bass.ds(n * P, P), :], prod[k][:, RELS, :]).then_inc(t_kept[k], 16)
                        over_tiles(e, body)
                        for k in range(2):
                            e.wait_ge(t_kept[k], 32 * (NT // 2 + (NT % 2 if k == 0 else 0)))

                    @block.gpsimd
                    def _(e):
                        def body(i, k):
                            n = 2 * i + k
                            if l:
                                fetch_ends(e, tail, n, i, k, S, end_in, PER)
                            inverse_root(e, k, S, n * PER + (3 if l == 0 else 10))
                            e.wait_ge(S["step"], n * PER + PER)
                            e.sem_inc(S["held"], 1)
                            e.dma_start(keep_d[bass.ds(n * P, P), :], h_new[k][:, :]).then_inc(h_kept[k], 16)
                        over_tiles(e, body)
                        for k in range(2):
                            e.wait_ge(h_kept[k], 16 * (NT // 2 + (NT % 2 if k == 0 else 0)))

        stats = [sb(f"stats{k}", [P, 6]) for k in range(2)]
        mvs = [sb(f"mv{k}", [P, 2]) for k in range(2)]
        rss = [sb(f"rstd{k}", [P, 1]) for k in range(2)]
        ves = [sb(f"var_eps{k}", [P, 1]) for k in range(2)]

        TAIL_STEPS = 12
        TAIL_LOADS = 4 + 1
        VECS = 3

        def tail_buffers(tag, sc):
            t = {}
            for k in range(2):
                t["rows", k] = sb(f"{tag}_rows{k}", [P, 2, P], F32, sc)
                t["self", k] = sb(f"{tag}_self{k}", [P, D], F32, sc)
                t["root", k] = sb(f"{tag}_root{k}", [P, D], F32, sc)
                t["end", k] = sb(f"{tag}_end{k}", [P, D], F32, sc)
                t["idx", k] = sb(f"{tag}_idx{k}", [P, 1], I32, sc)
                t["cross", k] = sb(f"{tag}_cross{k}", [P, P], F32, sc)
                t["ge", k] = sb(f"{tag}_ge{k}", [P, P], F32, sc)
                t["acc", k] = sb(f"{tag}_acc{k}", [P, D], F32, sc)
            for n in ("bias", "gain", "shift"):
                t[n] = sb(f"{tag}_{n}", [P, D], F32, sc)
            return t

        def load_vectors(e, t, l, vec_in):
            for n, arr in (("bias", f"L0_gnn_bias{l}"), ("gain", f"L0_gnn_ln{l}_g"), ("shift", f"L0_gnn_ln{l}_b")):
                e.dma_start(t[n][:, :], a[arr].unsqueeze(0).to_broadcast([P, D])).then_inc(vec_in, 16)

        def tail_loads(e, t, l, n, k, full):
            for j in range(2):
                e.dma_start(t["rows", k][:, j, :], bounds_gnn[j, bass.ds(n * P, P)].unsqueeze(0).to_broadcast([P, P])).then_inc(full, 16)
            own = table[l - 1][bass.ds(n * P, P), (RELS - 1) * D:RELS * D]
            e.dma_start(t["self", k][:, :], own).then_inc(full, 16)
            e.dma_start(t["root", k][:, :], rooted[l - 1][bass.ds(n * P, P), :]).then_inc(full, 16)

        def fetch_ends(e, t, n, i, k, S, end_in, PER):
            e.wait_ge(S["h_taken"], n + 1)
            e.sem_inc(S["held"], 1)
            e.tensor_copy(t["idx", k][:, :], last_gnn_i[:, bass.ds(n, 1)]).then_inc(S["idx_set"], 1)
            e.wait_ge(S["idx_set"], n + 1)
            e.sem_inc(S["held"], 1)
            e.indirect_dma_start(out=t["end", k][:, :], out_offset=None, in_=run_d[:, :],
                                 in_offset=bass.IndirectOffsetOnAxis(ap=t["idx", k][:, 0:1], axis=0)).then_inc(end_in[k], 16)

        def cross_product(e, t, n, k, psC, S, PER):
            e.wait_ge(S["step"], n * PER + 2)
            nc.tensor.matmul(psC[:, 0:D], t["cross", k][:, :], carry[:, :], start=True, stop=True).then_inc(S["carried"], 1)

        def tail_steps(e, st, t, l, n, i, k, h, h_new, psC, S, end_in, roots, free):
            v = nc.vector
            acc = t["acc", k]
            st(v.tensor_scalar(t["ge", k][:, :], t["rows", k][:, 0, :], split_gnn[:, :], None, ALU.is_lt))
            st.wait()
            st(v.scalar_tensor_tensor(out=t["cross", k][:, :], in0=t["rows", k][:, 1, :], scalar=split_gnn[:, :],
                                      in1=t["ge", k][:, :], op0=ALU.is_gt, op1=ALU.mult))
            e.wait_ge(end_in[k], 16 * (i + 1))
            e.wait_ge(S["carried"], n + 1)
            st(v.scalar_tensor_tensor(out=acc[:, :], in0=t["end", k][:, :], scalar=has_gnn[:, bass.ds(n, 1)],
                                      in1=psC[:, 0:D], op0=ALU.mult, op1=ALU.add))
            st(v.tensor_tensor(t["root", k][:, :], t["root", k][:, :], t["bias"][:, :], ALU.add))
            st.wait()
            st(v.tensor_tensor(acc[:, :], acc[:, :], t["self", k][:, :], ALU.add))
            st.wait()
            st(v.scalar_tensor_tensor(out=acc[:, :], in0=acc[:, :], scalar=inv_gnn[:, bass.ds(n, 1)],
                                      in1=t["root", k][:, :], op0=ALU.mult, op1=ALU.add))
            st.wait()
            st(v.tensor_tensor(acc[:, :], acc[:, :], h[:, :], ALU.add))
            layer_norm(e, st, acc, acc, k, roots, S)
            st.wait()
            st(v.tensor_tensor(acc[:, :], acc[:, :], t["gain"][:, :], ALU.mult))
            free()
            st.wait()
            st(v.tensor_tensor(acc[:, :], acc[:, :], t["shift"][:, :], ALU.add))
            st.wait()
            st(v.tensor_relu(h_new[:, :], acc[:, :]))
            st.wait()
            assert st.k == TAIL_STEPS, st.k

        def inverse_root(e, k, S, step):
            e.wait_ge(S["step"], step)
            e.tensor_tensor(rss[k][:, :], ves[k][:, :], minus_half[:, :], ALU.pow).then_inc(S["rooted"], 1)

        def layer_norm(e, st, dst, src, k, roots, S):
            v = nc.vector
            stat, mv, rs = stats[k], mvs[k], rss[k]
            st.wait()
            st(v.bn_stats(stat[:, :], src[:, :]))
            st.wait()
            e.sem_inc(S["held"], 1)
            st(v.bn_aggr(mv[:, :], stat[:, :]))
            st.wait()
            st(v.tensor_scalar(ves[k][:, :], mv[:, 1:2], EPS, None, ALU.add))
            e.wait_ge(S["rooted"], roots)
            st(v.tensor_scalar(dst[:, :], src[:, :], mv[:, 0:1], rs[:, :], ALU.subtract, ALU.mult))

        TAIL_STEPS = 14

        def edge_loop(l):
            with phase() as sc:
                tag = f"e{l}"
                H = U // 2
                got = sb(f"{tag}_got", [P, U, D], F32, sc)
                msg = sb(f"{tag}_msg", [P, U, D], F32, sc)
                run = sb(f"{tag}_run", [P, U, D], F32, sc)
                idx = sb(f"{tag}_idx", [P, U], I32, sc)
                ea_s = sb(f"{tag}_ea", [P, U], F32, sc)
                keep_s = sb(f"{tag}_keep", [P, U], F32, sc)
                idx_set, held, weighted, summed, ea_set, keep_set = (
                    sem(f"{tag}_{n}") for n in ("idx_set", "held", "weighted", "summed", "ea_set", "keep_set"))
                arrived = [sem(f"{tag}_arrived{j}") for j in range(U)]
                run_kept = [sem(f"{tag}_run_kept{h}") for h in range(2)]
                turns = T_GNN // U
                rows = table[l][:, :].rearrange("n (r o) -> (n r) o", o=D)
                run_view = run_d[:, :].rearrange("(p t) o -> p t o", t=T_GNN)
                with nc.Block() as block:
                    @block.gpsimd
                    def _(e):
                        def body(i, first):
                            if not first:
                                for j in range(U):
                                    e.wait_ge(arrived[j], 16 * i)
                            e.sem_inc(held, 1)
                            e.tensor_copy(idx[:, :], hidx[:, bass.ds(i * U, U)]).then_inc(idx_set, 1)
                            for h in range(2):
                                if not first:
                                    e.wait_ge(weighted, (i - 1) * U + (h + 1) * H)
                                if h == 0:
                                    e.wait_ge(idx_set, i + 1)
                                e.sem_inc(held, 1)
                                for j in range(h * H, (h + 1) * H):
                                    e.indirect_dma_start(out=got[:, j, :], out_offset=None, in_=rows,
                                                         in_offset=bass.IndirectOffsetOnAxis(ap=idx[:, j:j + 1], axis=0)).then_inc(arrived[j], 16)
                        body(0, True)
                        with e.Fori(1, turns) as i:
                            body(i, False)

                    @block.scalar
                    def _(e):
                        def body(i, first):
                            if not first:
                                e.wait_ge(weighted, i * U)
                                e.sem_inc(held, 1)
                            nc.scalar.activation(ea_s[:, :], ea[:, bass.ds(i * U, U)], ACT.Copy).then_inc(ea_set, 1)
                            e.wait_ge(ea_set, i + 1)
                            for j in range(U):
                                e.wait_ge(arrived[j], 16 * (i + 1))
                                if not first:
                                    e.wait_ge(summed, (i - 1) * U + j + 2)
                                nc.scalar.activation(msg[:, j, :], got[:, j, :], ACT.Copy, scale=ea_s[:, j:j + 1]).then_inc(weighted, 1)
                        body(0, True)
                        with e.Fori(1, turns) as i:
                            body(i, False)

                    @block.vector
                    def _(e):
                        v = nc.vector
                        v.memset(run[:, U - 1, :], 0.0).then_inc(summed, 1)

                        def body(i, first):
                            if not first:
                                e.wait_ge(summed, i * U + 1)
                                e.sem_inc(held, 1)
                            v.tensor_copy(keep_s[:, :], keep[:, bass.ds(i * U, U)]).then_inc(keep_set, 1)
                            e.wait_ge(keep_set, i + 1)
                            for j in range(U):
                                if j % H == 0 and not first:
                                    e.wait_ge(run_kept[j // H], 16 * i)
                                e.wait_ge(weighted, i * U + j + 1)
                                e.wait_ge(summed, i * U + j + 1)
                                v.scalar_tensor_tensor(out=run[:, j, :], in0=run[:, (j - 1) % U, :], scalar=keep_s[:, j:j + 1],
                                                       in1=msg[:, j, :], op0=ALU.mult, op1=ALU.add).then_inc(summed, 1)
                        body(0, True)
                        with e.Fori(1, turns) as i:
                            body(i, False)
                        e.wait_ge(summed, T_GNN + 1)
                        v.tensor_copy(carry[:, :], run[:, U - 1, :])

                    @block.sync
                    def _(e):
                        with e.Fori(0, turns) as i:
                            for h in range(2):
                                e.wait_ge(summed, i * U + (h + 1) * H + 1)
                                e.dma_start(run_view[:, bass.ds(i * U + h * H, H), :], run[:, h * H:(h + 1) * H, :]).then_inc(run_kept[h], 16)
                        for h in range(2):
                            e.wait_ge(run_kept[h], 16 * turns)


        def gate_rows():
            with phase() as sc:
                tag = "g"
                wg = sb("wg", [P, 2, HEADS * EXPERTS], F32, sc)
                h_in = [sb(f"g_h_in{k}", [P, D], F32, sc) for k in range(2)]
                x_in = [sb(f"g_x_in{k}", [P, D], F32, sc) for k in range(2)]
                relu = [sb(f"g_relu{k}", [P, D], F32, sc) for k in range(2)]
                x_new = [sb(f"g_x_new{k}", [P, D], F32, sc) for k in range(2)]
                h_new = [sb(f"g_h_new{k}", [P, D], F32, sc) for k in range(2)]
                hT = [sb(f"g_hT{k}", [P, 2, P], F32, sc) for k in range(2)]
                psT = [sc.enter_context(nc.psum_tensor(f"g_psT{k}", [P, 512], F32)) for k in range(2)]
                psG = [sc.enter_context(nc.psum_tensor(f"g_psG{k}", [P, 512], F32)) for k in range(2)]
                psC = sc.enter_context(nc.psum_tensor("g_psC", [P, 512], F32))
                S = {n: sem(f"g_{n}") for n in (
                    "step", "h_taken", "turned", "hT_ready", "product", "evacuated", "held", "carried", "idx_set", "vec_in", "rooted", "wg_in")}
                h_full = [sem(f"g_h_full{k}") for k in range(2)]
                h_kept = [sem(f"g_h_kept{k}") for k in range(2)]
                end_in = [sem(f"g_end_in{k}") for k in range(2)]
                tail = tail_buffers(tag, sc)
                PER = TAIL_STEPS + 5
                with nc.Block() as block:
                    @block.sync
                    def _(e):
                        load_vectors(e, tail, 2, S["vec_in"])
                        e.dma_start(wg[:, :, :], a["L0_ffn_W_gat"].rearrange("(c p) m -> p c m", p=P)).then_inc(S["wg_in"], 16)

                        def body(i, k):
                            n = 2 * i + k
                            e.wait_ge(S["h_taken"], n + 1)
                            e.dma_start(h_in[k][:, :], h1_d[bass.ds(n * P, P), :]).then_inc(h_full[k], 16)
                            e.dma_start(x_in[k][:, :], x_pad[bass.ds(n * P, P), :]).then_inc(h_full[k], 16)
                            tail_loads(e, tail, 2, n, k, h_full[k])
                        over_tiles(e, body)

                    @block.vector
                    def _(e):
                        v = nc.vector
                        e.sem_inc(S["h_taken"], 2)
                        e.wait_ge(S["vec_in"], VECS * 16)

                        def body(i, k):
                            n = 2 * i + k
                            st = Steps(e, S["step"], n, PER)
                            e.wait_ge(h_full[k], (i + 1) * 16 * (TAIL_LOADS + 1))
                            tail_steps(e, st, tail, 2, n, i, k, h_in[k], relu[k], psC, S, end_in, 2 * n + 1, lambda: None)
                            if later(i):
                                e.wait_ge(h_kept[k], 32 * i)
                                e.wait_ge(S["turned"], n - 1)
                            st.wait()
                            st(v.tensor_tensor(x_new[k][:, :], relu[k][:, :], x_in[k][:, :], ALU.add))
                            layer_norm(e, st, h_new[k], x_new[k], k, 2 * n + 2, S)
                            st.wait()
                            assert st.k == PER
                            e.sem_inc(S["h_taken"], 1)
                        over_tiles(e, body)

                    @block.tensor
                    def _(e):
                        e.wait_ge(S["wg_in"], 16)

                        def body(i, k):
                            n = 2 * i + k
                            cross_product(e, tail, n, k, psC, S, PER)
                            e.wait_ge(S["step"], n * PER + PER)
                            for c in range(2):
                                m = nc.tensor.transpose(psT[k][:, c * P:(c + 1) * P], h_new[k][:, c * P:(c + 1) * P], ident[:, :])
                            m.then_inc(S["turned"], 1)
                            e.wait_ge(S["hT_ready"], n + 1)
                            e.wait_ge(S["evacuated"], n + 1)
                            for c in range(2):
                                m = nc.tensor.matmul(psG[k][:, 0:16], hT[k][:, c, :], wg[:, c, :], start=(c == 0), stop=(c == 1))
                            m.then_inc(S["product"], 1)
                        over_tiles(e, body)

                    @block.scalar
                    def _(e):
                        e.sem_inc(S["evacuated"], 2)

                        def body(i, k):
                            n = 2 * i + k
                            e.wait_ge(S["turned"], n + 1)
                            nc.scalar.activation(hT[k][:, :, :].rearrange("p c n -> p (c n)"), psT[k][:, 0:2 * P], ACT.Copy).then_inc(S["hT_ready"], 1)
                            e.wait_ge(S["product"], n + 1)
                            e.sem_inc(S["held"], 1)
                            nc.scalar.activation(proj[:, bass.ds(n, 1), :].rearrange("p a m -> p (a m)"), psG[k][:, 0:16], ACT.Copy).then_inc(S["evacuated"], 1)
                        over_tiles(e, body)
                        e.wait_ge(S["evacuated"], NT + 2)

                    @block.gpsimd
                    def _(e):
                        def body(i, k):
                            n = 2 * i + k
                            fetch_ends(e, tail, n, i, k, S, end_in, PER)
                            inverse_root(e, k, S, n * PER + 10)
                            inverse_root(e, k, S, n * PER + TAIL_STEPS + 4)
                            e.wait_ge(S["step"], n * PER + PER)
                            e.sem_inc(S["held"], 1)
                            e.dma_start(x2_d[bass.ds(n * P, P), :], x_new[k][:, :]).then_inc(h_kept[k], 16)
                            e.dma_start(xf_d[bass.ds(n * P, P), :], h_new[k][:, :]).then_inc(h_kept[k], 16)
                        over_tiles(e, body)
                        for k in range(2):
                            e.wait_ge(h_kept[k], 32 * (NT // 2 + (NT % 2 if k == 0 else 0)))

        def gat_keys():
            C = T_GAT // P
            with phase() as sc:
                raw = [sb(f"raw{r}", [P, T_GAT], I32, sc) for r in range(2)]
                rawf = [sb(f"rawf{r}", [P, T_GAT], F32, sc) for r in range(2)]
                part = [sb(f"gat_part{r}", [P, T_GAT], I32, sc) for r in range(2)]
                ps = [[sc.enter_context(nc.psum_tensor(f"k_ps{r}{h}", [P, 512], F32)) for h in range(2)] for r in range(2)]
                k_in, k_step, k_turned = sem("k_in"), sem("k_step"), sem("k_turned")
                with nc.Block() as block:
                    @block.sync
                    def _(e):
                        for r in range(2):
                            e.dma_start(raw[r][:, :], a["L0_ffn_edge_index"][r, :].rearrange("(p t) -> p t", t=T_GAT)).then_inc(k_in, 16)
                        e.wait_ge(k_in, 32)

                    @block.tensor
                    def _(e):
                        e.wait_ge(k_step, 2)
                        for r in range(2):
                            for c in range(C):
                                m = nc.tensor.transpose(ps[r][c // 4][:, (c % 4) * P:(c % 4 + 1) * P], rawf[r][:, c * P:(c + 1) * P], ident[:, :])
                        m.then_inc(k_turned, 1)

                    @block.vector
                    def _(e):
                        v = nc.vector
                        st = Steps(e, k_step, 0, 99)
                        e.wait_ge(k_in, 32)
                        st(v.tensor_scalar(rawf[0][:, :], raw[0][:, :], float(N - 1), None, ALU.min))
                        st(v.tensor_copy(rawf[1][:, :], raw[1][:, :]))
                        e.wait_ge(k_turned, 1)
                        for h in range(2):
                            for r in range(2):
                                view = edge_pair[:, :, r].rearrange("p (q c) -> p c q", c=C)[:, 4 * h:4 * h + 4, :]
                                st(v.tensor_copy(view, ps[r][h][:, :].rearrange("p (j q) -> p j q", j=4)))
                            view = gat_dst[:, :].rearrange("p (q c) -> p c q", c=C)[:, 4 * h:4 * h + 4, :]
                            st(v.tensor_copy(view, ps[1][h][:, :].rearrange("p (j q) -> p j q", j=4)))
                        st.wait()
                        st(v.tensor_single_scalar(part[0][:, :], edge_pair[:, :, 1], P - 1, ALU.bitwise_and))
                        st(v.tensor_single_scalar(part[1][:, :], edge_pair[:, :, 1], 7, ALU.logical_shift_right))
                        st.wait()
                        st(v.tensor_copy(gat_lo[:, :], part[0][:, :]))
                        st(v.tensor_copy(gat_hi[:, :], part[1][:, :]))
                        st.wait()

        def finish_gat(v, st, cnt):
            st(v.tensor_scalar(gat_has[:, :], cnt[:, :], 1.0, None, ALU.min))
            st(v.tensor_scalar(gat_last_i[:, :], gat_after[:, :], -1.0, 0.0, ALU.add, ALU.max))
            st.wait()
            st(v.tensor_scalar(gat_tmp[:, :], gat_has[:, :], -1.0, 1.0, ALU.mult, ALU.add))
            st(v.tensor_tensor(gat_tmp2[:, :], gat_first[:, :], gat_has[:, :], ALU.mult))
            st.wait()
            st(v.tensor_tensor(gat_tmp[:, :], gat_tmp[:, :], gat_spare[:, :], ALU.mult))
            st.wait()
            st(v.tensor_tensor(gat_tmp[:, :], gat_tmp[:, :], gat_tmp2[:, :], ALU.add))
            st.wait()
            st(v.tensor_copy(gat_start_i[:, :], gat_tmp[:, :]))
            st.wait()

        def gat_sort():
            G = 8
            turns = T_GAT // (2 * G)
            with phase() as sc:
                eq_lo = [sb(f"s_eq_lo{j}", [P, G, P], BF16, sc) for j in range(2)]
                eq_hi = [sb(f"s_eq_hi{j}", [P, G, KH], BF16, sc) for j in range(2)]
                rows = [sb(f"s_rows{j}", [P, G * P], I32, sc) for j in range(2)]
                dst_s = [sb(f"s_dst{j}", [P, G], F32, sc) for j in range(2)]
                identb = sb("s_identb", [P, P], BF16, sc)
                eqT = [sb(f"s_eqT{j}", [P, P], F32, sc) for j in range(2)]
                base = [sb(f"s_base{j}", [P, KH], F32, sc) for j in range(2)]
                junk = sb("s_junk", [P, P], F32, sc)
                junk2 = sb("s_junk2", [P, KH], F32, sc)
                rank = [sb(f"s_rank{j}", [P, G], F32, sc) for j in range(2)]
                place = [sb(f"s_place{j}", [P, G], F32, sc) for j in range(2)]
                place_i = [sb(f"s_place_i{j}", [P, G], I32, sc) for j in range(2)]
                pair_s = [sb(f"s_pair{j}", [P, G, 2], I32, sc) for j in range(2)]
                psT = [sc.enter_context(nc.psum_tensor(f"s_psT{j}", [P, 1024], BF16)) for j in range(2)]
                psB = [sc.enter_context(nc.psum_tensor(f"s_psB{j}", [P, 512], F32)) for j in range(2)]
                psR = sc.enter_context(nc.psum_tensor("s_psR", [P, 512], F32))
                (b_set, eq_ready, turned, eqT_ready, based, looked, added, dst_set, ranked, placed, placed_i, pair_set, held) = (
                    sem(f"s_{n}") for n in ("b_set", "eq_ready", "turned", "eqT_ready", "based", "looked", "added", "dst_set", "ranked",
                                            "placed", "placed_i", "pair_set", "held"))
                rows_in = [sem(f"s_rows_in{j}") for j in range(2)]
                sent = [[sem(f"s_sent{j}_{g}") for g in range(G)] for j in range(2)]
                with nc.Block() as block:
                    @block.sync
                    def _(e):
                        def body(i):
                            for j in range(2):
                                if later(i):
                                    e.wait_ge(ranked, (2 * i + j - 1) * G)
                                src = a["L0_ffn_edge_index"][1, bass.ds((2 * i + j) * G * P, G * P)]
                                e.dma_start(rows[j][:, :], src.unsqueeze(0).to_broadcast([P, G * P])).then_inc(rows_in[j], 16)
                        body(0)
                        with e.Fori(1, turns) as i:
                            body(i)

                    @block.vector
                    def _(e):
                        v = nc.vector
                        v.tensor_copy(identb[:, :], ident[:, :]).then_inc(b_set, 1)

                        def body(i):
                            for j in range(2):
                                g0 = 2 * i + j
                                if later(i):
                                    e.wait_ge(added, (g0 - 1) * G + 1)
                                    e.wait_ge(placed, (g0 - 1) * G)
                                at = bass.ds(g0 * G, G)
                                v.tensor_tensor(eq_lo[j][:, :, :], gat_lo[:, at].unsqueeze(2).to_broadcast([P, G, P]),
                                                iota_row[:, :].unsqueeze(1).to_broadcast([P, G, P]), ALU.is_equal).then_inc(eq_ready, 1)
                                v.tensor_tensor(eq_hi[j][:, :, :], gat_hi[:, at].unsqueeze(2).to_broadcast([P, G, KH]),
                                                iota_row[:, 0:KH].unsqueeze(1).to_broadcast([P, G, KH]), ALU.is_equal).then_inc(eq_ready, 1)
                                if later(i):
                                    e.wait_ge(ranked, (g0 - 1) * G)
                                    e.sem_inc(held, 1)
                                v.tensor_copy(dst_s[j][:, :], gat_dst[:, at]).then_inc(dst_set, 1)
                                e.wait_ge(dst_set, g0 + 1)
                                e.wait_ge(rows_in[j], 16 * (i + 1))
                                for g in range(G):
                                    if later(i) or j or g:
                                        e.wait_ge(ranked, g0 * G + g)
                                    v.scalar_tensor_tensor(out=junk[:, :], in0=rows[j][:, g * P:(g + 1) * P], scalar=dst_s[j][:, g:g + 1],
                                                           in1=earlier[:, :], op0=ALU.is_equal, op1=ALU.mult,
                                                           accum_out=rank[j][:, g:g + 1]).then_inc(ranked, 1)
                                e.wait_ge(ranked, (g0 + 1) * G)
                                e.wait_ge(eq_ready, 2 * g0 + 2)
                                for g in range(G):
                                    e.wait_ge(looked, g0 * G + g + 1)
                                    if later(i) or j or g:
                                        e.wait_ge(placed, g0 * G + g)
                                    v.scalar_tensor_tensor(out=junk2[:, :], in0=psB[g % 2][:, 0:KH], scalar=rank[j][:, g:g + 1],
                                                           in1=eq_hi[j][:, g, :], op0=ALU.add, op1=ALU.mult,
                                                           accum_out=place[j][:, g:g + 1]).then_inc(placed, 1)
                                e.wait_ge(placed, (g0 + 1) * G)
                                if later(i):
                                    for g in range(G):
                                        e.wait_ge(sent[j][g], 16 * i)
                                v.tensor_copy(place_i[j][:, :], place[j][:, :]).then_inc(placed_i, 1)
                        body(0)
                        with e.Fori(1, turns) as i:
                            body(i)

                    @block.tensor
                    def _(e):
                        nc.tensor.matmul(psR[:, 0:KH], ident[:, :], gat_first[:, :], start=True, stop=True).then_inc(added, 1)
                        e.wait_ge(b_set, 1)

                        def body(i):
                            for j in range(2):
                                g0 = 2 * i + j
                                e.wait_ge(eq_ready, 2 * g0 + 2)
                                for g in range(G):
                                    t = g0 * G + g
                                    first = not later(i) and not j and g < 2
                                    if not first:
                                        e.wait_ge(eqT_ready, t - 1)
                                    nc.tensor.transpose(psT[g % 2][:, 0:P], eq_lo[j][:, g, :], identb[:, :]).then_inc(turned, 1)
                                    e.wait_ge(eqT_ready, t + 1)
                                    e.wait_ge(based, t + 1)
                                    if not first:
                                        e.wait_ge(placed, t - 1)
                                    nc.tensor.matmul(psB[g % 2][:, 0:KH], eqT[g % 2][:, :], base[g % 2][:, :], start=True, stop=True).then_inc(looked, 1)
                                    nc.tensor.matmul(psR[:, 0:KH], eq_lo[j][:, g, :], eq_hi[j][:, g, :], start=False, stop=True,
                                                     skip_group_check=True).then_inc(added, 1)
                        body(0)
                        with e.Fori(1, turns) as i:
                            body(i)

                    @block.scalar
                    def _(e):
                        def body(i):
                            for j in range(2):
                                for g in range(G):
                                    t = (2 * i + j) * G + g
                                    if not (not later(i) and not j and g < 2):
                                        e.wait_ge(looked, t - 1)
                                    e.wait_ge(added, t + 1)
                                    nc.scalar.activation(base[g % 2][:, :], psR[:, 0:KH], ACT.Copy).then_inc(based, 1)
                                    e.wait_ge(turned, t + 1)
                                    nc.scalar.activation(eqT[g % 2][:, :], psT[g % 2][:, 0:P], ACT.Copy).then_inc(eqT_ready, 1)
                        body(0)
                        with e.Fori(1, turns) as i:
                            body(i)

                    @block.gpsimd
                    def _(e):
                        def body(i):
                            for j in range(2):
                                g0 = 2 * i + j
                                if later(i):
                                    for g in range(G):
                                        e.wait_ge(sent[j][g], 16 * i)
                                    e.sem_inc(held, 1)
                                e.tensor_copy(pair_s[j][:, :, :], edge_pair[:, bass.ds(g0 * G, G), :]).then_inc(pair_set, 1)
                                e.wait_ge(pair_set, g0 + 1)
                                e.wait_ge(placed_i, g0 + 1)
                                e.sem_inc(held, 1)
                                for g in range(G):
                                    e.indirect_dma_start(out=sorted_d[:, :], out_offset=bass.IndirectOffsetOnAxis(ap=place_i[j][:, g:g + 1], axis=0),
                                                         in_=pair_s[j][:, g, :], in_offset=None).then_inc(sent[j][g], 16)
                        body(0)
                        with e.Fori(1, turns) as i:
                            body(i)
                        for j in range(2):
                            for g in range(G):
                                e.wait_ge(sent[j][g], 16 * turns)

        x2_d, xf_d = dram("x2_d", (NP, D)), dram("xf_d", (NP, D))
        sorted_d = dram("sorted_d", (E_GAT, 2), I32)
        bounds_gat = dram("bounds_gat", (2, KEYS))
        proj = sb("proj", [P, NT, HEADS * EXPERTS])
        gat_first, gat_after, gat_has, gat_tmp, gat_tmp2, gat_spare = (
            sb(n, [P, KH]) for n in ("gat_first", "gat_after", "gat_has", "gat_tmp", "gat_tmp2", "gat_spare"))
        gat_last_i, gat_start_i, spare_i = (sb(n, [P, KH], I32) for n in ("gat_last_i", "gat_start_i", "spare_i"))
        split_gat, split_gat_i = sb("split_gat", [P, 1]), sb("split_gat_i", [P, 1], I32)
        earlier = sb("earlier", [P, P])

        def gat_constants(gk):
            c_made, c_cast = sem("c_made"), sem("c_cast")
            with nc.Block() as block:
                @block.gpsimd
                def _(e):
                    e.iota(spare_i[:, :], pattern=[[P, KH]], base=E_GAT, channel_multiplier=1).then_inc(c_made, 1)
                    e.iota(split_gat_i[:, :], pattern=[[0, 1]], base=T_GAT, channel_multiplier=T_GAT).then_inc(c_made, 1)
                    e.affine_select(out=earlier[:, :], in_=ones[:, :], compare_op=ALU.is_gt, fill=0.0, base=0,
                                    pattern=[[-1, P]], channel_multiplier=1).then_inc(c_made, 1)
                    e.wait_ge(c_made, 3)

                @block.vector
                def _(e):
                    e.wait_ge(c_made, 2)
                    nc.vector.tensor_copy(gat_spare[:, :], spare_i[:, :]).then_inc(c_cast, 1)
                    nc.vector.tensor_copy(split_gat[:, :], split_gat_i[:, :]).then_inc(c_cast, 1)
                    e.wait_ge(c_cast, 2)

        with phase() as gk:
            gat_constants(gk)
            edge_pair = sb("edge_pair", [P, T_GAT, 2], I32, gk)
            gat_dst, gat_lo, gat_hi = (sb(n, [P, T_GAT], F32, gk) for n in ("gat_dst", "gat_lo", "gat_hi"))
            gat_keys()
            count("gat", gat_lo, gat_hi, T_GAT, gat_first, gat_after, bounds_gat, finish_gat)
            gat_sort()
        node_loop(0)
        edge_loop(0)
        node_loop(1)
        edge_loop(1)
        gate_rows()

        REDUCE_LAST = AX.X
        BIG = 1e30
        gat_table = dram("gat_table", (NP, REC))
        mx_d = dram("mx_d", (E_GAT, HEADS))
        start_d = dram("start_d", (E_GAT + KEYS, 2 * HEADS))
        node_d = dram("node_d", (NP, 2 * HEADS))
        run20_d = dram("run20_d", (E_GAT, REC))
        a_src, a_dst = (sb(n, [P, NT, HEADS]) for n in ("a_src", "a_dst"))
        gates = sb("gates", [P, NT, EXPERTS])
        C16 = HEADS * EXPERTS

        def spread(ap, shape):
            return ap.unsqueeze(len(shape) - 1).to_broadcast(shape)

        def gat_records(sc, srt):
            rec = sb("rec_all", [P, NT, REC], F32, sc)
            att = [sb(f"att_v{r}", [P, C16], F32, sc) for r in range(2)]
            tmp = [sb(f"att_tmp{r}", [P, NT, C16], F32, sc) for r in range(2)]
            att_in, r_step, rec_out, srt_in = sem("att_in"), sem("r_step"), sem("rec_out"), sem("srt_in")
            with nc.Block() as block:
                @block.sync
                def _(e):
                    for r, n in enumerate(("L0_ffn_att_src", "L0_ffn_att_dst")):
                        e.dma_start(att[r][:, :], a[n].rearrange("h x -> (h x)").unsqueeze(0).to_broadcast([P, C16])).then_inc(att_in, 16)
                    e.dma_start(srt[:, :, :], sorted_d[:, :].rearrange("(p t) c -> p t c", t=T_GAT)).then_inc(srt_in, 16)
                    e.wait_ge(r_step, 6)
                    e.dma_start(gat_table[:, :].rearrange("(t p) c -> p t c", p=P), rec[:, :, :]).then_inc(rec_out, 16)
                    e.wait_ge(rec_out, 16)
                    e.wait_ge(srt_in, 16)

                @block.vector
                def _(e):
                    v = nc.vector
                    st = Steps(e, r_step, 0, 99)
                    e.wait_ge(att_in, 32)
                    for r in range(2):
                        st(v.tensor_tensor(tmp[r][:, :, :], proj[:, :, :], att[r][:, :].unsqueeze(1).to_broadcast([P, NT, C16]), ALU.mult))
                    for r, dst in enumerate((a_src, a_dst)):
                        st.wait()
                        st(v.reduce_sum(dst[:, :, :].rearrange("p n h -> p (n h)"),
                                        tmp[r][:, :, :].rearrange("p n (h x) -> p (n h) x", x=EXPERTS), REDUCE_LAST))
                    st.wait()
                    st(v.tensor_copy(rec[:, :, 0:HEADS], a_src[:, :, :]))
                    st(v.tensor_copy(rec[:, :, HEADS:REC], proj[:, :, :]))

        def gat_gather(srt, rec):
            with phase() as sc:
                H = U // 2
                turns = T_GAT // U
                got = sb("t_got", [P, U, REC], F32, sc)
                idx = sb("t_idx", [P, U], I32, sc)
                idx_set, held, taken = sem("t_idx_set"), sem("t_held"), sem("t_taken")
                arrived = [sem(f"t_arrived{j}") for j in range(U)]
                with nc.Block() as block:
                    @block.gpsimd
                    def _(e):
                        def body(i):
                            if later(i):
                                for j in range(U):
                                    e.wait_ge(arrived[j], 16 * i)
                            e.sem_inc(held, 1)
                            e.tensor_copy(idx[:, :], srt[:, bass.ds(i * U, U), 0]).then_inc(idx_set, 1)
                            for h in range(2):
                                if later(i):
                                    e.wait_ge(taken, (i - 1) * 2 + h + 1)
                                if h == 0:
                                    e.wait_ge(idx_set, i + 1)
                                e.sem_inc(held, 1)
                                for j in range(h * H, (h + 1) * H):
                                    e.indirect_dma_start(out=got[:, j, :], out_offset=None, in_=gat_table[:, :],
                                                         in_offset=bass.IndirectOffsetOnAxis(ap=idx[:, j:j + 1], axis=0)).then_inc(arrived[j], 16)
                        body(0)
                        with e.Fori(1, turns) as i:
                            body(i)

                    @block.scalar
                    def _(e):
                        with e.Fori(0, turns) as i:
                            for h in range(2):
                                for j in range(h * H, (h + 1) * H):
                                    e.wait_ge(arrived[j], 16 * (i + 1))
                                e.sem_inc(held, 1)
                                nc.scalar.activation(rec[:, bass.ds(i * U + h * H, H), :], got[:, h * H:(h + 1) * H, :], ACT.Copy).then_inc(taken, 1)
                        e.wait_ge(taken, 2 * turns)

        def gat_softmax(srt, rec, sc):
            T = T_GAT
            mx = sb("mx", [P, T, HEADS], F32, sc)
            fill = sb("fill", [P, T, 2 * HEADS], F32, sc)
            keep_t = sb("keep_t", [P, T], F32, sc)
            pen = sb("pen", [P, T], F32, sc)
            cols = sb("edge_cols", [P, 3 * HEADS], F32, sc)
            rows = sb("edge_rows", [HEADS, 3, P], F32, sc)
            link, thru, thru_pen, link_pen, c_out, c_in = (
                sb(n, [HEADS, P], F32, sc) for n in ("link", "thru", "thru_pen", "link_pen", "c_out", "c_in"))
            c_col = sb("c_col", [P, HEADS], F32, sc)
            mx_end = sb("mx_end", [P, NT, HEADS], F32, sc)
            zz = sb("zz", [P, NT, HEADS], F32, sc)
            pen_n = sb("pen_n", [P, NT], F32, sc)
            first_node = sb("first_node", [P, 1], I32, sc)
            init = sb("init", [P, 2 * HEADS], F32, sc)
            ps = sc.enter_context(nc.psum_tensor("m_ps", [P, 512], F32))
            ps2 = sc.enter_context(nc.psum_tensor("m_ps2", [P, 512], F32))
            d, t1, t2, mx_out, ends_in, zeroed, node_out, started, init_in, fill_in, z_set, ex_done, run_out, run_in = (
                sem(f"m_{n}") for n in ("d", "t1", "t2", "mx_out", "ends_in", "zeroed", "node_out", "started", "init_in", "fill_in",
                                        "z_set", "ex_done", "run_out", "run_in"))
            mark = {}
            with nc.Block() as block:
                @block.vector
                def _(e):
                    v = nc.vector
                    st = Steps(e, d, 0, 999)
                    dst = srt[:, :, 1]
                    st(v.memset(keep_t[:, 0:1], 1.0))
                    st(v.tensor_tensor(keep_t[:, 1:T], dst[:, 1:T], dst[:, 0:T - 1], ALU.is_equal))
                    st(v.memset(fill[:, :, :], 0.0))
                    mark["zero"] = st.k
                    st.wait()
                    st(v.tensor_scalar(pen[:, :], keep_t[:, :], -1.0, BIG, ALU.add, ALU.mult))
                    st(v.tensor_copy(cols[:, HEADS:2 * HEADS], dst[:, 0:1].to_broadcast([P, HEADS])))
                    st(v.tensor_copy(cols[:, 2 * HEADS:3 * HEADS], dst[:, T - 1:T].to_broadcast([P, HEADS])))
                    st(v.tensor_scalar(first_node[:, :], dst[:, 0:1], float(NP - 1), None, ALU.min))
                    st.wait()
                    for h in range(HEADS):
                        st(v.tensor_tensor_scan(mx[:, :, h], pen[:, :], rec[:, :, h], -BIG, ALU.add, ALU.max))
                    st.wait()
                    st(v.tensor_copy(cols[:, 0:HEADS], mx[:, T - 1, :]))
                    mark["cols"] = st.k
                    e.wait_ge(t1, 1)
                    st(v.tensor_copy(rows[:, :, :].rearrange("h c p -> h (c p)"), ps[0:HEADS, 0:3 * P]))
                    st.wait()
                    st(v.memset(link[:, 0:1], 0.0))
                    st(v.tensor_tensor(link[:, 1:P], rows[:, 1, 1:P], rows[:, 2, 0:P - 1], ALU.is_equal))
                    st(v.tensor_tensor(thru[:, :], rows[:, 1, :], rows[:, 2, :], ALU.is_equal))
                    st.wait()
                    st(v.tensor_tensor(thru[:, :], thru[:, :], link[:, :], ALU.mult))
                    st.wait()
                    st(v.tensor_scalar(thru_pen[:, :], thru[:, :], -1.0, BIG, ALU.add, ALU.mult))
                    st(v.tensor_scalar(link_pen[:, :], link[:, :], -1.0, BIG, ALU.add, ALU.mult))
                    st.wait()
                    st(v.tensor_tensor_scan(c_out[:, :], thru_pen[:, :], rows[:, 0, :], -BIG, ALU.add, ALU.max))
                    st.wait()
                    st(v.memset(c_in[:, 0:1], -BIG))
                    st(v.tensor_tensor(c_in[:, 1:P], c_out[:, 0:P - 1], link_pen[:, 1:P], ALU.add))
                    mark["c_in"] = st.k
                    e.wait_ge(t2, 1)
                    st(v.tensor_copy(c_col[:, :], ps2[:, 0:HEADS]))
                    st.wait()
                    for h in range(HEADS):
                        st(v.tensor_tensor_scan(mx[:, :, h], pen[:, :], rec[:, :, h], c_col[:, h:h + 1], ALU.add, ALU.max))
                    mark["mx"] = st.k
                    st(v.tensor_scalar(pen_n[:, :], gat_has[:, 0:NT], -1.0, BIG, ALU.add, ALU.mult))
                    e.wait_ge(ends_in, 16 * NT)
                    st.wait()
                    st(v.tensor_tensor(mx_end[:, :, :], mx_end[:, :, :], spread(pen_n[:, :], [P, NT, HEADS]), ALU.add))
                    st.wait()
                    st(v.tensor_tensor(mx_end[:, :, :], mx_end[:, :, :], a_src[:, :, :], ALU.max))
                    st.wait()
                    st(v.tensor_tensor(zz[:, :, :], mx_end[:, :, :], a_dst[:, :, :], ALU.add))
                    st.wait()
                    st(v.scalar_tensor_tensor(out=node8[:, :, HEADS:2 * HEADS], in0=zz[:, :, :], scalar=0.2, in1=zz[:, :, :],
                                              op0=ALU.mult, op1=ALU.max))
                    st(v.tensor_copy(node8[:, :, 0:HEADS], a_dst[:, :, :]))
                    mark["node8"] = st.k
                    e.wait_ge(fill_in, 16)
                    e.wait_ge(init_in, 16)
                    st(v.memset(fill[:, 0:1, :], 0.0))
                    st.wait()
                    for c in range(2 * HEADS):
                        st(v.tensor_tensor_scan(fill[:, :, c], keep_t[:, :], fill[:, :, c], init[:, c:c + 1], ALU.mult, ALU.add))
                    st.wait()
                    z = rec[:, :, 0:HEADS]
                    st(v.tensor_tensor(z, z, fill[:, :, 0:HEADS], ALU.add))
                    st.wait()
                    st(v.scalar_tensor_tensor(out=z, in0=z, scalar=0.2, in1=z, op0=ALU.mult, op1=ALU.max))
                    st.wait()
                    st(v.tensor_tensor(z, z, fill[:, :, HEADS:2 * HEADS], ALU.subtract))
                    st.wait()
                    st(v.tensor_scalar(z, z, 0.0, None, ALU.min))
                    mark["z"] = st.k
                    e.wait_ge(ex_done, 1)
                    for h in range(HEADS):
                        cells = rec[:, :, HEADS + EXPERTS * h:HEADS + EXPERTS * (h + 1)]
                        st(v.tensor_tensor(cells, cells, rec[:, :, h:h + 1].to_broadcast([P, T, EXPERTS]), ALU.mult))
                    st.wait()
                    for c in range(REC):
                        st(v.tensor_tensor_scan(rec[:, :, c], keep_t[:, :], rec[:, :, c], 0.0, ALU.mult, ALU.add))
                    st.wait()
                    st(v.tensor_copy(carry[:, 0:REC], rec[:, T - 1, :]))
                    mark["run"] = st.k
                    st.wait()

                @block.tensor
                def _(e):
                    e.wait_ge(d, mark["cols"])
                    for c in range(3):
                        m = nc.tensor.transpose(ps[0:HEADS, c * P:(c + 1) * P], cols[:, c * HEADS:(c + 1) * HEADS], ident[:, :])
                    m.then_inc(t1, 1)
                    e.wait_ge(d, mark["c_in"])
                    nc.tensor.transpose(ps2[:, 0:HEADS], c_in[:, :], ident[0:HEADS, 0:HEADS]).then_inc(t2, 1)

                @block.scalar
                def _(e):
                    e.wait_ge(d, mark["z"])
                    nc.scalar.activation(rec[:, :, 0:HEADS], rec[:, :, 0:HEADS], ACT.Exp).then_inc(ex_done, 1)

                @block.sync
                def _(e):
                    e.wait_ge(d, mark["zero"])
                    e.dma_start(start_d[0:E_GAT, :].rearrange("(p t) c -> p t c", t=T), fill[:, :, :]).then_inc(zeroed, 16)
                    e.wait_ge(d, mark["mx"])
                    e.dma_start(mx_d[:, :].rearrange("(p t) c -> p t c", t=T), mx[:, :, :]).then_inc(mx_out, 16)
                    e.wait_ge(d, mark["node8"])
                    e.dma_start(node_d[:, :].rearrange("(t p) c -> p t c", p=P), node8[:, :, :]).then_inc(node_out, 16)
                    e.wait_ge(started, 16 * NT)
                    e.dma_start(fill[:, :, :], start_d[0:E_GAT, :].rearrange("(p t) c -> p t c", t=T)).then_inc(fill_in, 16)
                    e.wait_ge(d, mark["run"])
                    e.dma_start(run20_d[:, :].rearrange("(p t) c -> p t c", t=T), rec[:, :, :]).then_inc(run_out, 16)

                @block.gpsimd
                def _(e):
                    e.wait_ge(mx_out, 16)
                    for n in range(NT):
                        e.indirect_dma_start(out=mx_end[:, n, :], out_offset=None, in_=mx_d[:, :],
                                             in_offset=bass.IndirectOffsetOnAxis(ap=gat_last_i[:, n:n + 1], axis=0)).then_inc(ends_in, 16)
                    e.wait_ge(node_out, 16)
                    e.indirect_dma_start(out=init[:, :], out_offset=None, in_=node_d[:, :],
                                         in_offset=bass.IndirectOffsetOnAxis(ap=first_node[:, 0:1], axis=0)).then_inc(init_in, 16)
                    e.wait_ge(zeroed, 16)
                    for n in range(NT):
                        e.indirect_dma_start(out=start_d[:, :], out_offset=bass.IndirectOffsetOnAxis(ap=gat_start_i[:, n:n + 1], axis=0),
                                             in_=node8[:, n, :], in_offset=None).then_inc(started, 16)
                    e.wait_ge(run_out, 16)
                    for n in range(NT):
                        e.indirect_dma_start(out=tot[:, n, :], out_offset=None, in_=run20_d[:, :],
                                             in_offset=bass.IndirectOffsetOnAxis(ap=gat_last_i[:, n:n + 1], axis=0)).then_inc(run_in, 16)
                    e.wait_ge(run_in, 16 * NT)

        def gat_cross():
            with phase() as sc:
                rows = [sb(f"x_rows{k}", [P, 2, P], F32, sc) for k in range(2)]
                below = [sb(f"x_below{k}", [P, P], F32, sc) for k in range(2)]
                cross = [sb(f"x_cross{k}", [P, P], F32, sc) for k in range(2)]
                ps = [sc.enter_context(nc.psum_tensor(f"x_ps{k}", [P, 512], F32)) for k in range(2)]
                step, crossed = sem("x_step"), sem("x_crossed")
                rows_in = [sem(f"x_rows_in{k}") for k in range(2)]
                with nc.Block() as block:
                    @block.sync
                    def _(e):
                        def body(i, k):
                            n = 2 * i + k
                            if later(i):
                                e.wait_ge(step, (n - 2) * 3 + 2)
                            for j in range(2):
                                e.dma_start(rows[k][:, j, :], bounds_gat[j, bass.ds(n * P, P)].unsqueeze(0).to_broadcast([P, P])).then_inc(rows_in[k], 16)
                        over_tiles(e, body)

                    @block.vector
                    def _(e):
                        v = nc.vector

                        def body(i, k):
                            n = 2 * i + k
                            st = Steps(e, step, n, 3)
                            e.wait_ge(rows_in[k], 32 * (i + 1))
                            if later(i):
                                e.wait_ge(crossed, n - 1)
                            st(v.tensor_scalar(below[k][:, :], rows[k][:, 0, :], split_gat[:, :], None, ALU.is_lt))
                            st.wait()
                            st(v.scalar_tensor_tensor(out=cross[k][:, :], in0=rows[k][:, 1, :], scalar=split_gat[:, :],
                                                      in1=below[k][:, :], op0=ALU.is_gt, op1=ALU.mult))
                            e.wait_ge(crossed, n + 1)
                            own = tot[:, bass.ds(n, 1), :].rearrange("p a c -> p (a c)")
                            st(v.scalar_tensor_tensor(out=own, in0=own, scalar=gat_has[:, bass.ds(n, 1)], in1=ps[k][:, 0:REC],
                                                      op0=ALU.mult, op1=ALU.add))
                        over_tiles(e, body)
                        e.wait_ge(step, 3 * NT)

                    @block.tensor
                    def _(e):
                        def body(i, k):
                            n = 2 * i + k
                            if later(i):
                                e.wait_ge(step, (n - 1) * 3)
                            e.wait_ge(step, n * 3 + 2)
                            nc.tensor.matmul(ps[k][:, 0:REC], cross[k][:, :], carry[:, 0:REC], start=True, stop=True).then_inc(crossed, 1)
                        over_tiles(e, body)

        def gat_gates():
            with phase() as sc:
                exs, den, sq4 = (sb(f"q_{n}", [P, NT, HEADS], F32, sc) for n in ("exs", "den", "sq4"))
                num, sq = (sb(f"q_{n}", [P, NT, C16], F32, sc) for n in ("num", "sq"))
                score, cmp, place, pick = (sb(f"q_{n}", [P, NT, EXPERTS], F32, sc) for n in ("score", "cmp", "place", "pick"))
                mean, var, rs, best = (sb(f"q_{n}", [P, NT], F32, sc) for n in ("mean", "var", "rs", "best"))
                vec = {n: sb(f"q_v_{n}", [P, C16], F32, sc) for n in ("b_gat", "ln_gamma", "ln_beta")}
                vec_in, d, es_done, rooted, e2_done = (sem(f"q_{n}") for n in ("vec_in", "d", "es_done", "rooted", "e2_done"))
                mark = {}
                w16, w4 = [P, NT, C16], [P, NT, EXPERTS]
                with nc.Block() as block:
                    @block.sync
                    def _(e):
                        for n in vec:
                            e.dma_start(vec[n][:, :], a[f"L0_ffn_{n}"].unsqueeze(0).to_broadcast([P, C16])).then_inc(vec_in, 16)
                        e.wait_ge(vec_in, 48)

                    @block.vector
                    def _(e):
                        v = nc.vector
                        st = Steps(e, d, 0, 999)

                        def do(instruction):
                            st(instruction)
                            st.wait()

                        do(v.tensor_tensor(exs[:, :, :], a_src[:, :, :], a_dst[:, :, :], ALU.add))
                        do(v.scalar_tensor_tensor(out=exs[:, :, :], in0=exs[:, :, :], scalar=0.2, in1=exs[:, :, :], op0=ALU.mult, op1=ALU.max))
                        do(v.tensor_tensor(exs[:, :, :], exs[:, :, :], node8[:, :, HEADS:2 * HEADS], ALU.subtract))
                        mark["exs"] = st.k
                        e.wait_ge(es_done, 1)
                        do(v.tensor_tensor(den[:, :, :], tot[:, :, 0:HEADS], exs[:, :, :], ALU.add))
                        do(v.tensor_scalar(den[:, :, :], den[:, :, :], 1e-16, None, ALU.add))
                        do(v.reciprocal(den[:, :, :], den[:, :, :]))
                        for h in range(HEADS):
                            c = slice(EXPERTS * h, EXPERTS * (h + 1))
                            do(v.tensor_tensor(num[:, :, c], proj[:, :, c], exs[:, :, h:h + 1].to_broadcast(w4), ALU.mult))
                            do(v.tensor_tensor(num[:, :, c], num[:, :, c], tot[:, :, HEADS + EXPERTS * h:HEADS + EXPERTS * (h + 1)], ALU.add))
                            do(v.tensor_tensor(num[:, :, c], num[:, :, c], den[:, :, h:h + 1].to_broadcast(w4), ALU.mult))
                        e.wait_ge(vec_in, 48)
                        do(v.tensor_tensor(num[:, :, :], num[:, :, :], vec["b_gat"][:, :].unsqueeze(1).to_broadcast(w16), ALU.add))
                        do(v.reduce_sum(mean[:, :], num[:, :, :], REDUCE_LAST))
                        do(v.tensor_scalar(mean[:, :], mean[:, :], 1.0 / C16, None, ALU.mult))
                        do(v.tensor_tensor(num[:, :, :], num[:, :, :], spread(mean[:, :], w16), ALU.subtract))
                        do(v.tensor_tensor(sq[:, :, :], num[:, :, :], num[:, :, :], ALU.mult))
                        do(v.reduce_sum(var[:, :], sq[:, :, :], REDUCE_LAST))
                        do(v.tensor_scalar(var[:, :], var[:, :], 1.0 / C16, EPS, ALU.mult, ALU.add))
                        mark["var"] = st.k
                        e.wait_ge(rooted, 1)
                        do(v.tensor_tensor(num[:, :, :], num[:, :, :], spread(rs[:, :], w16), ALU.mult))
                        do(v.tensor_tensor(num[:, :, :], num[:, :, :], vec["ln_gamma"][:, :].unsqueeze(1).to_broadcast(w16), ALU.mult))
                        do(v.tensor_tensor(num[:, :, :], num[:, :, :], vec["ln_beta"][:, :].unsqueeze(1).to_broadcast(w16), ALU.add))
                        do(v.tensor_tensor(score[:, :, :], num[:, :, 0:4], num[:, :, 4:8], ALU.add))
                        do(v.tensor_tensor(score[:, :, :], score[:, :, :], num[:, :, 8:12], ALU.add))
                        do(v.tensor_tensor(score[:, :, :], score[:, :, :], num[:, :, 12:16], ALU.add))
                        do(v.tensor_scalar(score[:, :, :], score[:, :, :], 1.0 / HEADS, None, ALU.mult))
                        do(v.memset(place[:, :, :], 0.0))
                        for j in range(EXPERTS):
                            other = score[:, :, j:j + 1]
                            if j:
                                do(v.tensor_tensor(cmp[:, :, 0:j], other.to_broadcast([P, NT, j]), score[:, :, 0:j], ALU.is_gt))
                                do(v.tensor_tensor(place[:, :, 0:j], place[:, :, 0:j], cmp[:, :, 0:j], ALU.add))
                            m = EXPERTS - 1 - j
                            if m:
                                do(v.tensor_tensor(cmp[:, :, j + 1:EXPERTS], other.to_broadcast([P, NT, m]), score[:, :, j + 1:EXPERTS], ALU.is_ge))
                                do(v.tensor_tensor(place[:, :, j + 1:EXPERTS], place[:, :, j + 1:EXPERTS], cmp[:, :, j + 1:EXPERTS], ALU.add))
                        do(v.tensor_scalar(pick[:, :, :], place[:, :, :], 2.0, None, ALU.is_lt))
                        do(v.reduce_max(best[:, :], score[:, :, :], REDUCE_LAST))
                        do(v.tensor_tensor(score[:, :, :], score[:, :, :], spread(best[:, :], w4), ALU.subtract))
                        mark["score"] = st.k
                        e.wait_ge(e2_done, 1)
                        do(v.tensor_tensor(score[:, :, :], score[:, :, :], pick[:, :, :], ALU.mult))
                        do(v.reduce_sum(best[:, :], score[:, :, :], REDUCE_LAST))
                        do(v.reciprocal(best[:, :], best[:, :]))
                        do(v.tensor_tensor(gates[:, :, :], score[:, :, :], spread(best[:, :], w4), ALU.mult))

                    @block.scalar
                    def _(e):
                        e.wait_ge(d, mark["exs"])
                        nc.scalar.activation(exs[:, :, :], exs[:, :, :], ACT.Exp).then_inc(es_done, 1)
                        e.wait_ge(d, mark["score"])
                        nc.scalar.activation(score[:, :, :], score[:, :, :], ACT.Exp).then_inc(e2_done, 1)

                    @block.gpsimd
                    def _(e):
                        e.wait_ge(d, mark["var"])
                        e.tensor_tensor(rs[:, :], var[:, :], minus_half[:, :].to_broadcast([P, NT]), ALU.pow).then_inc(rooted, 1)

        def experts():
            FC = FF // P
            with phase() as sc:
                w1 = sb("f_w1", [P, EXPERTS, 2, FF], F32, sc)
                w2 = sb("f_w2", [P, EXPERTS, FC, D], F32, sc)
                b1 = sb("f_b1", [P, EXPERTS, FC], F32, sc)
                b2 = sb("f_b2", [P, EXPERTS, D], F32, sc)
                xf = [sb(f"f_xf{k}", [P, 2, D], F32, sc) for k in range(2)]
                acc = [sb(f"f_acc{k}", [P, 2, D], F32, sc) for k in range(2)]
                xT = sb("f_xT", [P, 2, 2 * P], F32, sc)
                hid = [sb(f"f_hid{j}", [P, FC, 2 * P], F32, sc) for j in range(2)]
                psT = sc.enter_context(nc.psum_tensor("f_psT", [P, 512], F32))
                psU = [sc.enter_context(nc.psum_tensor(f"f_psU{j}", [P, 512], F32)) for j in range(3)]
                psY = [[sc.enter_context(nc.psum_tensor(f"f_psY{j}{m}", [P, 512], F32)) for m in range(2)] for j in range(2)]
                w_in, b_in, turned, xT_ready, up, hidden, down, summed, held, xf_read = (
                    sem(f"f_{n}") for n in ("w_in", "b_in", "turned", "xT_ready", "up", "hidden", "down", "summed", "held", "xf_read"))
                tile_in = [sem(f"f_tile_in{k}") for k in range(2)]
                out_kept = [sem(f"f_out_kept{k}") for k in range(2)]
                PAIRS = -(-NT // 2)
                ADD = 2 * 2 * EXPERTS

                def over_pairs(eng, body):
                    body(0, 0, 2)
                    body(0, 1, 2)
                    with eng.Fori(1, PAIRS // 2) as i:
                        for k in range(2):
                            body(i, k, 2)
                    body(PAIRS // 2, 0, 1)
                assert PAIRS % 2 == 1 and NT % 2 == 1

                with nc.Block() as block:
                    @block.sync
                    def _(e):
                        def load(i, k, m):
                            q = 2 * i + k
                            if later(i):
                                e.wait_ge(turned, q - 1)
                                e.sem_inc(held, 1)
                                e.wait_ge(out_kept[k], 16 * i)
                                e.sem_inc(held, 1)
                            at = bass.ds(q * 2 * P, m * P)
                            e.dma_start(xf[k][:, 0:m, :], xf_d[at, :].rearrange("(m p) c -> p m c", p=P)).then_inc(tile_in[k], 16)
                            e.dma_start(acc[k][:, 0:m, :], x2_d[at, :].rearrange("(m p) c -> p m c", p=P)).then_inc(tile_in[k], 16)
                        for q in range(EXPERTS):
                            e.dma_start(w1[:, q, :, :], a["L0_ffn_W1"][q].rearrange("(c p) f -> p c f", p=P)).then_inc(w_in, 16)
                            e.dma_start(w2[:, q, :, :], a["L0_ffn_W2"][q].rearrange("(c p) d -> p c d", p=P)).then_inc(w_in, 16)
                        over_pairs(e, load)

                    @block.gpsimd
                    def _(e):
                        with nc.allow_non_contiguous_dma(reason="2048 words, once"):
                            e.dma_start(b1[:, :, :], a["L0_ffn_b1"].rearrange("q (c p) -> p q c", p=P)).then_inc(b_in, 16)
                        e.dma_start(b2[:, :, :].rearrange("p q c -> p (q c)"),
                                    a["L0_ffn_b2"].rearrange("q c -> (q c)").unsqueeze(0).to_broadcast([P, EXPERTS * D])).then_inc(b_in, 16)

                        def store(i, k, m):
                            q = 2 * i + k
                            e.wait_ge(summed, q * ADD + m * ADD // 2)
                            e.sem_inc(held, 1)
                            if m == 2:
                                e.dma_start(out[bass.ds(q * 2 * P, 2 * P), :].rearrange("(m p) c -> p m c", p=P), acc[k][:, :, :]).then_inc(out_kept[k], 16)
                            else:
                                e.dma_start(out[q * 2 * P:N, :], acc[k][0:N - q * 2 * P, 0, :]).then_inc(out_kept[k], 16)
                        over_pairs(e, store)
                        for k in range(2):
                            e.wait_ge(out_kept[k], 16 * (PAIRS // 2 + (1 - k)))

                    @block.tensor
                    def _(e):
                        e.wait_ge(w_in, 32 * EXPERTS)

                        def body(i, k, m):
                            q = 2 * i + k
                            cols = m * P
                            e.wait_ge(tile_in[k], 32 * (i + 1))
                            for j in range(m):
                                for c in range(2):
                                    t = nc.tensor.transpose(psT[:, c * 2 * P + j * P:c * 2 * P + (j + 1) * P], xf[k][:, j, c * P:(c + 1) * P], ident[:, :])
                            t.then_inc(turned, 1)
                            e.wait_ge(xT_ready, q + 1)

                            def going_up(x):
                                for f in range(FC):
                                    u = FC * x + f
                                    if later(i) or k or u >= 3:
                                        e.wait_ge(hidden, q * EXPERTS * FC + u - 2)
                                    for c in range(2):
                                        t = nc.tensor.matmul(psU[bank(k, u)][:, 0:cols], w1[:, x, c, f * P:(f + 1) * P], xT[:, c, 0:cols],
                                                             start=(c == 0), stop=(c == 1))
                                    t.then_inc(up, 1)

                            def going_down(x):
                                e.wait_ge(hidden, q * EXPERTS * FC + FC * (x + 1))
                                for j in range(m):
                                    if x >= 2:
                                        e.wait_ge(summed, q * ADD + m * EXPERTS + (x - 2) * m + j + 1)
                                    elif later(i) or k:
                                        e.wait_ge(summed, q * ADD - 2 * (2 - x) + j + 1)
                                    for f in range(FC):
                                        t = nc.tensor.matmul(psY[x % 2][j][:, 0:D], hid[x % 2][:, f, j * P:(j + 1) * P], w2[:, x, f, :],
                                                             start=(f == 0), stop=(f == FC - 1))
                                    t.then_inc(down, 1)
                            going_up(0)
                            for x in range(1, EXPERTS):
                                going_up(x)
                                going_down(x - 1)
                            going_down(EXPERTS - 1)
                        over_pairs(e, body)

                    @block.scalar
                    def _(e):
                        e.wait_ge(b_in, 32)

                        def body(i, k, m):
                            q = 2 * i + k
                            cols = m * P
                            e.wait_ge(turned, q + 1)
                            if later(i) or k:
                                e.wait_ge(up, q * EXPERTS * FC)
                            nc.scalar.activation(xT[:, :, 0:cols], psT[:, :].rearrange("p (c n) -> p c n", c=2)[:, :, 0:cols], ACT.Copy).then_inc(xT_ready, 1)
                            for u in range(EXPERTS * FC):
                                x, f = divmod(u, FC)
                                if f == 0:
                                    if x >= 2:
                                        e.wait_ge(down, q * 2 * EXPERTS + m * (x - 1))
                                    elif later(i) or k:
                                        e.wait_ge(down, q * 2 * EXPERTS - 2 * (1 - x))
                                e.wait_ge(up, q * EXPERTS * FC + u + 1)
                                nc.scalar.activation(hid[x % 2][:, f, 0:cols], psU[bank(k, u)][:, 0:cols], ACT.Gelu,
                                                     bias=b1[:, x, f:f + 1]).then_inc(hidden, 1)
                        over_pairs(e, body)

                    @block.vector
                    def _(e):
                        v = nc.vector
                        e.wait_ge(b_in, 32)

                        def body(i, k, m):
                            q = 2 * i + k
                            e.wait_ge(tile_in[k], 32 * (i + 1))
                            done = 0
                            for part in range(2):
                                for x in range(EXPERTS):
                                    for j in range(m):
                                        if part:
                                            e.wait_ge(down, q * 2 * EXPERTS + x * m + j + 1)
                                        if done >= m:
                                            e.wait_ge(summed, q * ADD + done - m + 1)
                                        g = gates[:, bass.ds(2 * q + j, 1), x]
                                        what = psY[x % 2][j][:, 0:D] if part else b2[:, x, :]
                                        v.scalar_tensor_tensor(out=acc[k][:, j, :], in0=what, scalar=g, in1=acc[k][:, j, :],
                                                               op0=ALU.mult, op1=ALU.add).then_inc(summed, 1)
                                        done += 1
                        over_pairs(e, body)

        def bank(k, u):
            return u % 3

        with phase() as gs:
            tot = sb("tot", [P, NT, REC], F32, gs)
            node8 = sb("node8", [P, NT, 2 * HEADS], F32, gs)
            srt = sb("srt", [P, T_GAT, 2], I32, gs)
            with phase() as g2:
                gat_records(g2, srt)
            with phase() as g3:
                rec = sb("rec", [P, T_GAT, REC], F32, g3)
                gat_gather(srt, rec)
                gat_softmax(srt, rec, g3)
            gat_cross()
            gat_gates()
        experts()


def kernel(**inputs):
    import numpy as _np
    import concourse.bacc as _bacc
    from concourse import mybir as _mybir
    from concourse.bass_utils import run_bass_kernel_spmd as _run

    nc = _bacc.Bacc("TRN2", target_bir_lowering=False, num_devices=1)
    arrays, args = {}, {}
    for name, value in inputs.items():
        v = _np.ascontiguousarray(value)
        arrays[f"in_{name}"] = v
        args[name] = nc.dram_tensor(f"in_{name}", v.shape, _mybir.dt.from_np(v.dtype), kind="ExternalInput").ap()
    out = nc.dram_tensor("out_0", (N, D), F32, kind="ExternalOutput").ap()
    build(nc, args, out)
    r = _run(nc, [arrays], core_ids=[0])
    return r.results[0]["out_0"]
```

```python
import numpy as np
import concourse.bass as bass
from concourse import mybir
from contextlib import ExitStack, contextmanager

F32 = mybir.dt.float32
BF16 = mybir.dt.bfloat16
I32 = mybir.dt.int32
ALU = mybir.AluOpType
ACT = mybir.ActivationFunctionType
AX = mybir.AxisListType

P = 128
N, D = 6250, 256
NT = -(-N // P)
NP = NT * P
NL = NP + P
RELS, BASES = 16, 8
E_GNN, E_GAT = 100000, 131072
U = 16
T_GNN = -(-E_GNN // (P * U)) * U
T_GAT = E_GAT // P
KEYS = 8192
KH = KEYS // P
PAD = KEYS - 1
HEADS, EXPERTS, FF = 4, 4, 512
REC = HEADS + HEADS * EXPERTS
EPS = 1e-5
SG = 4


def over_tiles(eng, body):
    for k in range(2):
        body(0, k)
    with eng.Fori(1, NT // 2) as i:
        for k in range(2):
            body(i, k)
    if NT % 2:
        body(NT // 2, 0)


def later(i):
    return not isinstance(i, int) or i > 0


class Steps:

    def __init__(self, eng, sem, turn, per_turn):
        self.eng, self.sem, self.turn, self.per, self.k = eng, sem, turn, per_turn, 0

    def wait(self):
        if self.k or not isinstance(self.turn, int) or self.turn:
            if self.k:
                self.eng.wait_ge(self.sem, self.turn * self.per + self.k)

    def __call__(self, instruction):
        instruction.then_inc(self.sem, 1)
        self.k += 1


def build(nc, a, out):
    ctx = ExitStack()
    with ctx:
        top = ctx

        def sb(name, shape, dt=F32, scope=None):
            return (scope or top).enter_context(nc.sbuf_tensor(name, shape, dt))

        open_phases = []

        def sem(name):
            handle = nc.alloc_semaphore(name)
            open_phases[-1].append(handle)
            return handle

        @contextmanager
        def phase():
            with ExitStack() as scope:
                open_phases.append([])
                yield scope
                mine = open_phases.pop()
                if mine:
                    nc.clear_and_free_semaphores(mine)
                    nc.all_engine_barrier()


        def dram(name, shape, dt=F32):
            return nc.dram_tensor(name, shape, dt)

        x_pad = dram("x_pad", (NL, D))
        h0_d = dram("h0_d", (NL, D))
        h1_d = dram("h1_d", (NP, D))
        table = [dram(f"table{l}", (NP, RELS * D)) for l in range(2)]
        rooted = [dram(f"rooted{l}", (NP, D)) for l in range(2)]
        run_d = dram("run_d", (P * T_GNN, D))
        bounds_gnn = dram("bounds_gnn", (2, KEYS))

        ident = sb("ident", [P, P])
        upper = sb("upper", [P, P])
        ones = sb("ones", [P, P])
        iota_row = sb("iota_row", [P, P])
        iota_i = sb("iota_i", [P, P], I32)
        split_gnn = sb("split_gnn", [P, 1])
        split_i = sb("split_i", [P, 1], I32)
        hidx = sb("hidx", [P, T_GNN], I32)
        ea = sb("ea", [P, T_GNN])
        keep = sb("keep", [P, T_GNN])
        lo_gnn = sb("lo_gnn", [P, T_GNN])
        hi_gnn = sb("hi_gnn", [P, T_GNN])
        first_gnn = sb("first_gnn", [P, KH])
        after_gnn = sb("after_gnn", [P, KH])
        last_gnn_i = sb("last_gnn_i", [P, KH], I32)
        has_gnn = sb("has_gnn", [P, KH])
        inv_gnn = sb("inv_gnn", [P, KH])
        carry = sb("carry", [P, D])
        minus_half = sb("minus_half", [P, 1])

        with phase() as sc:
            dst_i = sb("dst_i", [P, T_GNN], I32, sc)
            src_i = sb("src_i", [P, T_GNN], I32, sc)
            typ_i = sb("typ_i", [P, T_GNN], I32, sc)
            part_i = sb("part_i", [P, T_GNN], I32, sc)
            zero_rows = sb("zero_rows", [NP - N, D], F32, sc)
            zero_tile = sb("zero_tile", [P, D], F32, sc)
            set_done, edges_in, iota_done, key_step, xpad_done = (
                sem(n) for n in ("set_done", "edges_in", "iota_done", "key_step", "xpad_done"))
            full, rest = E_GNN // T_GNN, E_GNN % T_GNN
            with nc.Block() as block:
                @block.gpsimd
                def _(e):
                    e.memset(dst_i[:, :], PAD).then_inc(set_done, 1)
                    e.memset(src_i[:, :], 0).then_inc(set_done, 1)
                    e.memset(typ_i[:, :], 0).then_inc(set_done, 1)
                    e.memset(ea[:, :], 0.0).then_inc(set_done, 1)
                    e.memset(zero_rows[:, :], 0.0).then_inc(set_done, 1)
                    e.memset(zero_tile[:, :], 0.0).then_inc(set_done, 1)
                    e.memset(ident[:, :], 0.0).then_inc(iota_done, 1)
                    e.memset(ones[:, :], 1.0).then_inc(iota_done, 1)
                    e.memset(minus_half[:, :], -0.5).then_inc(iota_done, 1)
                    e.iota(iota_i[:, :], pattern=[[1, P]], base=0, channel_multiplier=0).then_inc(iota_done, 1)
                    e.iota(split_i[:, :], pattern=[[0, 1]], base=T_GNN, channel_multiplier=T_GNN).then_inc(iota_done, 1)
                    e.wait_ge(iota_done, 5)
                    e.affine_select(out=ident[:, :], in_=ident[:, :], compare_op=ALU.not_equal, fill=1.0, base=0,
                                    pattern=[[-1, P]], channel_multiplier=1).then_inc(iota_done, 1)
                    e.affine_select(out=upper[:, :], in_=ones[:, :], compare_op=ALU.is_ge, fill=0.0, base=0,
                                    pattern=[[1, P]], channel_multiplier=-1).then_inc(iota_done, 1)
                    e.wait_ge(iota_done, 7)

                @block.sync
                def _(e):
                    e.wait_ge(set_done, 6)
                    for buf, arr in ((dst_i, a["dst"]), (src_i, a["src"]), (typ_i, a["edge_type_16"]), (ea, a["edge_weight"])):
                        e.dma_start(buf[0:full, :], arr[0:full * T_GNN].rearrange("(p t) -> p t", t=T_GNN)).then_inc(edges_in, 16)
                        e.dma_start(buf[full:full + 1, 0:rest], arr[full * T_GNN:E_GNN].rearrange("(p t) -> p t", p=1)).then_inc(edges_in, 16)
                    e.dma_start(x_pad[0:N, :], a["x"][:, :]).then_inc(xpad_done, 16)
                    e.dma_start(x_pad[N:NP, :], zero_rows[:, :]).then_inc(xpad_done, 16)
                    e.wait_ge(edges_in, 8 * 16)
                    e.dma_start(x_pad[NP:NL, :], zero_tile[:, :]).then_inc(xpad_done, 16)
                    e.wait_ge(xpad_done, 48)

                @block.vector
                def _(e):
                    st = Steps(e, key_step, 0, 99)
                    e.wait_ge(edges_in, 8 * 16)
                    e.wait_ge(iota_done, 5)
                    v = nc.vector
                    st(v.tensor_copy(iota_row[:, :], iota_i[:, :]))
                    st(v.tensor_copy(split_gnn[:, :], split_i[:, :]))
                    st(v.scalar_tensor_tensor(out=hidx[:, :], in0=src_i[:, :], scalar=float(RELS), in1=typ_i[:, :],
                                              op0=ALU.mult, op1=ALU.add))
                    st(v.memset(keep[:, 0:1], 0.0))
                    st(v.tensor_tensor(keep[:, 1:T_GNN], dst_i[:, 1:T_GNN], dst_i[:, 0:T_GNN - 1], ALU.is_equal))
                    st(v.tensor_single_scalar(part_i[:, :], dst_i[:, :], P - 1, ALU.bitwise_and))
                    st.wait()
                    st(v.tensor_copy(lo_gnn[:, :], part_i[:, :]))
                    st.wait()
                    st(v.tensor_single_scalar(part_i[:, :], dst_i[:, :], 7, ALU.logical_shift_right))
                    st.wait()
                    st(v.tensor_copy(hi_gnn[:, :], part_i[:, :]))

        def count(tag, lo, hi, T, first, after, bounds, finish):
            G = 8
            with phase() as sc:
                eq_lo = [sb(f"{tag}_eq_lo{j}", [P, G, P], BF16, sc) for j in range(2)]
                eq_hi = [sb(f"{tag}_eq_hi{j}", [P, G, KH], BF16, sc) for j in range(2)]
                cnt = sb(f"{tag}_cnt", [P, KH], F32, sc)
                before = sb(f"{tag}_before", [P, KH], F32, sc)
                zb = sb(f"{tag}_zb", [P, P], BF16, sc)
                ps = sc.enter_context(nc.psum_tensor(f"{tag}_ps", [P, 512], F32))
                ps2 = sc.enter_context(nc.psum_tensor(f"{tag}_ps2", [P, 512], F32))
                eq_ready, eq_used, zero_set, counted, tail, ranked, stored = (
                    sem(f"{tag}_{n}") for n in ("eq_ready", "eq_used", "zero_set", "counted", "tail", "ranked", "stored"))
                turns = T // (2 * G)
                with nc.Block() as block:
                    @block.vector
                    def _(e):
                        v = nc.vector
                        v.memset(zb[:, :], 0.0).then_inc(zero_set, 1)
                        with e.Fori(0, turns) as i:
                            for j in range(2):
                                e.wait_ge(eq_used, 2 * i + j + 1)
                                at = bass.ds((2 * i + j) * G, G)
                                v.tensor_tensor(eq_lo[j][:, :, :], lo[:, at].unsqueeze(2).to_broadcast([P, G, P]),
                                                iota_row[:, :].unsqueeze(1).to_broadcast([P, G, P]), ALU.is_equal).then_inc(eq_ready, 1)
                                v.tensor_tensor(eq_hi[j][:, :, :], hi[:, at].unsqueeze(2).to_broadcast([P, G, KH]),
                                                iota_row[:, 0:KH].unsqueeze(1).to_broadcast([P, G, KH]), ALU.is_equal).then_inc(eq_ready, 1)
                        e.wait_ge(counted, 1)
                        st = Steps(e, tail, 0, 99)
                        st(v.tensor_copy(cnt[:, :], ps[:, 0:KH]))
                        st.wait()
                        st(v.tensor_tensor_scan(before[:, :], ones[:, 0:KH], cnt[:, :], 0.0, ALU.mult, ALU.add))
                        st.wait()
                        st(v.tensor_tensor(before[:, :], before[:, :], cnt[:, :], ALU.subtract))
                        e.wait_ge(ranked, 1)
                        st(v.tensor_copy(after[:, :], ps2[:, 0:KH]))
                        st.wait()
                        st(v.tensor_tensor(first[:, :], after[:, :], cnt[:, :], ALU.subtract))
                        finish(v, st, cnt)

                    @block.tensor
                    def _(e):
                        e.wait_ge(zero_set, 1)
                        nc.tensor.matmul(ps[:, 0:KH], zb[:, :], zb[:, 0:KH], start=True, stop=False)
                        e.sem_inc(eq_used, 2)
                        with e.Fori(0, turns) as i:
                            for j in range(2):
                                e.wait_ge(eq_ready, 4 * i + 2 * j + 2)
                                for g in range(G):
                                    m = nc.tensor.matmul(ps[:, 0:KH], eq_lo[j][:, g, :], eq_hi[j][:, g, :], start=False, stop=False)
                                m.then_inc(eq_used, 1)
                        nc.tensor.matmul(ps[:, 0:KH], zb[:, :], zb[:, 0:KH], start=False, stop=True).then_inc(counted, 1)
                        e.wait_ge(tail, 3)
                        nc.tensor.matmul(ps2[:, 0:KH], upper[:, :], cnt[:, :], start=True, stop=False)
                        nc.tensor.matmul(ps2[:, 0:KH], ones[:, :], before[:, :], start=False, stop=True).then_inc(ranked, 1)

                    @block.sync
                    def _(e):
                        e.wait_ge(tail, 5)
                        with nc.allow_non_contiguous_dma(reason="8192 words, once"):
                            e.dma_start(bounds[0, :].rearrange("(h l) -> l h", l=P), first[:, :]).then_inc(stored, 16)
                            e.dma_start(bounds[1, :].rearrange("(h l) -> l h", l=P), after[:, :]).then_inc(stored, 16)
                        e.wait_ge(stored, 32)

        def finish_gnn(v, st, cnt):
            st(v.tensor_scalar(has_gnn[:, :], cnt[:, :], 1.0, None, ALU.min))
            st(v.tensor_scalar(inv_gnn[:, :], cnt[:, :], 1.0, None, ALU.add))
            st.wait()
            st(v.reciprocal(inv_gnn[:, :], inv_gnn[:, :]))
            st(v.tensor_scalar(last_gnn_i[:, :], after_gnn[:, :], -1.0, 0.0, ALU.add, ALU.max))
            st.wait()

        count("gnn", lo_gnn, hi_gnn, T_GNN, first_gnn, after_gnn, bounds_gnn, finish_gnn)

        def make_weights(l, weights, sc):
            basis, att, root = (a[f"L0_gnn_{n}{l + 1}"] for n in ("basis", "att", "root"))
            with phase() as s2:
                bs = [sb(f"basis{l}_{c}", [P, BASES, D], F32, s2) for c in range(2)]
                att_bc = sb(f"att_bc{l}", [P, RELS * BASES], F32, s2)
                loaded, mixed = sem(f"basis_in{l}"), sem(f"mixed{l}")
                with nc.Block() as block:
                    @block.sync
                    def _(e):
                        for c in range(2):
                            e.dma_start(bs[c][:, :, :], basis[:, c * P:(c + 1) * P, :].rearrange("b p o -> p b o")).then_inc(loaded, 16)
                            e.dma_start(weights[c][:, RELS, :], root[c * P:(c + 1) * P, :]).then_inc(loaded, 16)
                        e.dma_start(att_bc[:, :], att.rearrange("r b -> (r b)").unsqueeze(0).to_broadcast([P, RELS * BASES])).then_inc(loaded, 16)
                        e.wait_ge(loaded, 5 * 16)

                    @block.vector
                    def _(e):
                        v = nc.vector
                        e.wait_ge(loaded, 5 * 16)
                        n = 0
                        for b in range(BASES):
                            for r in range(RELS):
                                for c in range(2):
                                    w = weights[c][:, r, :]
                                    s = att_bc[:, r * BASES + b:r * BASES + b + 1]
                                    if b == 0:
                                        v.tensor_scalar(w, bs[c][:, b, :], s, None, ALU.mult).then_inc(mixed, 1)
                                    else:
                                        e.wait_ge(mixed, n - 2 * RELS + 1)
                                        v.scalar_tensor_tensor(out=w, in0=bs[c][:, b, :], scalar=s, in1=w,
                                                               op0=ALU.mult, op1=ALU.add).then_inc(mixed, 1)
                                    n += 1

        def node_loop(l):
            with phase() as sc:
                tag = f"n{l}"
                weights = [sb(f"{tag}_weights{c}", [P, RELS + 1, D], F32, sc) for c in range(2)]
                make_weights(l, weights, sc)
                h_in = [sb(f"{tag}_h_in{k}", [P, D], F32, sc) for k in range(2)]
                h_new = [sb(f"{tag}_h_new{k}", [P, D], F32, sc) for k in range(2)]
                hT = [sb(f"{tag}_hT{k}", [P, 2, P], F32, sc) for k in range(2)]
                prod = [sb(f"{tag}_prod{k}", [P, RELS + 1, D], F32, sc) for k in range(2)]
                psT = [sc.enter_context(nc.psum_tensor(f"{tag}_psT{k}", [P, 512], F32)) for k in range(2)]
                psP = [sc.enter_context(nc.psum_tensor(f"{tag}_psP{j}", [P, 512], F32)) for j in range(3)]
                psC = sc.enter_context(nc.psum_tensor(f"{tag}_psC", [P, 512], F32))
                S = {n: sem(f"{tag}_{n}") for n in (
                    "step", "h_taken", "turned", "hT_ready", "product", "evacuated", "held", "w_used", "carried", "idx_set", "vec_in", "rooted")}
                h_full = [sem(f"{tag}_h_full{k}") for k in range(2)]
                h_kept = [sem(f"{tag}_h_kept{k}") for k in range(2)]
                t_kept = [sem(f"{tag}_t_kept{k}") for k in range(2)]
                end_in = [sem(f"{tag}_end_in{k}") for k in range(2)]
                src_d, keep_d = (x_pad, h0_d) if l == 0 else (h0_d, h1_d)
                tail = tail_buffers(tag, sc) if l else None
                PER = 4 if l == 0 else TAIL_STEPS
                CH = 9
                with nc.Block() as block:
                    @block.sync
                    def _(e):
                        if l:
                            load_vectors(e, tail, l, S["vec_in"])
                        def body(i, k):
                            n = 2 * i + k
                            e.wait_ge(S["h_taken"], n + 1)
                            e.dma_start(h_in[k][:, :], src_d[bass.ds(n * P, P), :]).then_inc(h_full[k], 16)
                            if l:
                                tail_loads(e, tail, l, n, k, h_full[k])
                        over_tiles(e, body)

                    @block.vector
                    def _(e):
                        v = nc.vector
                        e.sem_inc(S["h_taken"], 2)
                        if l:
                            e.wait_ge(S["vec_in"], VECS * 16)

                        def body(i, k):
                            n = 2 * i + k
                            st = Steps(e, S["step"], n, PER)
                            e.wait_ge(h_full[k], (i + 1) * (16 if l == 0 else 16 * TAIL_LOADS))
                            if l == 0:
                                if later(i):
                                    e.wait_ge(h_kept[k], 16 * i)
                                    e.wait_ge(S["turned"], n - 1)
                                layer_norm(e, st, h_new[k], h_in[k], k, n + 1, S)
                                st.wait()
                                assert st.k == PER
                                e.sem_inc(S["h_taken"], 1)
                            else:
                                def free():
                                    if later(i):
                                        e.wait_ge(h_kept[k], 16 * i)
                                        e.wait_ge(S["turned"], n - 1)
                                tail_steps(e, st, tail, l, n, i, k, h_in[k], h_new[k], psC, S, end_in, n + 1, free)
                                e.sem_inc(S["h_taken"], 1)
                        over_tiles(e, body)

                    @block.tensor
                    def _(e):
                        def body(i, k):
                            n = 2 * i + k
                            if l:
                                cross_product(e, tail, n, k, psC, S, PER)
                            e.wait_ge(S["step"], n * PER + PER)
                            for c in range(2):
                                m = nc.tensor.transpose(psT[k][:, c * P:(c + 1) * P], h_new[k][:, c * P:(c + 1) * P], ident[:, :])
                            m.then_inc(S["turned"], 1)
                            e.wait_ge(S["hT_ready"], n + 1)
                            for q in range(CH):
                                e.wait_ge(S["evacuated"], n * CH + q + 1)
                                w = 512 if q < CH - 1 else D
                                for c in range(2):
                                    m = nc.tensor.matmul(psP[q % 3][:, 0:w], hT[k][:, c, :],
                                                         weights[c][:, 2 * q:2 * q + w // D, :].rearrange("p r o -> p (r o)"),
                                                         start=(c == 0), stop=(c == 1))
                                m.then_inc(S["product"], 1)
                        over_tiles(e, body)

                    @block.scalar
                    def _(e):
                        e.sem_inc(S["evacuated"], 3)

                        def body(i, k):
                            n = 2 * i + k
                            e.wait_ge(S["turned"], n + 1)
                            nc.scalar.activation(hT[k][:, :, :].rearrange("p c n -> p (c n)"), psT[k][:, 0:2 * P], ACT.Copy).then_inc(S["hT_ready"], 1)
                            if later(i):
                                e.wait_ge(t_kept[k], 32 * i)
                            for q in range(CH):
                                e.wait_ge(S["product"], n * CH + q + 1)
                                w = 512 if q < CH - 1 else D
                                nc.scalar.activation(prod[k][:, 2 * q:2 * q + w // D, :].rearrange("p r o -> p (r o)"),
                                                     psP[q % 3][:, 0:w], ACT.Copy).then_inc(S["evacuated"], 1)
                            e.wait_ge(S["evacuated"], 3 + (n + 1) * CH)
                            e.dma_start(table[l][bass.ds(n * P, P), :], prod[k][:, 0:RELS, :].rearrange("p r o -> p (r o)")).then_inc(t_kept[k], 16)
                            e.dma_start(rooted[l][bass.ds(n * P, P), :], prod[k][:, RELS, :]).then_inc(t_kept[k], 16)
                        over_tiles(e, body)
                        for k in range(2):
                            e.wait_ge(t_kept[k], 32 * (NT // 2 + (NT % 2 if k == 0 else 0)))

                    @block.gpsimd
                    def _(e):
                        def body(i, k):
                            n = 2 * i + k
                            if l:
                                fetch_ends(e, tail, n, i, k, S, end_in, PER)
                            inverse_root(e, k, S, n * PER + (3 if l == 0 else 10))
                            e.wait_ge(S["step"], n * PER + PER)
                            e.sem_inc(S["held"], 1)
                            e.dma_start(keep_d[bass.ds(n * P, P), :], h_new[k][:, :]).then_inc(h_kept[k], 16)
                        over_tiles(e, body)
                        for k in range(2):
                            e.wait_ge(h_kept[k], 16 * (NT // 2 + (NT % 2 if k == 0 else 0)))

        stats = [sb(f"stats{k}", [P, 6]) for k in range(2)]
        mvs = [sb(f"mv{k}", [P, 2]) for k in range(2)]
        rss = [sb(f"rstd{k}", [P, 1]) for k in range(2)]
        ves = [sb(f"var_eps{k}", [P, 1]) for k in range(2)]

        TAIL_STEPS = 12
        TAIL_LOADS = 4 + 1
        VECS = 3

        def tail_buffers(tag, sc):
            t = {}
            for k in range(2):
                t["rows", k] = sb(f"{tag}_rows{k}", [P, 2, P], F32, sc)
                t["self", k] = sb(f"{tag}_self{k}", [P, D], F32, sc)
                t["root", k] = sb(f"{tag}_root{k}", [P, D], F32, sc)
                t["end", k] = sb(f"{tag}_end{k}", [P, D], F32, sc)
                t["idx", k] = sb(f"{tag}_idx{k}", [P, 1], I32, sc)
                t["cross", k] = sb(f"{tag}_cross{k}", [P, P], F32, sc)
                t["ge", k] = sb(f"{tag}_ge{k}", [P, P], F32, sc)
                t["acc", k] = sb(f"{tag}_acc{k}", [P, D], F32, sc)
            for n in ("bias", "gain", "shift"):
                t[n] = sb(f"{tag}_{n}", [P, D], F32, sc)
            return t

        def load_vectors(e, t, l, vec_in):
            for n, arr in (("bias", f"L0_gnn_bias{l}"), ("gain", f"L0_gnn_ln{l}_g"), ("shift", f"L0_gnn_ln{l}_b")):
                e.dma_start(t[n][:, :], a[arr].unsqueeze(0).to_broadcast([P, D])).then_inc(vec_in, 16)

        def tail_loads(e, t, l, n, k, full):
            for j in range(2):
                e.dma_start(t["rows", k][:, j, :], bounds_gnn[j, bass.ds(n * P, P)].unsqueeze(0).to_broadcast([P, P])).then_inc(full, 16)
            own = table[l - 1][bass.ds(n * P, P), (RELS - 1) * D:RELS * D]
            e.dma_start(t["self", k][:, :], own).then_inc(full, 16)
            e.dma_start(t["root", k][:, :], rooted[l - 1][bass.ds(n * P, P), :]).then_inc(full, 16)

        def fetch_ends(e, t, n, i, k, S, end_in, PER):
            e.wait_ge(S["h_taken"], n + 1)
            e.sem_inc(S["held"], 1)
            e.tensor_copy(t["idx", k][:, :], last_gnn_i[:, bass.ds(n, 1)]).then_inc(S["idx_set"], 1)
            e.wait_ge(S["idx_set"], n + 1)
            e.sem_inc(S["held"], 1)
            e.indirect_dma_start(out=t["end", k][:, :], out_offset=None, in_=run_d[:, :],
                                 in_offset=bass.IndirectOffsetOnAxis(ap=t["idx", k][:, 0:1], axis=0)).then_inc(end_in[k], 16)

        def cross_product(e, t, n, k, psC, S, PER):
            e.wait_ge(S["step"], n * PER + 2)
            nc.tensor.matmul(psC[:, 0:D], t["cross", k][:, :], carry[:, :], start=True, stop=True).then_inc(S["carried"], 1)

        def tail_steps(e, st, t, l, n, i, k, h, h_new, psC, S, end_in, roots, free):
            v = nc.vector
            acc = t["acc", k]
            st(v.tensor_scalar(t["ge", k][:, :], t["rows", k][:, 0, :], split_gnn[:, :], None, ALU.is_lt))
            st.wait()
            st(v.scalar_tensor_tensor(out=t["cross", k][:, :], in0=t["rows", k][:, 1, :], scalar=split_gnn[:, :],
                                      in1=t["ge", k][:, :], op0=ALU.is_gt, op1=ALU.mult))
            e.wait_ge(end_in[k], 16 * (i + 1))
            e.wait_ge(S["carried"], n + 1)
            st(v.scalar_tensor_tensor(out=acc[:, :], in0=t["end", k][:, :], scalar=has_gnn[:, bass.ds(n, 1)],
                                      in1=psC[:, 0:D], op0=ALU.mult, op1=ALU.add))
            st(v.tensor_tensor(t["root", k][:, :], t["root", k][:, :], t["bias"][:, :], ALU.add))
            st.wait()
            st(v.tensor_tensor(acc[:, :], acc[:, :], t["self", k][:, :], ALU.add))
            st.wait()
            st(v.scalar_tensor_tensor(out=acc[:, :], in0=acc[:, :], scalar=inv_gnn[:, bass.ds(n, 1)],
                                      in1=t["root", k][:, :], op0=ALU.mult, op1=ALU.add))
            st.wait()
            st(v.tensor_tensor(acc[:, :], acc[:, :], h[:, :], ALU.add))
            layer_norm(e, st, acc, acc, k, roots, S)
            st.wait()
            st(v.tensor_tensor(acc[:, :], acc[:, :], t["gain"][:, :], ALU.mult))
            free()
            st.wait()
            st(v.tensor_tensor(acc[:, :], acc[:, :], t["shift"][:, :], ALU.add))
            st.wait()
            st(v.tensor_relu(h_new[:, :], acc[:, :]))
            st.wait()
            assert st.k == TAIL_STEPS, st.k

        def inverse_root(e, k, S, step):
            e.wait_ge(S["step"], step)
            e.tensor_tensor(rss[k][:, :], ves[k][:, :], minus_half[:, :], ALU.pow).then_inc(S["rooted"], 1)

        def layer_norm(e, st, dst, src, k, roots, S):
            v = nc.vector
            stat, mv, rs = stats[k], mvs[k], rss[k]
            st.wait()
            st(v.bn_stats(stat[:, :], src[:, :]))
            st.wait()
            e.sem_inc(S["held"], 1)
            st(v.bn_aggr(mv[:, :], stat[:, :]))
            st.wait()
            st(v.tensor_scalar(ves[k][:, :], mv[:, 1:2], EPS, None, ALU.add))
            e.wait_ge(S["rooted"], roots)
            st(v.tensor_scalar(dst[:, :], src[:, :], mv[:, 0:1], rs[:, :], ALU.subtract, ALU.mult))

        TAIL_STEPS = 14

        def edge_loop(l):
            with phase() as sc:
                tag = f"e{l}"
                H = U // 2
                got = sb(f"{tag}_got", [P, U, D], F32, sc)
                msg = sb(f"{tag}_msg", [P, U, D], F32, sc)
                run = sb(f"{tag}_run", [P, U, D], F32, sc)
                idx = sb(f"{tag}_idx", [P, U], I32, sc)
                ea_s = sb(f"{tag}_ea", [P, U], F32, sc)
                keep_s = sb(f"{tag}_keep", [P, U], F32, sc)
                idx_set, held, weighted, summed, ea_set, keep_set = (
                    sem(f"{tag}_{n}") for n in ("idx_set", "held", "weighted", "summed", "ea_set", "keep_set"))
                arrived = [sem(f"{tag}_arrived{j}") for j in range(U)]
                run_kept = [sem(f"{tag}_run_kept{h}") for h in range(2)]
                turns = T_GNN // U
                rows = table[l][:, :].rearrange("n (r o) -> (n r) o", o=D)
                run_view = run_d[:, :].rearrange("(p t) o -> p t o", t=T_GNN)
                with nc.Block() as block:
                    @block.gpsimd
                    def _(e):
                        def body(i, first):
                            if not first:
                                for j in range(U):
                                    e.wait_ge(arrived[j], 16 * i)
                            e.sem_inc(held, 1)
                            e.tensor_copy(idx[:, :], hidx[:, bass.ds(i * U, U)]).then_inc(idx_set, 1)
                            for h in range(2):
                                if not first:
                                    e.wait_ge(weighted, (i - 1) * U + (h + 1) * H)
                                if h == 0:
                                    e.wait_ge(idx_set, i + 1)
                                e.sem_inc(held, 1)
                                for j in range(h * H, (h + 1) * H):
                                    e.indirect_dma_start(out=got[:, j, :], out_offset=None, in_=rows,
                                                         in_offset=bass.IndirectOffsetOnAxis(ap=idx[:, j:j + 1], axis=0)).then_inc(arrived[j], 16)
                        body(0, True)
                        with e.Fori(1, turns) as i:
                            body(i, False)

                    @block.scalar
                    def _(e):
                        def body(i, first):
                            if not first:
                                e.wait_ge(weighted, i * U)
                                e.sem_inc(held, 1)
                            nc.scalar.activation(ea_s[:, :], ea[:, bass.ds(i * U, U)], ACT.Copy).then_inc(ea_set, 1)
                            e.wait_ge(ea_set, i + 1)
                            for j in range(U):
                                e.wait_ge(arrived[j], 16 * (i + 1))
                                if not first:
                                    e.wait_ge(summed, (i - 1) * U + j + 2)
                                nc.scalar.activation(msg[:, j, :], got[:, j, :], ACT.Copy, scale=ea_s[:, j:j + 1]).then_inc(weighted, 1)
                        body(0, True)
                        with e.Fori(1, turns) as i:
                            body(i, False)

                    @block.vector
                    def _(e):
                        v = nc.vector
                        v.memset(run[:, U - 1, :], 0.0).then_inc(summed, 1)

                        def body(i, first):
                            if not first:
                                e.wait_ge(summed, i * U + 1)
                                e.sem_inc(held, 1)
                            v.tensor_copy(keep_s[:, :], keep[:, bass.ds(i * U, U)]).then_inc(keep_set, 1)
                            e.wait_ge(keep_set, i + 1)
                            for j in range(U):
                                if j % H == 0 and not first:
                                    e.wait_ge(run_kept[j // H], 16 * i)
                                e.wait_ge(weighted, i * U + j + 1)
                                e.wait_ge(summed, i * U + j + 1)
                                v.scalar_tensor_tensor(out=run[:, j, :], in0=run[:, (j - 1) % U, :], scalar=keep_s[:, j:j + 1],
                                                       in1=msg[:, j, :], op0=ALU.mult, op1=ALU.add).then_inc(summed, 1)
                        body(0, True)
                        with e.Fori(1, turns) as i:
                            body(i, False)
                        e.wait_ge(summed, T_GNN + 1)
                        v.tensor_copy(carry[:, :], run[:, U - 1, :])

                    @block.sync
                    def _(e):
                        with e.Fori(0, turns) as i:
                            for h in range(2):
                                e.wait_ge(summed, i * U + (h + 1) * H + 1)
                                e.dma_start(run_view[:, bass.ds(i * U + h * H, H), :], run[:, h * H:(h + 1) * H, :]).then_inc(run_kept[h], 16)
                        for h in range(2):
                            e.wait_ge(run_kept[h], 16 * turns)


        def gate_rows():
            with phase() as sc:
                tag = "g"
                wg = sb("wg", [P, 2, HEADS * EXPERTS], F32, sc)
                h_in = [sb(f"g_h_in{k}", [P, D], F32, sc) for k in range(2)]
                x_in = [sb(f"g_x_in{k}", [P, D], F32, sc) for k in range(2)]
                relu = [sb(f"g_relu{k}", [P, D], F32, sc) for k in range(2)]
                x_new = [sb(f"g_x_new{k}", [P, D], F32, sc) for k in range(2)]
                h_new = [sb(f"g_h_new{k}", [P, D], F32, sc) for k in range(2)]
                hT = [sb(f"g_hT{k}", [P, 2, P], F32, sc) for k in range(2)]
                psT = [sc.enter_context(nc.psum_tensor(f"g_psT{k}", [P, 512], F32)) for k in range(2)]
                psG = [sc.enter_context(nc.psum_tensor(f"g_psG{k}", [P, 512], F32)) for k in range(2)]
                psC = sc.enter_context(nc.psum_tensor("g_psC", [P, 512], F32))
                S = {n: sem(f"g_{n}") for n in (
                    "step", "h_taken", "turned", "hT_ready", "product", "evacuated", "held", "carried", "idx_set", "vec_in", "rooted", "wg_in")}
                h_full = [sem(f"g_h_full{k}") for k in range(2)]
                h_kept = [sem(f"g_h_kept{k}") for k in range(2)]
                end_in = [sem(f"g_end_in{k}") for k in range(2)]
                tail = tail_buffers(tag, sc)
                PER = TAIL_STEPS + 5
                with nc.Block() as block:
                    @block.sync
                    def _(e):
                        load_vectors(e, tail, 2, S["vec_in"])
                        e.dma_start(wg[:, :, :], a["L0_ffn_W_gat"].rearrange("(c p) m -> p c m", p=P)).then_inc(S["wg_in"], 16)

                        def body(i, k):
                            n = 2 * i + k
                            e.wait_ge(S["h_taken"], n + 1)
                            e.dma_start(h_in[k][:, :], h1_d[bass.ds(n * P, P), :]).then_inc(h_full[k], 16)
                            e.dma_start(x_in[k][:, :], x_pad[bass.ds(n * P, P), :]).then_inc(h_full[k], 16)
                            tail_loads(e, tail, 2, n, k, h_full[k])
                        over_tiles(e, body)

                    @block.vector
                    def _(e):
                        v = nc.vector
                        e.sem_inc(S["h_taken"], 2)
                        e.wait_ge(S["vec_in"], VECS * 16)

                        def body(i, k):
                            n = 2 * i + k
                            st = Steps(e, S["step"], n, PER)
                            e.wait_ge(h_full[k], (i + 1) * 16 * (TAIL_LOADS + 1))
                            tail_steps(e, st, tail, 2, n, i, k, h_in[k], relu[k], psC, S, end_in, 2 * n + 1, lambda: None)
                            if later(i):
                                e.wait_ge(h_kept[k], 32 * i)
                                e.wait_ge(S["turned"], n - 1)
                            st.wait()
                            st(v.tensor_tensor(x_new[k][:, :], relu[k][:, :], x_in[k][:, :], ALU.add))
                            layer_norm(e, st, h_new[k], x_new[k], k, 2 * n + 2, S)
                            st.wait()
                            assert st.k == PER
                            e.sem_inc(S["h_taken"], 1)
                        over_tiles(e, body)

                    @block.tensor
                    def _(e):
                        e.wait_ge(S["wg_in"], 16)

                        def body(i, k):
                            n = 2 * i + k
                            cross_product(e, tail, n, k, psC, S, PER)
                            e.wait_ge(S["step"], n * PER + PER)
                            for c in range(2):
                                m = nc.tensor.transpose(psT[k][:, c * P:(c + 1) * P], h_new[k][:, c * P:(c + 1) * P], ident[:, :])
                            m.then_inc(S["turned"], 1)
                            e.wait_ge(S["hT_ready"], n + 1)
                            e.wait_ge(S["evacuated"], n + 1)
                            for c in range(2):
                                m = nc.tensor.matmul(psG[k][:, 0:16], hT[k][:, c, :], wg[:, c, :], start=(c == 0), stop=(c == 1))
                            m.then_inc(S["product"], 1)
                        over_tiles(e, body)

                    @block.scalar
                    def _(e):
                        e.sem_inc(S["evacuated"], 2)

                        def body(i, k):
                            n = 2 * i + k
                            e.wait_ge(S["turned"], n + 1)
                            nc.scalar.activation(hT[k][:, :, :].rearrange("p c n -> p (c n)"), psT[k][:, 0:2 * P], ACT.Copy).then_inc(S["hT_ready"], 1)
                            e.wait_ge(S["product"], n + 1)
                            e.sem_inc(S["held"], 1)
                            nc.scalar.activation(proj[:, bass.ds(n, 1), :].rearrange("p a m -> p (a m)"), psG[k][:, 0:16], ACT.Copy).then_inc(S["evacuated"], 1)
                        over_tiles(e, body)
                        e.wait_ge(S["evacuated"], NT + 2)

                    @block.gpsimd
                    def _(e):
                        def body(i, k):
                            n = 2 * i + k
                            fetch_ends(e, tail, n, i, k, S, end_in, PER)
                            inverse_root(e, k, S, n * PER + 10)
                            inverse_root(e, k, S, n * PER + TAIL_STEPS + 4)
                            e.wait_ge(S["step"], n * PER + PER)
                            e.sem_inc(S["held"], 1)
                            e.dma_start(x2_d[bass.ds(n * P, P), :], x_new[k][:, :]).then_inc(h_kept[k], 16)
                            e.dma_start(xf_d[bass.ds(n * P, P), :], h_new[k][:, :]).then_inc(h_kept[k], 16)
                        over_tiles(e, body)
                        for k in range(2):
                            e.wait_ge(h_kept[k], 32 * (NT // 2 + (NT % 2 if k == 0 else 0)))

        def gat_keys():
            C = T_GAT // P
            with phase() as sc:
                raw = [sb(f"raw{r}", [P, T_GAT], I32, sc) for r in range(2)]
                rawf = [sb(f"rawf{r}", [P, T_GAT], F32, sc) for r in range(2)]
                part = [sb(f"gat_part{r}", [P, T_GAT], I32, sc) for r in range(2)]
                ps = [[sc.enter_context(nc.psum_tensor(f"k_ps{r}{h}", [P, 512], F32)) for h in range(2)] for r in range(2)]
                k_in, k_step, k_turned = sem("k_in"), sem("k_step"), sem("k_turned")
                with nc.Block() as block:
                    @block.sync
                    def _(e):
                        for r in range(2):
                            e.dma_start(raw[r][:, :], a["L0_ffn_edge_index"][r, :].rearrange("(p t) -> p t", t=T_GAT)).then_inc(k_in, 16)
                        e.wait_ge(k_in, 32)

                    @block.tensor
                    def _(e):
                        e.wait_ge(k_step, 2)
                        for r in range(2):
                            for c in range(C):
                                m = nc.tensor.transpose(ps[r][c // 4][:, (c % 4) * P:(c % 4 + 1) * P], rawf[r][:, c * P:(c + 1) * P], ident[:, :])
                        m.then_inc(k_turned, 1)

                    @block.vector
                    def _(e):
                        v = nc.vector
                        st = Steps(e, k_step, 0, 99)
                        e.wait_ge(k_in, 32)
                        st(v.tensor_scalar(rawf[0][:, :], raw[0][:, :], float(N - 1), None, ALU.min))
                        st(v.tensor_copy(rawf[1][:, :], raw[1][:, :]))
                        e.wait_ge(k_turned, 1)
                        for h in range(2):
                            for r in range(2):
                                view = edge_pair[:, :, r].rearrange("p (q c) -> p c q", c=C)[:, 4 * h:4 * h + 4, :]
                                st(v.tensor_copy(view, ps[r][h][:, :].rearrange("p (j q) -> p j q", j=4)))
                            view = gat_dst[:, :].rearrange("p (q c) -> p c q", c=C)[:, 4 * h:4 * h + 4, :]
                            st(v.tensor_copy(view, ps[1][h][:, :].rearrange("p (j q) -> p j q", j=4)))
                        st.wait()
                        st(v.tensor_single_scalar(part[0][:, :], edge_pair[:, :, 1], P - 1, ALU.bitwise_and))
                        st(v.tensor_single_scalar(part[1][:, :], edge_pair[:, :, 1], 7, ALU.logical_shift_right))
                        st.wait()
                        st(v.tensor_copy(gat_lo[:, :], part[0][:, :]))
                        st(v.tensor_copy(gat_hi[:, :], part[1][:, :]))
                        st.wait()

        def finish_gat(v, st, cnt):
            st(v.tensor_scalar(gat_has[:, :], cnt[:, :], 1.0, None, ALU.min))
            st(v.tensor_scalar(gat_last_i[:, :], gat_after[:, :], -1.0, 0.0, ALU.add, ALU.max))
            st.wait()
            st(v.tensor_scalar(gat_tmp[:, :], gat_has[:, :], -1.0, 1.0, ALU.mult, ALU.add))
            st(v.tensor_tensor(gat_tmp2[:, :], gat_first[:, :], gat_has[:, :], ALU.mult))
            st.wait()
            st(v.tensor_tensor(gat_tmp[:, :], gat_tmp[:, :], gat_spare[:, :], ALU.mult))
            st.wait()
            st(v.tensor_tensor(gat_tmp[:, :], gat_tmp[:, :], gat_tmp2[:, :], ALU.add))
            st.wait()
            st(v.tensor_copy(gat_start_i[:, :], gat_tmp[:, :]))
            st.wait()

        class Sorter:

            def __init__(self, tag, sc, slots, base_group, start):
                self.SG, self.base_group, self.start = slots, base_group, start
                G = self.G = 8
                self.eq_lo = [sb(f"{tag}_eq_lo{j}", [P, G, P], BF16, sc) for j in range(slots)]
                self.eq_hi = [sb(f"{tag}_eq_hi{j}", [P, G, KH], BF16, sc) for j in range(slots)]
                self.rows = [sb(f"{tag}_rows{j}", [P, G * P], I32, sc) for j in range(slots)]
                self.dst_s = [sb(f"{tag}_dst{j}", [P, G], F32, sc) for j in range(slots)]
                self.rank = [sb(f"{tag}_rank{j}", [P, G], F32, sc) for j in range(slots)]
                self.place = [sb(f"{tag}_place{j}", [P, G], F32, sc) for j in range(slots)]
                self.place_i = [sb(f"{tag}_place_i{j}", [P, G], I32, sc) for j in range(slots)]
                self.pair_s = [sb(f"{tag}_pair{j}", [P, G, 2], I32, sc) for j in range(slots)]
                self.eqT = [sb(f"{tag}_eqT{j}", [P, P], F32, sc) for j in range(2)]
                self.base = [sb(f"{tag}_base{j}", [P, KH], F32, sc) for j in range(2)]
                self.junk = sb(f"{tag}_junk", [P, P], F32, sc)
                self.junk2 = sb(f"{tag}_junk2", [P, KH], F32, sc)
                self.psT = sc.enter_context(nc.psum_tensor(f"{tag}_psT", [P, 1024], BF16))
                self.psB = [sc.enter_context(nc.psum_tensor(f"{tag}_psB{j}", [P, 512], F32)) for j in range(2)]
                self.psR = sc.enter_context(nc.psum_tensor(f"{tag}_psR", [P, 512], F32))
                (self.eq_ready, self.turned, self.eqT_ready, self.based, self.looked, self.added, self.dst_set, self.ranked,
                 self.placed, self.placed_i, self.pair_set, self.held) = (
                    sem(f"{tag}_{n}") for n in ("eq_ready", "turned", "eqT_ready", "based", "looked", "added", "dst_set", "ranked",
                                                "placed", "placed_i", "pair_set", "held"))
                self.rows_in = [sem(f"{tag}_rows_in{j}") for j in range(slots)]
                self.sent = [[sem(f"{tag}_sent{j}_{g}") for g in range(G)] for j in range(slots)]

            def after(self, i, j, g=None):
                if g is not None and g + 1 < self.G:
                    return i, j, g + 1
                at = (i, j + 1) if j + 1 < self.SG else (i + 1, 0)
                return at if g is None else (*at, 0)

            def load_rows(self, e, i, j):
                gl, G = i * self.SG + j, self.G
                if later(i):
                    e.wait_ge(self.ranked, (gl - self.SG + 1) * G)
                    e.sem_inc(self.held, 1)
                src = a["L0_ffn_edge_index"][1, bass.ds((gl + self.base_group) * G * P, G * P)]
                e.dma_start(self.rows[j][:, :], src.unsqueeze(0).to_broadcast([P, G * P])).then_inc(self.rows_in[j], 16)

            def masks(self, e, i, j):
                gl, G, v = i * self.SG + j, self.G, nc.vector
                if later(i):
                    e.wait_ge(self.added, (gl - self.SG + 1) * G + 1)
                    e.wait_ge(self.placed, (gl - self.SG + 1) * G)
                at = bass.ds((gl + self.base_group) * G, G)
                v.tensor_tensor(self.eq_lo[j][:, :, :], gat_lo[:, at].unsqueeze(2).to_broadcast([P, G, P]),
                                iota_row[:, :].unsqueeze(1).to_broadcast([P, G, P]), ALU.is_equal).then_inc(self.eq_ready, 1)
                v.tensor_tensor(self.eq_hi[j][:, :, :], gat_hi[:, at].unsqueeze(2).to_broadcast([P, G, KH]),
                                iota_row[:, 0:KH].unsqueeze(1).to_broadcast([P, G, KH]), ALU.is_equal).then_inc(self.eq_ready, 1)
                if later(i):
                    e.wait_ge(self.ranked, (gl - self.SG + 1) * G)
                    e.sem_inc(self.held, 1)
                v.tensor_copy(self.dst_s[j][:, :], gat_dst[:, at]).then_inc(self.dst_set, 1)
                e.wait_ge(self.dst_set, gl + 1)
                e.wait_ge(self.rows_in[j], 16 * (i + 1))

            def rank_tile(self, e, i, j, g):
                t = (i * self.SG + j) * self.G + g
                if later(i) or j or g:
                    e.wait_ge(self.ranked, t)
                nc.vector.scalar_tensor_tensor(out=self.junk[:, :], in0=self.rows[j][:, g * P:(g + 1) * P], scalar=self.dst_s[j][:, g:g + 1],
                                               in1=earlier[:, :], op0=ALU.is_equal, op1=ALU.mult,
                                               accum_out=self.rank[j][:, g:g + 1]).then_inc(self.ranked, 1)

            def place_tile(self, e, i, j, g):
                gl = i * self.SG + j
                t = gl * self.G + g
                if g == 0:
                    e.wait_ge(self.ranked, (gl + 1) * self.G)
                    e.wait_ge(self.eq_ready, 2 * gl + 2)
                e.wait_ge(self.looked, t + 1)
                if later(i) or j or g:
                    e.wait_ge(self.placed, t)
                nc.vector.scalar_tensor_tensor(out=self.junk2[:, :], in0=self.psB[g % 2][:, 0:KH], scalar=self.rank[j][:, g:g + 1],
                                               in1=self.eq_hi[j][:, g, :], op0=ALU.add, op1=ALU.mult,
                                               accum_out=self.place[j][:, g:g + 1]).then_inc(self.placed, 1)

            def finish_group(self, e, i, j):
                e.wait_ge(self.placed, (i * self.SG + j + 1) * self.G)
                if later(i):
                    for g in range(self.G):
                        e.wait_ge(self.sent[j][g], 16 * i)
                nc.vector.tensor_copy(self.place_i[j][:, :], self.place[j][:, :]).then_inc(self.placed_i, 1)

            def seed(self, e):
                nc.tensor.matmul(self.psR[:, 0:KH], ident[:, :], self.start[:, :], start=True, stop=True).then_inc(self.added, 1)
                self.turn_tile(e, 0, 0, 0)

            def turn_tile(self, e, i, j, g):
                gl = i * self.SG + j
                if g == 0:
                    e.wait_ge(self.eq_ready, 2 * gl + 2)
                if later(i) or j or g:
                    e.wait_ge(self.eqT_ready, gl * self.G + g)
                nc.tensor.transpose(self.psT[:, 0:P], self.eq_lo[j][:, g, :], identb[:, :]).then_inc(self.turned, 1)

            def use_tile(self, e, i, j, g):
                t = (i * self.SG + j) * self.G + g
                e.wait_ge(self.eqT_ready, t + 1)
                e.wait_ge(self.based, t + 1)
                if later(i) or j or g >= 2:
                    e.wait_ge(self.placed, t - 1)
                nc.tensor.matmul(self.psB[g % 2][:, 0:KH], self.eqT[g % 2][:, :], self.base[g % 2][:, :], start=True, stop=True).then_inc(self.looked, 1)
                nc.tensor.matmul(self.psR[:, 0:KH], self.eq_lo[j][:, g, :], self.eq_hi[j][:, g, :], start=False, stop=True,
                                 skip_group_check=True).then_inc(self.added, 1)

            def copy_tile(self, e, i, j, g):
                t = (i * self.SG + j) * self.G + g
                if later(i) or j or g >= 2:
                    e.wait_ge(self.looked, t - 1)
                e.wait_ge(self.turned, t + 1)
                nc.scalar.activation(self.eqT[g % 2][:, :], self.psT[:, 0:P], ACT.Copy).then_inc(self.eqT_ready, 1)
                e.wait_ge(self.added, t + 1)
                nc.scalar.activation(self.base[g % 2][:, :], self.psR[:, 0:KH], ACT.Copy).then_inc(self.based, 1)

            def keep_running(self, e, tiles):
                e.wait_ge(self.added, tiles + 1)
                nc.scalar.activation(gat_running[:, :], self.psR[:, 0:KH], ACT.Copy).then_inc(self.held, 1)

            def send_group(self, e, i, j):
                gl, G = i * self.SG + j, self.G
                if later(i):
                    for g in range(G):
                        e.wait_ge(self.sent[j][g], 16 * i)
                    e.sem_inc(self.held, 1)
                e.tensor_copy(self.pair_s[j][:, :, :], edge_pair[:, bass.ds((gl + self.base_group) * G, G), :]).then_inc(self.pair_set, 1)
                e.wait_ge(self.pair_set, gl + 1)
                e.wait_ge(self.placed_i, gl + 1)
                e.sem_inc(self.held, 1)
                for g in range(G):
                    e.indirect_dma_start(out=sorted_d[:, :], out_offset=bass.IndirectOffsetOnAxis(ap=self.place_i[j][:, g:g + 1], axis=0),
                                         in_=self.pair_s[j][:, g, :], in_offset=None).then_inc(self.sent[j][g], 16)

            def all_sent(self, e, turns):
                for j in range(self.SG):
                    for g in range(self.G):
                        e.wait_ge(self.sent[j][g], 16 * turns)

        def over_turns(eng, turns, body):
            body(0)
            with eng.Fori(1, turns) as i:
                body(i)

        def sort_rest(base_group, groups):
            turns = groups // 2
            with phase() as sc:
                so = Sorter("s", sc, 2, base_group, gat_running)
                G = so.G
                with nc.Block() as block:
                    @block.sync
                    def _(e):
                        over_turns(e, turns, lambda i: [so.load_rows(e, i, j) for j in range(2)])

                    @block.vector
                    def _(e):
                        def body(i):
                            for j in range(2):
                                so.masks(e, i, j)
                                for g in range(G):
                                    so.rank_tile(e, i, j, g)
                                for g in range(G):
                                    so.place_tile(e, i, j, g)
                                so.finish_group(e, i, j)
                        over_turns(e, turns, body)

                    @block.tensor
                    def _(e):
                        nc.tensor.matmul(so.psR[:, 0:KH], ident[:, :], so.start[:, :], start=True, stop=True).then_inc(so.added, 1)

                        def body(i):
                            for j in range(2):
                                for g in range(G):
                                    so.turn_tile(e, i, j, g)
                                    so.use_tile(e, i, j, g)
                        over_turns(e, turns, body)

                    @block.scalar
                    def _(e):
                        over_turns(e, turns, lambda i: [so.copy_tile(e, i, j, g) for j in range(2) for g in range(G)])

                    @block.gpsimd
                    def _(e):
                        over_turns(e, turns, lambda i: [so.send_group(e, i, j) for j in range(2)])
                        so.all_sent(e, turns)

        def first_nodes_and_sort():
            TURNS = NT // 2
            CH = 9
            HALF = 2 * CH
            SLOTS = 2 * (HALF + 1)
            with phase() as sc:
                weights = [sb(f"m_weights{c}", [P, RELS + 1, D], F32, sc) for c in range(2)]
                make_weights(0, weights, sc)
                so = Sorter("m", sc, SG, 0, gat_first)
                G = so.G
                TILES = SG * G
                h_in = [sb(f"m_h_in{k}", [P, D], F32, sc) for k in range(2)]
                h_new = [sb(f"m_h_new{k}", [P, D], F32, sc) for k in range(2)]
                hT = [sb(f"m_hT{k}", [P, 2, P], F32, sc) for k in range(2)]
                prod = [sb(f"m_prod{k}", [P, RELS + 1, D], F32, sc) for k in range(2)]
                psT = sc.enter_context(nc.psum_tensor("m_psTh", [P, 512], F32))
                psP = [sc.enter_context(nc.psum_tensor(f"m_psP{q}", [P, 512], F32)) for q in range(3)]
                S = {n: sem(f"m_{n}") for n in ("step", "h_turned", "hT_ready", "product", "evacuated", "held2", "rooted")}
                S["held"] = S["held2"]
                h_full = [sem(f"m_h_full{k}") for k in range(2)]
                h_kept = [sem(f"m_h_kept{k}") for k in range(2)]
                t_kept = [sem(f"m_t_kept{k}") for k in range(2)]
                PER = 4

                def tiles_after(slot):
                    return range(slot * TILES // SLOTS, (slot + 1) * TILES // SLOTS)

                def load(e, i, k):
                    n = 2 * i + k
                    if later(i):
                        e.wait_ge(S["step"], (n - 1) * PER)
                        e.sem_inc(S["held"], 1)
                    e.dma_start(h_in[k][:, :], x_pad[bass.ds(n * P, P), :]).then_inc(h_full[k], 16)

                def norm_begin(e, i, k):
                    n = 2 * i + k
                    e.wait_ge(h_full[k], 16 * (i + 1))
                    st = Steps(e, S["step"], n, PER)
                    st(nc.vector.bn_stats(stats[k][:, :], h_in[k][:, :]))
                    st.wait()
                    e.sem_inc(S["held"], 1)
                    st(nc.vector.bn_aggr(mvs[k][:, :], stats[k][:, :]))
                    st.wait()
                    st(nc.vector.tensor_scalar(ves[k][:, :], mvs[k][:, 1:2], EPS, None, ALU.add))

                def norm_end(e, i, k):
                    n = 2 * i + k
                    e.wait_ge(S["rooted"], n + 1)
                    if later(i):
                        e.wait_ge(h_kept[k], 16 * i)
                        e.wait_ge(S["h_turned"], n - 1)
                    nc.vector.tensor_scalar(h_new[k][:, :], h_in[k][:, :], mvs[k][:, 0:1], rss[k][:, :], ALU.subtract, ALU.mult).then_inc(S["step"], 1)

                def root(e, i, k):
                    inverse_root(e, k, S, (2 * i + k) * PER + 3)

                def keep(e, i, k):
                    n = 2 * i + k
                    e.wait_ge(S["step"], (n + 1) * PER)
                    e.sem_inc(S["held"], 1)
                    e.dma_start(h0_d[bass.ds(n * P, P), :], h_new[k][:, :]).then_inc(h_kept[k], 16)

                with nc.Block() as block:
                    @block.sync
                    def _(e):
                        for k in range(2):
                            load(e, 0, k)
                        so.load_rows(e, 0, 0)

                        def body(i):
                            for j in range(SG):
                                if j in (0, SG // 2):
                                    load(e, i + 1, int(j > 0))
                                so.load_rows(e, *so.after(i, j))
                        over_turns(e, TURNS, body)

                    @block.vector
                    def _(e):
                        for k in range(2):
                            norm_begin(e, 0, k)
                            norm_end(e, 0, k)
                        so.masks(e, 0, 0)
                        for g in range(G):
                            so.rank_tile(e, 0, 0, g)

                        def body(i):
                            for j in range(SG):
                                nxt = so.after(i, j)
                                so.masks(e, *nxt)
                                if j in (0, SG // 2):
                                    norm_begin(e, i + 1, int(j > 0))
                                for g in range(G):
                                    so.place_tile(e, i, j, g)
                                    so.rank_tile(e, *nxt, g)
                                so.finish_group(e, i, j)
                                if j in (SG // 2 - 1, SG - 1):
                                    norm_end(e, i + 1, int(j == SG - 1))
                        over_turns(e, TURNS, body)

                    def multiply(e, i, k, sorting):
                        n = 2 * i + k
                        e.wait_ge(S["step"], (n + 1) * PER)
                        if later(i) or k:
                            e.wait_ge(S["hT_ready"], n)
                        for c in range(2):
                            m = nc.tensor.transpose(psT[:, c * P:(c + 1) * P], h_new[k][:, c * P:(c + 1) * P], ident[:, :])
                        m.then_inc(S["h_turned"], 1)
                        sorting(k * (HALF + 1))
                        e.wait_ge(S["hT_ready"], n + 1)
                        for q in range(CH):
                            if later(i) or k or q >= 3:
                                e.wait_ge(S["evacuated"], n * CH + q - 2)
                            w = 512 if q < CH - 1 else D
                            for c in range(2):
                                m = nc.tensor.matmul(psP[q % 3][:, 0:w], hT[k][:, c, :],
                                                     weights[c][:, 2 * q:2 * q + w // D, :].rearrange("p r o -> p (r o)"),
                                                     start=(c == 0), stop=(c == 1))
                                if c:
                                    m.then_inc(S["product"], 1)
                                sorting(k * (HALF + 1) + 1 + 2 * q + c)

                    @block.tensor
                    def _(e):
                        so.seed(e)

                        def body(i):
                            def sorting(slot):
                                for t in tiles_after(slot):
                                    so.use_tile(e, i, *divmod(t, G))
                                    so.turn_tile(e, *so.after(i, *divmod(t, G)))
                            for k in range(2):
                                multiply(e, i, k, sorting)
                        over_turns(e, TURNS, body)
                        multiply(e, TURNS, 0, lambda slot: None)

                    def evacuate(e, i, k, sorting):
                        n = 2 * i + k
                        e.wait_ge(S["h_turned"], n + 1)
                        if later(i):
                            e.wait_ge(S["product"], (n - 1) * CH)
                        nc.scalar.activation(hT[k][:, :, :].rearrange("p c n -> p (c n)"), psT[:, 0:2 * P], ACT.Copy).then_inc(S["hT_ready"], 1)
                        sorting(k * (HALF + 1))
                        if later(i):
                            e.wait_ge(t_kept[k], 32 * i)
                        for q in range(CH):
                            sorting(k * (HALF + 1) + 1 + 2 * q)
                            e.wait_ge(S["product"], n * CH + q + 1)
                            w = 512 if q < CH - 1 else D
                            nc.scalar.activation(prod[k][:, 2 * q:2 * q + w // D, :].rearrange("p r o -> p (r o)"),
                                                 psP[q % 3][:, 0:w], ACT.Copy).then_inc(S["evacuated"], 1)
                            sorting(k * (HALF + 1) + 2 + 2 * q)
                        e.wait_ge(S["evacuated"], (n + 1) * CH)
                        e.sem_inc(S["held"], 1)
                        e.dma_start(table[0][bass.ds(n * P, P), :], prod[k][:, 0:RELS, :].rearrange("p r o -> p (r o)")).then_inc(t_kept[k], 16)
                        e.dma_start(rooted[0][bass.ds(n * P, P), :], prod[k][:, RELS, :]).then_inc(t_kept[k], 16)

                    @block.scalar
                    def _(e):
                        so.copy_tile(e, 0, 0, 0)

                        def body(i):
                            def sorting(slot):
                                for t in tiles_after(slot):
                                    so.copy_tile(e, *so.after(i, *divmod(t, G)))
                            for k in range(2):
                                evacuate(e, i, k, sorting)
                        over_turns(e, TURNS, body)
                        evacuate(e, TURNS, 0, lambda slot: None)
                        so.keep_running(e, TURNS * TILES)
                        for k in range(2):
                            e.wait_ge(t_kept[k], 32 * (TURNS + (1 - k)))

                    @block.gpsimd
                    def _(e):
                        for k in range(2):
                            root(e, 0, k)
                            keep(e, 0, k)

                        def body(i):
                            for j in range(SG):
                                if j in (0, SG // 2):
                                    root(e, i + 1, int(j > 0))
                                so.send_group(e, i, j)
                                if j in (SG // 2 - 1, SG - 1):
                                    keep(e, i + 1, int(j == SG - 1))
                        over_turns(e, TURNS, body)
                        so.all_sent(e, TURNS)
                        for k in range(2):
                            e.wait_ge(h_kept[k], 16 * (TURNS + 1))

        x2_d, xf_d = dram("x2_d", (NP, D)), dram("xf_d", (NP, D))
        sorted_d = dram("sorted_d", (E_GAT, 2), I32)
        y_d = dram("y_d", (NP, EXPERTS, D))
        bounds_gat = dram("bounds_gat", (2, KEYS))
        proj = sb("proj", [P, NT, HEADS * EXPERTS])
        gat_first, gat_after, gat_has, gat_tmp, gat_tmp2, gat_spare = (
            sb(n, [P, KH]) for n in ("gat_first", "gat_after", "gat_has", "gat_tmp", "gat_tmp2", "gat_spare"))
        gat_last_i, gat_start_i, spare_i = (sb(n, [P, KH], I32) for n in ("gat_last_i", "gat_start_i", "spare_i"))
        split_gat, split_gat_i = sb("split_gat", [P, 1]), sb("split_gat_i", [P, 1], I32)
        earlier = sb("earlier", [P, P])
        identb = sb("identb", [P, P], BF16)
        gat_running = sb("gat_running", [P, KH])

        def gat_constants(gk):
            c_made, c_cast = sem("c_made"), sem("c_cast")
            with nc.Block() as block:
                @block.gpsimd
                def _(e):
                    e.iota(spare_i[:, :], pattern=[[P, KH]], base=E_GAT, channel_multiplier=1).then_inc(c_made, 1)
                    e.iota(split_gat_i[:, :], pattern=[[0, 1]], base=T_GAT, channel_multiplier=T_GAT).then_inc(c_made, 1)
                    e.affine_select(out=earlier[:, :], in_=ones[:, :], compare_op=ALU.is_gt, fill=0.0, base=0,
                                    pattern=[[-1, P]], channel_multiplier=1).then_inc(c_made, 1)
                    e.wait_ge(c_made, 3)

                @block.vector
                def _(e):
                    e.wait_ge(c_made, 2)
                    nc.vector.tensor_copy(gat_spare[:, :], spare_i[:, :]).then_inc(c_cast, 1)
                    nc.vector.tensor_copy(split_gat[:, :], split_gat_i[:, :]).then_inc(c_cast, 1)
                    nc.vector.tensor_copy(identb[:, :], ident[:, :]).then_inc(c_cast, 1)
                    e.wait_ge(c_cast, 3)

        with phase() as gk:
            gat_constants(gk)
            edge_pair = sb("edge_pair", [P, T_GAT, 2], I32, gk)
            gat_dst, gat_lo, gat_hi = (sb(n, [P, T_GAT], F32, gk) for n in ("gat_dst", "gat_lo", "gat_hi"))
            gat_keys()
            count("gat", gat_lo, gat_hi, T_GAT, gat_first, gat_after, bounds_gat, finish_gat)
            first_nodes_and_sort()
            sort_rest(NT // 2 * SG, T_GAT // 8 - NT // 2 * SG)
        edge_loop(0)
        node_loop(1)
        edge_loop(1)
        gate_rows()

        REDUCE_LAST = AX.X
        BIG = 1e30
        gat_table = dram("gat_table", (NP, REC))
        mx_d = dram("mx_d", (E_GAT, HEADS))
        start_d = dram("start_d", (E_GAT + KEYS, 2 * HEADS))
        node_d = dram("node_d", (NP, 2 * HEADS))
        run20_d = dram("run20_d", (E_GAT, REC))
        a_src, a_dst = (sb(n, [P, NT, HEADS]) for n in ("a_src", "a_dst"))
        gates = sb("gates", [P, NT, EXPERTS])
        C16 = HEADS * EXPERTS

        def spread(ap, shape):
            return ap.unsqueeze(len(shape) - 1).to_broadcast(shape)

        def gat_records(sc, srt):
            rec = sb("rec_all", [P, NT, REC], F32, sc)
            att = [sb(f"att_v{r}", [P, C16], F32, sc) for r in range(2)]
            tmp = [sb(f"att_tmp{r}", [P, NT, C16], F32, sc) for r in range(2)]
            att_in, r_step, rec_out, srt_in = sem("att_in"), sem("r_step"), sem("rec_out"), sem("srt_in")
            with nc.Block() as block:
                @block.sync
                def _(e):
                    for r, n in enumerate(("L0_ffn_att_src", "L0_ffn_att_dst")):
                        e.dma_start(att[r][:, :], a[n].rearrange("h x -> (h x)").unsqueeze(0).to_broadcast([P, C16])).then_inc(att_in, 16)
                    e.dma_start(srt[:, :, :], sorted_d[:, :].rearrange("(p t) c -> p t c", t=T_GAT)).then_inc(srt_in, 16)
                    e.wait_ge(r_step, 6)
                    e.dma_start(gat_table[:, :].rearrange("(t p) c -> p t c", p=P), rec[:, :, :]).then_inc(rec_out, 16)
                    e.wait_ge(rec_out, 16)
                    e.wait_ge(srt_in, 16)

                @block.vector
                def _(e):
                    v = nc.vector
                    st = Steps(e, r_step, 0, 99)
                    e.wait_ge(att_in, 32)
                    for r in range(2):
                        st(v.tensor_tensor(tmp[r][:, :, :], proj[:, :, :], att[r][:, :].unsqueeze(1).to_broadcast([P, NT, C16]), ALU.mult))
                    for r, dst in enumerate((a_src, a_dst)):
                        st.wait()
                        st(v.reduce_sum(dst[:, :, :].rearrange("p n h -> p (n h)"),
                                        tmp[r][:, :, :].rearrange("p n (h x) -> p (n h) x", x=EXPERTS), REDUCE_LAST))
                    st.wait()
                    st(v.tensor_copy(rec[:, :, 0:HEADS], a_src[:, :, :]))
                    st(v.tensor_copy(rec[:, :, HEADS:REC], proj[:, :, :]))

        def gat_gather(srt, rec, sc):
            H = U // 2
            turns = T_GAT // U
            got = sb("t_got", [P, U, REC], F32, sc)
            idx = sb("t_idx", [P, U], I32, sc)
            idx_set, held, taken = sem("t_idx_set"), sem("t_held"), sem("t_taken")
            arrived = [sem(f"t_arrived{j}") for j in range(U)]

            def fetch(e):
                def body(i):
                    if later(i):
                        for j in range(U):
                            e.wait_ge(arrived[j], 16 * i)
                    e.sem_inc(held, 1)
                    e.tensor_copy(idx[:, :], srt[:, bass.ds(i * U, U), 0]).then_inc(idx_set, 1)
                    for h in range(2):
                        if later(i):
                            e.wait_ge(taken, (i - 1) * 2 + h + 1)
                        if h == 0:
                            e.wait_ge(idx_set, i + 1)
                        e.sem_inc(held, 1)
                        for j in range(h * H, (h + 1) * H):
                            e.indirect_dma_start(out=got[:, j, :], out_offset=None, in_=gat_table[:, :],
                                                 in_offset=bass.IndirectOffsetOnAxis(ap=idx[:, j:j + 1], axis=0)).then_inc(arrived[j], 16)
                body(0)
                with e.Fori(1, turns) as i:
                    body(i)

            def file(e):
                with e.Fori(0, turns) as i:
                    for h in range(2):
                        for j in range(h * H, (h + 1) * H):
                            e.wait_ge(arrived[j], 16 * (i + 1))
                        e.sem_inc(held, 1)
                        nc.vector.tensor_copy(rec[:, bass.ds(i * U + h * H, H), :], got[:, h * H:(h + 1) * H, :]).then_inc(taken, 1)
                e.wait_ge(taken, 2 * turns)
            return fetch, file

        def gat_softmax(srt, rec, sc):
            T = T_GAT
            mx = sb("mx", [P, T, HEADS], F32, sc)
            fill = sb("fill", [P, T, 2 * HEADS], F32, sc)
            keep_t = sb("keep_t", [P, T], F32, sc)
            pen = sb("pen", [P, T], F32, sc)
            cols = sb("edge_cols", [P, 3 * HEADS], F32, sc)
            rows = sb("edge_rows", [HEADS, 3, P], F32, sc)
            link, thru, thru_pen, link_pen, c_out, c_in = (
                sb(n, [HEADS, P], F32, sc) for n in ("link", "thru", "thru_pen", "link_pen", "c_out", "c_in"))
            c_col = sb("c_col", [P, HEADS], F32, sc)
            mx_end = sb("mx_end", [P, NT, HEADS], F32, sc)
            zz = sb("zz", [P, NT, HEADS], F32, sc)
            pen_n = sb("pen_n", [P, NT], F32, sc)
            first_node = sb("first_node", [P, 1], I32, sc)
            init = sb("init", [P, 2 * HEADS], F32, sc)
            ps = sc.enter_context(nc.psum_tensor("m_ps", [P, 512], F32))
            ps2 = sc.enter_context(nc.psum_tensor("m_ps2", [P, 512], F32))
            d, t1, t2, mx_out, ends_in, zeroed, node_out, started, init_in, fill_in, z_set, ex_done, run_out, run_in = (
                sem(f"m_{n}") for n in ("d", "t1", "t2", "mx_out", "ends_in", "zeroed", "node_out", "started", "init_in", "fill_in",
                                        "z_set", "ex_done", "run_out", "run_in"))
            mark = {}
            with nc.Block() as block:
                @block.vector
                def _(e):
                    v = nc.vector
                    st = Steps(e, d, 0, 999)
                    dst = srt[:, :, 1]
                    st(v.memset(keep_t[:, 0:1], 1.0))
                    st(v.tensor_tensor(keep_t[:, 1:T], dst[:, 1:T], dst[:, 0:T - 1], ALU.is_equal))
                    st(v.memset(fill[:, :, :], 0.0))
                    mark["zero"] = st.k
                    st.wait()
                    st(v.tensor_scalar(pen[:, :], keep_t[:, :], -1.0, BIG, ALU.add, ALU.mult))
                    st(v.tensor_copy(cols[:, HEADS:2 * HEADS], dst[:, 0:1].to_broadcast([P, HEADS])))
                    st(v.tensor_copy(cols[:, 2 * HEADS:3 * HEADS], dst[:, T - 1:T].to_broadcast([P, HEADS])))
                    st(v.tensor_scalar(first_node[:, :], dst[:, 0:1], float(NP - 1), None, ALU.min))
                    st.wait()
                    for h in range(HEADS):
                        st(v.tensor_tensor_scan(mx[:, :, h], pen[:, :], rec[:, :, h], -BIG, ALU.add, ALU.max))
                    st.wait()
                    st(v.tensor_copy(cols[:, 0:HEADS], mx[:, T - 1, :]))
                    mark["cols"] = st.k
                    e.wait_ge(t1, 1)
                    st(v.tensor_copy(rows[:, :, :].rearrange("h c p -> h (c p)"), ps[0:HEADS, 0:3 * P]))
                    st.wait()
                    st(v.memset(link[:, 0:1], 0.0))
                    st(v.tensor_tensor(link[:, 1:P], rows[:, 1, 1:P], rows[:, 2, 0:P - 1], ALU.is_equal))
                    st(v.tensor_tensor(thru[:, :], rows[:, 1, :], rows[:, 2, :], ALU.is_equal))
                    st.wait()
                    st(v.tensor_tensor(thru[:, :], thru[:, :], link[:, :], ALU.mult))
                    st.wait()
                    st(v.tensor_scalar(thru_pen[:, :], thru[:, :], -1.0, BIG, ALU.add, ALU.mult))
                    st(v.tensor_scalar(link_pen[:, :], link[:, :], -1.0, BIG, ALU.add, ALU.mult))
                    st.wait()
                    st(v.tensor_tensor_scan(c_out[:, :], thru_pen[:, :], rows[:, 0, :], -BIG, ALU.add, ALU.max))
                    st.wait()
                    st(v.memset(c_in[:, 0:1], -BIG))
                    st(v.tensor_tensor(c_in[:, 1:P], c_out[:, 0:P - 1], link_pen[:, 1:P], ALU.add))
                    mark["c_in"] = st.k
                    e.wait_ge(t2, 1)
                    st(v.tensor_copy(c_col[:, :], ps2[:, 0:HEADS]))
                    st.wait()
                    for h in range(HEADS):
                        st(v.tensor_tensor_scan(mx[:, :, h], pen[:, :], rec[:, :, h], c_col[:, h:h + 1], ALU.add, ALU.max))
                    mark["mx"] = st.k
                    st(v.tensor_scalar(pen_n[:, :], gat_has[:, 0:NT], -1.0, BIG, ALU.add, ALU.mult))
                    e.wait_ge(ends_in, 16 * NT)
                    st.wait()
                    st(v.tensor_tensor(mx_end[:, :, :], mx_end[:, :, :], spread(pen_n[:, :], [P, NT, HEADS]), ALU.add))
                    st.wait()
                    st(v.tensor_tensor(mx_end[:, :, :], mx_end[:, :, :], a_src[:, :, :], ALU.max))
                    st.wait()
                    st(v.tensor_tensor(zz[:, :, :], mx_end[:, :, :], a_dst[:, :, :], ALU.add))
                    st.wait()
                    st(v.scalar_tensor_tensor(out=node8[:, :, HEADS:2 * HEADS], in0=zz[:, :, :], scalar=0.2, in1=zz[:, :, :],
                                              op0=ALU.mult, op1=ALU.max))
                    st(v.tensor_copy(node8[:, :, 0:HEADS], a_dst[:, :, :]))
                    mark["node8"] = st.k
                    e.wait_ge(fill_in, 16)
                    e.wait_ge(init_in, 16)
                    st(v.memset(fill[:, 0:1, :], 0.0))
                    st.wait()
                    for c in range(2 * HEADS):
                        st(v.tensor_tensor_scan(fill[:, :, c], keep_t[:, :], fill[:, :, c], init[:, c:c + 1], ALU.mult, ALU.add))
                    st.wait()
                    z = rec[:, :, 0:HEADS]
                    st(v.tensor_tensor(z, z, fill[:, :, 0:HEADS], ALU.add))
                    st.wait()
                    st(v.scalar_tensor_tensor(out=z, in0=z, scalar=0.2, in1=z, op0=ALU.mult, op1=ALU.max))
                    st.wait()
                    st(v.tensor_tensor(z, z, fill[:, :, HEADS:2 * HEADS], ALU.subtract))
                    st.wait()
                    st(v.tensor_scalar(z, z, 0.0, None, ALU.min))
                    mark["z"] = st.k
                    e.wait_ge(ex_done, 1)
                    for h in range(HEADS):
                        cells = rec[:, :, HEADS + EXPERTS * h:HEADS + EXPERTS * (h + 1)]
                        st(v.tensor_tensor(cells, cells, rec[:, :, h:h + 1].to_broadcast([P, T, EXPERTS]), ALU.mult))
                    st.wait()
                    for c in range(REC):
                        st(v.tensor_tensor_scan(rec[:, :, c], keep_t[:, :], rec[:, :, c], 0.0, ALU.mult, ALU.add))
                    st.wait()
                    st(v.tensor_copy(carry[:, 0:REC], rec[:, T - 1, :]))
                    mark["run"] = st.k
                    st.wait()

                @block.tensor
                def _(e):
                    e.wait_ge(d, mark["cols"])
                    for c in range(3):
                        m = nc.tensor.transpose(ps[0:HEADS, c * P:(c + 1) * P], cols[:, c * HEADS:(c + 1) * HEADS], ident[:, :])
                    m.then_inc(t1, 1)
                    e.wait_ge(d, mark["c_in"])
                    nc.tensor.transpose(ps2[:, 0:HEADS], c_in[:, :], ident[0:HEADS, 0:HEADS]).then_inc(t2, 1)

                @block.scalar
                def _(e):
                    e.wait_ge(d, mark["z"])
                    nc.scalar.activation(rec[:, :, 0:HEADS], rec[:, :, 0:HEADS], ACT.Exp).then_inc(ex_done, 1)

                @block.sync
                def _(e):
                    e.wait_ge(d, mark["zero"])
                    e.dma_start(start_d[0:E_GAT, :].rearrange("(p t) c -> p t c", t=T), fill[:, :, :]).then_inc(zeroed, 16)
                    e.wait_ge(d, mark["mx"])
                    e.dma_start(mx_d[:, :].rearrange("(p t) c -> p t c", t=T), mx[:, :, :]).then_inc(mx_out, 16)
                    e.wait_ge(d, mark["node8"])
                    e.dma_start(node_d[:, :].rearrange("(t p) c -> p t c", p=P), node8[:, :, :]).then_inc(node_out, 16)
                    e.wait_ge(started, 16 * NT)
                    e.dma_start(fill[:, :, :], start_d[0:E_GAT, :].rearrange("(p t) c -> p t c", t=T)).then_inc(fill_in, 16)
                    e.wait_ge(d, mark["run"])
                    e.dma_start(run20_d[:, :].rearrange("(p t) c -> p t c", t=T), rec[:, :, :]).then_inc(run_out, 16)

                @block.gpsimd
                def _(e):
                    e.wait_ge(mx_out, 16)
                    for n in range(NT):
                        e.indirect_dma_start(out=mx_end[:, n, :], out_offset=None, in_=mx_d[:, :],
                                             in_offset=bass.IndirectOffsetOnAxis(ap=gat_last_i[:, n:n + 1], axis=0)).then_inc(ends_in, 16)
                    e.wait_ge(node_out, 16)
                    e.indirect_dma_start(out=init[:, :], out_offset=None, in_=node_d[:, :],
                                         in_offset=bass.IndirectOffsetOnAxis(ap=first_node[:, 0:1], axis=0)).then_inc(init_in, 16)
                    e.wait_ge(zeroed, 16)
                    for n in range(NT):
                        e.indirect_dma_start(out=start_d[:, :], out_offset=bass.IndirectOffsetOnAxis(ap=gat_start_i[:, n:n + 1], axis=0),
                                             in_=node8[:, n, :], in_offset=None).then_inc(started, 16)
                    e.wait_ge(run_out, 16)
                    for n in range(NT):
                        e.indirect_dma_start(out=tot[:, n, :], out_offset=None, in_=run20_d[:, :],
                                             in_offset=bass.IndirectOffsetOnAxis(ap=gat_last_i[:, n:n + 1], axis=0)).then_inc(run_in, 16)
                    e.wait_ge(run_in, 16 * NT)

        def gat_cross():
            with phase() as sc:
                rows = [sb(f"x_rows{k}", [P, 2, P], F32, sc) for k in range(2)]
                below = [sb(f"x_below{k}", [P, P], F32, sc) for k in range(2)]
                cross = [sb(f"x_cross{k}", [P, P], F32, sc) for k in range(2)]
                ps = [sc.enter_context(nc.psum_tensor(f"x_ps{k}", [P, 512], F32)) for k in range(2)]
                step, crossed = sem("x_step"), sem("x_crossed")
                rows_in = [sem(f"x_rows_in{k}") for k in range(2)]
                with nc.Block() as block:
                    @block.sync
                    def _(e):
                        def body(i, k):
                            n = 2 * i + k
                            if later(i):
                                e.wait_ge(step, (n - 2) * 3 + 2)
                            for j in range(2):
                                e.dma_start(rows[k][:, j, :], bounds_gat[j, bass.ds(n * P, P)].unsqueeze(0).to_broadcast([P, P])).then_inc(rows_in[k], 16)
                        over_tiles(e, body)

                    @block.vector
                    def _(e):
                        v = nc.vector

                        def body(i, k):
                            n = 2 * i + k
                            st = Steps(e, step, n, 3)
                            e.wait_ge(rows_in[k], 32 * (i + 1))
                            if later(i):
                                e.wait_ge(crossed, n - 1)
                            st(v.tensor_scalar(below[k][:, :], rows[k][:, 0, :], split_gat[:, :], None, ALU.is_lt))
                            st.wait()
                            st(v.scalar_tensor_tensor(out=cross[k][:, :], in0=rows[k][:, 1, :], scalar=split_gat[:, :],
                                                      in1=below[k][:, :], op0=ALU.is_gt, op1=ALU.mult))
                            e.wait_ge(crossed, n + 1)
                            own = tot[:, bass.ds(n, 1), :].rearrange("p a c -> p (a c)")
                            st(v.scalar_tensor_tensor(out=own, in0=own, scalar=gat_has[:, bass.ds(n, 1)], in1=ps[k][:, 0:REC],
                                                      op0=ALU.mult, op1=ALU.add))
                        over_tiles(e, body)
                        e.wait_ge(step, 3 * NT)

                    @block.tensor
                    def _(e):
                        def body(i, k):
                            n = 2 * i + k
                            if later(i):
                                e.wait_ge(step, (n - 1) * 3)
                            e.wait_ge(step, n * 3 + 2)
                            nc.tensor.matmul(ps[k][:, 0:REC], cross[k][:, :], carry[:, 0:REC], start=True, stop=True).then_inc(crossed, 1)
                        over_tiles(e, body)

        def gat_gates():
            with phase() as sc:
                exs, den, sq4 = (sb(f"q_{n}", [P, NT, HEADS], F32, sc) for n in ("exs", "den", "sq4"))
                num, sq = (sb(f"q_{n}", [P, NT, C16], F32, sc) for n in ("num", "sq"))
                score, cmp, place, pick = (sb(f"q_{n}", [P, NT, EXPERTS], F32, sc) for n in ("score", "cmp", "place", "pick"))
                mean, var, rs, best = (sb(f"q_{n}", [P, NT], F32, sc) for n in ("mean", "var", "rs", "best"))
                vec = {n: sb(f"q_v_{n}", [P, C16], F32, sc) for n in ("b_gat", "ln_gamma", "ln_beta")}
                vec_in, d, es_done, rooted, e2_done = (sem(f"q_{n}") for n in ("vec_in", "d", "es_done", "rooted", "e2_done"))
                mark = {}
                w16, w4 = [P, NT, C16], [P, NT, EXPERTS]
                with nc.Block() as block:
                    @block.sync
                    def _(e):
                        for n in vec:
                            e.dma_start(vec[n][:, :], a[f"L0_ffn_{n}"].unsqueeze(0).to_broadcast([P, C16])).then_inc(vec_in, 16)
                        e.wait_ge(vec_in, 48)

                    @block.vector
                    def _(e):
                        v = nc.vector
                        st = Steps(e, d, 0, 999)

                        def do(instruction):
                            st(instruction)
                            st.wait()

                        do(v.tensor_tensor(exs[:, :, :], a_src[:, :, :], a_dst[:, :, :], ALU.add))
                        do(v.scalar_tensor_tensor(out=exs[:, :, :], in0=exs[:, :, :], scalar=0.2, in1=exs[:, :, :], op0=ALU.mult, op1=ALU.max))
                        do(v.tensor_tensor(exs[:, :, :], exs[:, :, :], node8[:, :, HEADS:2 * HEADS], ALU.subtract))
                        mark["exs"] = st.k
                        e.wait_ge(es_done, 1)
                        do(v.tensor_tensor(den[:, :, :], tot[:, :, 0:HEADS], exs[:, :, :], ALU.add))
                        do(v.tensor_scalar(den[:, :, :], den[:, :, :], 1e-16, None, ALU.add))
                        do(v.reciprocal(den[:, :, :], den[:, :, :]))
                        for h in range(HEADS):
                            c = slice(EXPERTS * h, EXPERTS * (h + 1))
                            do(v.tensor_tensor(num[:, :, c], proj[:, :, c], exs[:, :, h:h + 1].to_broadcast(w4), ALU.mult))
                            do(v.tensor_tensor(num[:, :, c], num[:, :, c], tot[:, :, HEADS + EXPERTS * h:HEADS + EXPERTS * (h + 1)], ALU.add))
                            do(v.tensor_tensor(num[:, :, c], num[:, :, c], den[:, :, h:h + 1].to_broadcast(w4), ALU.mult))
                        e.wait_ge(vec_in, 48)
                        do(v.tensor_tensor(num[:, :, :], num[:, :, :], vec["b_gat"][:, :].unsqueeze(1).to_broadcast(w16), ALU.add))
                        do(v.reduce_sum(mean[:, :], num[:, :, :], REDUCE_LAST))
                        do(v.tensor_scalar(mean[:, :], mean[:, :], 1.0 / C16, None, ALU.mult))
                        do(v.tensor_tensor(num[:, :, :], num[:, :, :], spread(mean[:, :], w16), ALU.subtract))
                        do(v.tensor_tensor(sq[:, :, :], num[:, :, :], num[:, :, :], ALU.mult))
                        do(v.reduce_sum(var[:, :], sq[:, :, :], REDUCE_LAST))
                        do(v.tensor_scalar(var[:, :], var[:, :], 1.0 / C16, EPS, ALU.mult, ALU.add))
                        mark["var"] = st.k
                        e.wait_ge(rooted, 1)
                        do(v.tensor_tensor(num[:, :, :], num[:, :, :], spread(rs[:, :], w16), ALU.mult))
                        do(v.tensor_tensor(num[:, :, :], num[:, :, :], vec["ln_gamma"][:, :].unsqueeze(1).to_broadcast(w16), ALU.mult))
                        do(v.tensor_tensor(num[:, :, :], num[:, :, :], vec["ln_beta"][:, :].unsqueeze(1).to_broadcast(w16), ALU.add))
                        do(v.tensor_tensor(score[:, :, :], num[:, :, 0:4], num[:, :, 4:8], ALU.add))
                        do(v.tensor_tensor(score[:, :, :], score[:, :, :], num[:, :, 8:12], ALU.add))
                        do(v.tensor_tensor(score[:, :, :], score[:, :, :], num[:, :, 12:16], ALU.add))
                        do(v.tensor_scalar(score[:, :, :], score[:, :, :], 1.0 / HEADS, None, ALU.mult))
                        do(v.memset(place[:, :, :], 0.0))
                        for j in range(EXPERTS):
                            other = score[:, :, j:j + 1]
                            if j:
                                do(v.tensor_tensor(cmp[:, :, 0:j], other.to_broadcast([P, NT, j]), score[:, :, 0:j], ALU.is_gt))
                                do(v.tensor_tensor(place[:, :, 0:j], place[:, :, 0:j], cmp[:, :, 0:j], ALU.add))
                            m = EXPERTS - 1 - j
                            if m:
                                do(v.tensor_tensor(cmp[:, :, j + 1:EXPERTS], other.to_broadcast([P, NT, m]), score[:, :, j + 1:EXPERTS], ALU.is_ge))
                                do(v.tensor_tensor(place[:, :, j + 1:EXPERTS], place[:, :, j + 1:EXPERTS], cmp[:, :, j + 1:EXPERTS], ALU.add))
                        do(v.tensor_scalar(pick[:, :, :], place[:, :, :], 2.0, None, ALU.is_lt))
                        do(v.reduce_max(best[:, :], score[:, :, :], REDUCE_LAST))
                        do(v.tensor_tensor(score[:, :, :], score[:, :, :], spread(best[:, :], w4), ALU.subtract))
                        mark["score"] = st.k
                        e.wait_ge(e2_done, 1)
                        do(v.tensor_tensor(score[:, :, :], score[:, :, :], pick[:, :, :], ALU.mult))
                        do(v.reduce_sum(best[:, :], score[:, :, :], REDUCE_LAST))
                        do(v.reciprocal(best[:, :], best[:, :]))
                        do(v.tensor_tensor(gates[:, :, :], score[:, :, :], spread(best[:, :], w4), ALU.mult))

                    @block.scalar
                    def _(e):
                        e.wait_ge(d, mark["exs"])
                        nc.scalar.activation(exs[:, :, :], exs[:, :, :], ACT.Exp).then_inc(es_done, 1)
                        e.wait_ge(d, mark["score"])
                        nc.scalar.activation(score[:, :, :], score[:, :, :], ACT.Exp).then_inc(e2_done, 1)

                    @block.gpsimd
                    def _(e):
                        e.wait_ge(d, mark["var"])
                        e.tensor_tensor(rs[:, :], var[:, :], minus_half[:, :].to_broadcast([P, NT]), ALU.pow).then_inc(rooted, 1)

        def experts_and_gather(srt, rec):
            FC = FF // P
            with phase() as sc:
                fetch, file = gat_gather(srt, rec, sc)
                w1 = sb("f_w1", [P, EXPERTS, 2, FF], F32, sc)
                w2 = sb("f_w2", [P, EXPERTS, FC, D], F32, sc)
                b1 = sb("f_b1", [P, EXPERTS, FC], F32, sc)
                b2 = sb("f_b2", [1, EXPERTS, D], F32, sc)
                xf = [sb(f"f_xf{k}", [P, 2, D], F32, sc) for k in range(2)]
                y = sb("f_y", [P, 2, EXPERTS, D], F32, sc)
                xT = sb("f_xT", [P, 2, 2 * P], F32, sc)
                hid = [sb(f"f_hid{j}", [P, FC, 2 * P], F32, sc) for j in range(2)]
                psT = sc.enter_context(nc.psum_tensor("f_psT", [P, 512], F32))
                psU = [sc.enter_context(nc.psum_tensor(f"f_psU{j}", [P, 512], F32)) for j in range(3)]
                psY = [sc.enter_context(nc.psum_tensor(f"f_psY{j}", [P, 2, D], F32)) for j in range(2)]
                w_in, b_in, turned, xT_ready, up, hidden, down, copied, held, y_kept = (
                    sem(f"f_{n}") for n in ("w_in", "b_in", "turned", "xT_ready", "up", "hidden", "down", "copied", "held", "y_kept"))
                tile_in = [sem(f"f_tile_in{k}") for k in range(2)]
                PAIRS = -(-NT // 2)
                UP, DOWN = EXPERTS * FC, EXPERTS

                def over_pairs(eng, body):
                    body(0, 0, 2)
                    body(0, 1, 2)
                    with eng.Fori(1, PAIRS // 2) as i:
                        for k in range(2):
                            body(i, k, 2)
                    body(PAIRS // 2, 0, 1)
                assert PAIRS % 2 == 1 and NT % 2 == 1

                with nc.Block() as block:
                    block.gpsimd(fetch)
                    block.vector(file)

                    @block.sync
                    def _(e):
                        for x in range(EXPERTS):
                            e.dma_start(w1[:, x, :, :], a["L0_ffn_W1"][x].rearrange("(c p) f -> p c f", p=P)).then_inc(w_in, 16)
                            e.dma_start(w2[:, x, :, :], a["L0_ffn_W2"][x].rearrange("(c p) d -> p c d", p=P)).then_inc(w_in, 16)
                        with nc.allow_non_contiguous_dma(reason="2048 words, once"):
                            e.dma_start(b1[:, :, :], a["L0_ffn_b1"].rearrange("q (c p) -> p q c", p=P)).then_inc(b_in, 16)
                        e.dma_start(b2[:, :, :], a["L0_ffn_b2"].unsqueeze(0)).then_inc(b_in, 16)

                        def load(i, k, m):
                            q = 2 * i + k
                            if later(i):
                                e.wait_ge(turned, q - 1)
                                e.sem_inc(held, 1)
                            e.dma_start(xf[k][:, 0:m, :], xf_d[bass.ds(q * 2 * P, m * P), :].rearrange("(m p) c -> p m c", p=P)).then_inc(tile_in[k], 16)
                        over_pairs(e, load)

                    @block.tensor
                    def _(e):
                        e.wait_ge(w_in, 32 * EXPERTS)
                        e.wait_ge(b_in, 32)

                        def body(i, k, m):
                            q = 2 * i + k
                            cols = m * P
                            e.wait_ge(tile_in[k], 16 * (i + 1))
                            if later(i) or k:
                                e.wait_ge(xT_ready, q)
                            for j in range(m):
                                for c in range(2):
                                    t = nc.tensor.transpose(psT[:, c * 2 * P + j * P:c * 2 * P + (j + 1) * P], xf[k][:, j, c * P:(c + 1) * P], ident[:, :])
                            t.then_inc(turned, 1)
                            e.wait_ge(xT_ready, q + 1)

                            def going_up(x):
                                for f in range(FC):
                                    u = FC * x + f
                                    if u >= 3:
                                        e.wait_ge(hidden, q * UP + u - 2)
                                    elif later(i) or k:
                                        e.wait_ge(hidden, q * UP)
                                    for c in range(2):
                                        t = nc.tensor.matmul(psU[u % 3][:, 0:cols], w1[:, x, c, f * P:(f + 1) * P], xT[:, c, 0:cols],
                                                             start=(c == 0), stop=(c == 1))
                                    t.then_inc(up, 1)

                            def going_down(x):
                                e.wait_ge(hidden, q * UP + FC * (x + 1))
                                if later(i) or k or x >= 2:
                                    e.wait_ge(copied, q * DOWN + x - 1)
                                for j in range(m):
                                    nc.tensor.matmul(psY[x % 2][:, j, :], ones[0:1, :], b2[0:1, x, :], start=True, stop=False)
                                    for f in range(FC):
                                        t = nc.tensor.matmul(psY[x % 2][:, j, :], hid[x % 2][:, f, j * P:(j + 1) * P], w2[:, x, f, :],
                                                             start=False, stop=(f == FC - 1))
                                t.then_inc(down, 1)
                            going_up(0)
                            for x in range(1, EXPERTS):
                                going_up(x)
                                going_down(x - 1)
                            going_down(EXPERTS - 1)
                        over_pairs(e, body)

                    @block.scalar
                    def _(e):
                        e.wait_ge(b_in, 32)

                        def body(i, k, m):
                            q = 2 * i + k
                            cols = m * P
                            e.wait_ge(turned, q + 1)
                            if later(i) or k:
                                e.wait_ge(up, q * UP)
                            nc.scalar.activation(xT[:, :, 0:cols], psT[:, :].rearrange("p (c n) -> p c n", c=2)[:, :, 0:cols], ACT.Copy).then_inc(xT_ready, 1)

                            def gelus(x):
                                if later(i) or k or x >= 2:
                                    e.wait_ge(down, q * DOWN + x - 1)
                                for f in range(FC):
                                    u = FC * x + f
                                    e.wait_ge(up, q * UP + u + 1)
                                    nc.scalar.activation(hid[x % 2][:, f, 0:cols], psU[u % 3][:, 0:cols], ACT.Gelu,
                                                         bias=b1[:, x, f:f + 1]).then_inc(hidden, 1)

                            def copy_out(x):
                                e.wait_ge(down, q * DOWN + x + 1)
                                if x == 0 and (later(i) or k):
                                    e.wait_ge(y_kept, 16 * q)
                                nc.scalar.activation(y[:, 0:m, x, :], psY[x % 2][:, 0:m, :], ACT.Copy).then_inc(copied, 1)
                            gelus(0)
                            gelus(1)
                            for x in range(2, EXPERTS):
                                copy_out(x - 2)
                                gelus(x)
                            copy_out(EXPERTS - 2)
                            copy_out(EXPERTS - 1)
                            e.wait_ge(copied, (q + 1) * DOWN)
                            e.sem_inc(held, 1)
                            e.dma_start(y_d[bass.ds(q * 2 * P, m * P), :, :].rearrange("(m p) x c -> p m x c", p=P) if m > 1 else
                                        y_d[bass.ds(q * 2 * P, P), :, :], y[:, 0:m, :, :] if m > 1 else y[:, 0, :, :]).then_inc(y_kept, 16)
                        over_pairs(e, body)
                        e.wait_ge(y_kept, 16 * PAIRS)

        def combine():
            with phase() as sc:
                y = [sb(f"o_y{k}", [P, EXPERTS, D], F32, sc) for k in range(2)]
                acc = [sb(f"o_acc{k}", [P, D], F32, sc) for k in range(2)]
                step, held = sem("o_step"), sem("o_held")
                tile_in = [sem(f"o_tile_in{k}") for k in range(2)]
                out_kept = [sem(f"o_out_kept{k}") for k in range(2)]
                with nc.Block() as block:
                    @block.sync
                    def _(e):
                        def body(i, k):
                            n = 2 * i + k
                            if later(i):
                                e.wait_ge(step, (n - 1) * EXPERTS)
                                e.sem_inc(held, 1)
                                e.wait_ge(out_kept[k], 16 * i)
                                e.sem_inc(held, 1)
                            e.dma_start(y[k][:, :, :], y_d[bass.ds(n * P, P), :, :]).then_inc(tile_in[k], 16)
                            e.dma_start(acc[k][:, :], x2_d[bass.ds(n * P, P), :]).then_inc(tile_in[k], 16)
                        over_tiles(e, body)

                    @block.vector
                    def _(e):
                        def body(i, k):
                            n = 2 * i + k
                            st = Steps(e, step, n, EXPERTS)
                            e.wait_ge(tile_in[k], 32 * (i + 1))
                            for x in range(EXPERTS):
                                st.wait()
                                st(nc.vector.scalar_tensor_tensor(out=acc[k][:, :], in0=y[k][:, x, :], scalar=gates[:, bass.ds(n, 1), x],
                                                                  in1=acc[k][:, :], op0=ALU.mult, op1=ALU.add))
                        over_tiles(e, body)

                    @block.scalar
                    def _(e):
                        def body(i, k):
                            n = 2 * i + k
                            rows = P if not isinstance(n, int) or n < NT - 1 else N - n * P
                            e.wait_ge(step, (n + 1) * EXPERTS)
                            e.sem_inc(held, 1)
                            e.dma_start(out[bass.ds(n * P, rows), :], acc[k][0:rows, :]).then_inc(out_kept[k], 16)
                        over_tiles(e, body)
                        for k in range(2):
                            e.wait_ge(out_kept[k], 16 * (NT // 2 + (NT % 2 if k == 0 else 0)))

        with phase() as gs:
            tot = sb("tot", [P, NT, REC], F32, gs)
            node8 = sb("node8", [P, NT, 2 * HEADS], F32, gs)
            srt = sb("srt", [P, T_GAT, 2], I32, gs)
            with phase() as g2:
                gat_records(g2, srt)
            with phase() as g3:
                rec = sb("rec", [P, T_GAT, REC], F32, g3)
                experts_and_gather(srt, rec)
                gat_softmax(srt, rec, g3)
            gat_cross()
            gat_gates()
        combine()


def kernel(**inputs):
    import numpy as _np
    import concourse.bacc as _bacc
    from concourse import mybir as _mybir
    from concourse.bass_utils import run_bass_kernel_spmd as _run

    nc = _bacc.Bacc("TRN2", target_bir_lowering=False, num_devices=1)
    arrays, args = {}, {}
    for name, value in inputs.items():
        v = _np.ascontiguousarray(value)
        arrays[f"in_{name}"] = v
        args[name] = nc.dram_tensor(f"in_{name}", v.shape, _mybir.dt.from_np(v.dtype), kind="ExternalInput").ap()
    out = nc.dram_tensor("out_0", (N, D), F32, kind="ExternalOutput").ap()
    build(nc, args, out)
    r = _run(nc, [arrays], core_ids=[0])
    return r.results[0]["out_0"]
```

```python
import numpy as np
import concourse.bass as bass
from concourse import mybir
from contextlib import ExitStack, contextmanager

F32 = mybir.dt.float32
BF16 = mybir.dt.bfloat16
I32 = mybir.dt.int32
ALU = mybir.AluOpType
ACT = mybir.ActivationFunctionType
AX = mybir.AxisListType

P = 128
N, D = 6250, 256
NT = -(-N // P)
NP = NT * P
NL = NP + P
RELS, BASES = 16, 8
E_GNN, E_GAT = 100000, 131072
U = 16
T_GNN = -(-E_GNN // (P * U)) * U
T_GAT = E_GAT // P
KEYS = 8192
KH = KEYS // P
PAD = KEYS - 1
HEADS, EXPERTS, FF = 4, 4, 512
REC = HEADS + HEADS * EXPERTS
EPS = 1e-5
SORT = (3, 6)
EDGE_SORT = (2, 6)


def over_tiles(eng, body):
    for k in range(2):
        body(0, k)
    with eng.Fori(1, NT // 2) as i:
        for k in range(2):
            body(i, k)
    if NT % 2:
        body(NT // 2, 0)


def later(i):
    return not isinstance(i, int) or i > 0


def has_next(i, k):
    return not isinstance(i, int) or 2 * i + k + 1 < NT


def next_tile(i, k):
    return (i, 1) if k == 0 else (i + 1, 0)


class Steps:

    def __init__(self, eng, sem, turn, per_turn, offset=0):
        self.eng, self.sem, self.turn, self.per, self.offset, self.k = eng, sem, turn, per_turn, offset, 0

    def wait(self):
        if self.k or self.offset:
            self.eng.wait_ge(self.sem, self.turn * self.per + self.offset + self.k)

    def __call__(self, instruction):
        instruction.then_inc(self.sem, 1)
        self.k += 1


def build(nc, a, out):
    ctx = ExitStack()
    with ctx:
        top = ctx

        def sb(name, shape, dt=F32, scope=None):
            return (scope or top).enter_context(nc.sbuf_tensor(name, shape, dt))

        open_phases = []

        def sem(name):
            handle = nc.alloc_semaphore(name)
            open_phases[-1].append(handle)
            return handle

        @contextmanager
        def phase():
            with ExitStack() as scope:
                open_phases.append([])
                yield scope
                mine = open_phases.pop()
                if mine:
                    nc.clear_and_free_semaphores(mine)
                    nc.all_engine_barrier()


        def dram(name, shape, dt=F32):
            return nc.dram_tensor(name, shape, dt)

        x_pad = dram("x_pad", (NL, D))
        table = [dram(f"table{l}", (NP, RELS * D)) for l in range(2)]
        rooted = [dram(f"rooted{l}", (NP, D)) for l in range(2)]
        run_d = dram("run_d", (P * T_GNN, D))
        bounds_gnn = dram("bounds_gnn", (2, KEYS))

        ident = sb("ident", [P, P])
        upper = sb("upper", [P, P])
        ones = sb("ones", [P, P])
        iota_row = sb("iota_row", [P, P])
        iota_i = sb("iota_i", [P, P], I32)
        split_gnn = sb("split_gnn", [P, 1])
        split_i = sb("split_i", [P, 1], I32)
        hidx = sb("hidx", [P, T_GNN], I32)
        ea = sb("ea", [P, T_GNN])
        keep = sb("keep", [P, T_GNN])
        lo_gnn = sb("lo_gnn", [P, T_GNN])
        hi_gnn = sb("hi_gnn", [P, T_GNN])
        first_gnn = sb("first_gnn", [P, KH])
        after_gnn = sb("after_gnn", [P, KH])
        last_gnn_i = sb("last_gnn_i", [P, KH], I32)
        has_gnn = sb("has_gnn", [P, KH])
        inv_gnn = sb("inv_gnn", [P, KH])
        carry = sb("carry", [P, D])
        mixed_d = [dram(f"mixed_d{l}", (RELS + 1, D, D)) for l in range(2)]
        minus_half = sb("minus_half", [P, 1])

        with phase() as sc:
            dst_i = sb("dst_i", [P, T_GNN], I32, sc)
            src_i = sb("src_i", [P, T_GNN], I32, sc)
            typ_i = sb("typ_i", [P, T_GNN], I32, sc)
            part_i = sb("part_i", [P, T_GNN], I32, sc)
            set_done, edges_in, iota_done, key_step = (sem(n) for n in ("set_done", "edges_in", "iota_done", "key_step"))
            full, rest = E_GNN // T_GNN, E_GNN % T_GNN
            even = full // 16 * 16
            with nc.Block() as block:
                @block.gpsimd
                def _(e):
                    e.memset(dst_i[:, :], PAD).then_inc(set_done, 1)
                    e.memset(src_i[:, :], 0).then_inc(set_done, 1)
                    e.memset(typ_i[:, :], 0).then_inc(set_done, 1)
                    e.memset(ea[:, :], 0.0).then_inc(set_done, 1)
                    e.memset(ident[:, :], 0.0).then_inc(iota_done, 1)
                    e.memset(ones[:, :], 1.0).then_inc(iota_done, 1)
                    e.memset(minus_half[:, :], -0.5).then_inc(iota_done, 1)
                    e.iota(iota_i[:, :], pattern=[[1, P]], base=0, channel_multiplier=0).then_inc(iota_done, 1)
                    e.iota(split_i[:, :], pattern=[[0, 1]], base=T_GNN, channel_multiplier=T_GNN).then_inc(iota_done, 1)
                    e.wait_ge(iota_done, 5)
                    e.affine_select(out=ident[:, :], in_=ident[:, :], compare_op=ALU.not_equal, fill=1.0, base=0,
                                    pattern=[[-1, P]], channel_multiplier=1).then_inc(iota_done, 1)
                    e.affine_select(out=upper[:, :], in_=ones[:, :], compare_op=ALU.is_ge, fill=0.0, base=0,
                                    pattern=[[1, P]], channel_multiplier=-1).then_inc(iota_done, 1)
                    e.wait_ge(iota_done, 7)

                @block.sync
                def _(e):
                    e.wait_ge(set_done, 4)
                    for buf, arr in ((dst_i, a["dst"]), (src_i, a["src"]), (typ_i, a["edge_type_16"]), (ea, a["edge_weight"])):
                        for p0, p1 in ((0, even), (even, full)):
                            e.dma_start(buf[p0:p1, :], arr[p0 * T_GNN:p1 * T_GNN].rearrange("(p t) -> p t", t=T_GNN)).then_inc(edges_in, 16)
                        e.dma_start(buf[full:full + 1, 0:rest], arr[full * T_GNN:E_GNN].rearrange("(p t) -> p t", p=1)).then_inc(edges_in, 16)
                    e.wait_ge(edges_in, 12 * 16)

                @block.vector
                def _(e):
                    st = Steps(e, key_step, 0, 99)
                    e.wait_ge(edges_in, 12 * 16)
                    e.wait_ge(iota_done, 5)
                    v = nc.vector
                    st(v.tensor_copy(iota_row[:, :], iota_i[:, :]))
                    st(v.tensor_copy(split_gnn[:, :], split_i[:, :]))
                    st(v.scalar_tensor_tensor(out=hidx[:, :], in0=src_i[:, :], scalar=float(RELS), in1=typ_i[:, :],
                                              op0=ALU.mult, op1=ALU.add))
                    st(v.memset(keep[:, 0:1], 0.0))
                    st(v.tensor_tensor(keep[:, 1:T_GNN], dst_i[:, 1:T_GNN], dst_i[:, 0:T_GNN - 1], ALU.is_equal))
                    st(v.tensor_single_scalar(part_i[:, :], dst_i[:, :], P - 1, ALU.bitwise_and))
                    st.wait()
                    st(v.tensor_copy(lo_gnn[:, :], part_i[:, :]))
                    st.wait()
                    st(v.tensor_single_scalar(part_i[:, :], dst_i[:, :], 7, ALU.logical_shift_right))
                    st.wait()
                    st(v.tensor_copy(hi_gnn[:, :], part_i[:, :]))

        class Positions:

            def __init__(self, tag, sc, counted, ps, ps2, first, after, bounds, finish):
                self.counted, self.ps, self.ps2, self.first, self.after, self.bounds, self.finish = counted, ps, ps2, first, after, bounds, finish
                self.cnt = sb(f"{tag}_cnt", [P, KH], F32, sc)
                self.before = sb(f"{tag}_before", [P, KH], F32, sc)
                self.tail, self.ranked, self.stored = (sem(f"{tag}_{n}") for n in ("tail", "ranked", "stored"))

            def vector(self, e):
                v, cnt, before = nc.vector, self.cnt, self.before
                e.wait_ge(self.counted, 1)
                st = Steps(e, self.tail, 0, 99)
                st(v.tensor_copy(cnt[:, :], self.ps))
                st.wait()
                st(v.tensor_tensor_scan(before[:, :], ones[:, 0:KH], cnt[:, :], 0.0, ALU.mult, ALU.add))
                st.wait()
                st(v.tensor_tensor(before[:, :], before[:, :], cnt[:, :], ALU.subtract))
                e.wait_ge(self.ranked, 1)
                st(v.tensor_copy(self.after[:, :], self.ps2))
                st.wait()
                st(v.tensor_tensor(self.first[:, :], self.after[:, :], cnt[:, :], ALU.subtract))
                self.finish(v, st, cnt)

            def tensor(self, e):
                e.wait_ge(self.tail, 3)
                nc.tensor.matmul(self.ps2, upper[:, :], self.cnt[:, :], start=True, stop=False)
                nc.tensor.matmul(self.ps2, ones[:, :], self.before[:, :], start=False, stop=True).then_inc(self.ranked, 1)

            def sync(self, e):
                e.wait_ge(self.tail, 5)
                with nc.allow_non_contiguous_dma(reason="8192 words, once"):
                    e.dma_start(self.bounds[0, :].rearrange("(h l) -> l h", l=P), self.first[:, :]).then_inc(self.stored, 16)
                    e.dma_start(self.bounds[1, :].rearrange("(h l) -> l h", l=P), self.after[:, :]).then_inc(self.stored, 16)
                e.wait_ge(self.stored, 32)

        def count(tag, lo, hi, T, first, after, bounds, finish, beside):
            G = 8
            with phase() as sc:
                eq_lo = [sb(f"{tag}_eq_lo{j}", [P, G, P], BF16, sc) for j in range(2)]
                eq_hi = [sb(f"{tag}_eq_hi{j}", [P, G, KH], BF16, sc) for j in range(2)]
                diff = [sb(f"{tag}_diff{j}", [P, G, KH], BF16, sc) for j in range(2)]
                square = [sb(f"{tag}_square{j}", [P, G, KH], BF16, sc) for j in range(2)]
                zb = sb(f"{tag}_zb", [P, P], BF16, sc)
                ps = sc.enter_context(nc.psum_tensor(f"{tag}_ps", [P, 512], F32))
                ps2 = sc.enter_context(nc.psum_tensor(f"{tag}_ps2", [P, 512], F32))
                eq_ready, diff_ready, squared, hi_ready, eq_used, zero_set, counted = (
                    sem(f"{tag}_{n}") for n in ("eq_ready", "diff_ready", "squared", "hi_ready", "eq_used", "zero_set", "counted"))
                positions = Positions(tag, sc, counted, ps[:, 0:KH], ps2[:, 0:KH], first, after, bounds, finish)
                other = beside(sc)
                turns = T // (2 * G)
                with nc.Block() as block:
                    @block.vector
                    def _(e):
                        v = nc.vector
                        v.memset(zb[:, :], 0.0).then_inc(zero_set, 1)
                        with e.Fori(0, turns) as i:
                            for j in range(2):
                                e.wait_ge(eq_used, 2 * i + j + 1)
                                at = bass.ds((2 * i + j) * G, G)
                                v.tensor_tensor(eq_lo[j][:, :, :], lo[:, at].unsqueeze(2).to_broadcast([P, G, P]),
                                                iota_row[:, :].unsqueeze(1).to_broadcast([P, G, P]), ALU.is_equal).then_inc(eq_ready, 1)
                        other.vector(e)
                        positions.vector(e)

                    @block.gpsimd
                    def _(e):
                        other.gpsimd_loads(e)
                        with e.Fori(0, turns) as i:
                            for j in range(2):
                                e.wait_ge(squared, 2 * i + j + 1)
                                e.tensor_tensor(diff[j][:, :, :], hi[:, bass.ds((2 * i + j) * G, G)].unsqueeze(2).to_broadcast([P, G, KH]),
                                                iota_row[:, 0:KH].unsqueeze(1).to_broadcast([P, G, KH]), ALU.subtract).then_inc(diff_ready, 1)
                        other.gpsimd_stores(e)

                    @block.scalar
                    def _(e):
                        nc.scalar.activation(square[1][:, 0, 0:1], ones[:, 0:1], ACT.Square).then_inc(squared, 1)
                        e.wait_ge(squared, 1)
                        e.sem_inc(squared, 1)
                        with e.Fori(0, turns) as i:
                            for j in range(2):
                                e.wait_ge(diff_ready, 2 * i + j + 1)
                                nc.scalar.activation(square[j][:, :, :], diff[j][:, :, :], ACT.Square).then_inc(squared, 1)
                                e.wait_ge(squared, 2 * i + j + 3)
                                e.wait_ge(eq_used, 2 * i + j + 1)
                                nc.scalar.activation(eq_hi[j][:, :, :], square[j][:, :, :], ACT.Relu, bias=ones[:, 0:1], scale=-1.0).then_inc(hi_ready, 1)
                        other.scalar(e)

                    @block.tensor
                    def _(e):
                        e.wait_ge(zero_set, 1)
                        nc.tensor.matmul(ps[:, 0:KH], zb[:, :], zb[:, 0:KH], start=True, stop=False)
                        e.sem_inc(eq_used, 2)
                        with e.Fori(0, turns) as i:
                            for j in range(2):
                                e.wait_ge(eq_ready, 2 * i + j + 1)
                                e.wait_ge(hi_ready, 2 * i + j + 1)
                                for g in range(G):
                                    m = nc.tensor.matmul(ps[:, 0:KH], eq_lo[j][:, g, :], eq_hi[j][:, g, :], start=False, stop=False)
                                m.then_inc(eq_used, 1)
                        nc.tensor.matmul(ps[:, 0:KH], zb[:, :], zb[:, 0:KH], start=False, stop=True).then_inc(counted, 1)
                        positions.tensor(e)
                        other.tensor(e)

                    @block.sync
                    def _(e):
                        other.sync_loads(e)
                        positions.sync(e)
                        other.sync_stores(e)

        def finish_gnn(v, st, cnt):
            st(v.tensor_scalar(has_gnn[:, :], cnt[:, :], 1.0, None, ALU.min))
            st(v.tensor_scalar(inv_gnn[:, :], cnt[:, :], 1.0, None, ALU.add))
            st.wait()
            st(v.reciprocal(inv_gnn[:, :], inv_gnn[:, :]))
            st(v.tensor_scalar(last_gnn_i[:, :], after_gnn[:, :], -1.0, 0.0, ALU.add, ALU.max))
            st.wait()

        class Mix:
            S = P // BASES
            BLOCKS = D // S
            HALF_R = RELS // 2
            ZP = next(q for q in range(P, 0, -1) if (NL - N) % q == 0)

            def __init__(self, sc):
                S, BLOCKS = self.S, self.BLOCKS
                assert self.HALF_R * S == P
                self.basis = [sb(f"w_basis{l}", [P, BLOCKS, D], F32, sc) for l in range(2)]
                self.root = [sb(f"w_root{l}", [P, 2, D], F32, sc) for l in range(2)]
                self.att = [sb(f"w_att{l}", [P, RELS], F32, sc) for l in range(2)]
                self.spread_att = [sb(f"w_spread{l}", [P, RELS, S], F32, sc) for l in range(2)]
                self.mixed = [sb(f"w_mixed{h}", [P, BLOCKS, D], F32, sc) for h in range(2)]
                self.same_s = sb("w_same_s", [P, S], F32, sc)
                self.zeros = sb("w_zeros", [self.ZP, (NL - N) // self.ZP * D], F32, sc)
                self.ps = [sc.enter_context(nc.psum_tensor(f"w_ps{q}", [P, 512], F32)) for q in range(4)]
                (self.att_in, self.root_in, self.root_kept, self.step, self.product, self.copied, self.zeroed, self.zeros_kept,
                 self.x_copied) = (sem(f"w_{n}") for n in ("att_in", "root_in", "root_kept", "step", "product", "copied", "zeroed",
                                                           "zeros_kept", "x_copied"))
                self.basis_in = [sem(f"w_basis_in{l}") for l in range(2)]
                self.stored = [sem(f"w_stored{h}") for h in range(2)]

            def piece(self, l, h, b):
                return (l * 2 + h) * (self.BLOCKS // 2) + b

            def sync_loads(self, e):
                for l in range(2):
                    w = a[f"L0_gnn_basis{l + 1}"]
                    for b in range(BASES):
                        e.dma_start(self.basis[l][b * self.S:(b + 1) * self.S, :, :], w[b].rearrange("(k s) o -> s k o", s=self.S)).then_inc(self.basis_in[l], 16)
                e.dma_start(x_pad[0:N, :], a["x"][:, :]).then_inc(self.x_copied, 16)
                e.wait_ge(self.zeroed, 1)
                e.dma_start(x_pad[N:NL, :].rearrange("(q a) o -> q (a o)", q=self.ZP), self.zeros[:, :]).then_inc(self.zeros_kept, 16)

            def sync_stores(self, e):
                for l in range(2):
                    for h in range(2):
                        e.wait_ge(self.copied, self.piece(l, h, self.BLOCKS // 2))
                        for r in range(self.HALF_R):
                            e.dma_start(mixed_d[l][h * self.HALF_R + r].rearrange("(k s) o -> s k o", s=self.S),
                                        self.mixed[h][r * self.S:(r + 1) * self.S, :, :]).then_inc(self.stored[h], 16)
                for h in range(2):
                    e.wait_ge(self.stored[h], 16 * 2 * self.HALF_R)
                e.wait_ge(self.x_copied, 16)
                e.wait_ge(self.zeros_kept, 16)

            def gpsimd_loads(self, e):
                with nc.allow_non_contiguous_dma(reason="128 words, once"):
                    for l in range(2):
                        w = a[f"L0_gnn_att{l + 1}"].rearrange("r b -> b r")
                        for b in range(BASES):
                            e.dma_start(self.att[l][b * self.S:(b + 1) * self.S, :], w[b:b + 1, :].to_broadcast([self.S, RELS])).then_inc(self.att_in, 16)
                for l in range(2):
                    e.dma_start(self.root[l][:, :, :], a[f"L0_gnn_root{l + 1}"].rearrange("(c p) o -> p c o", p=P)).then_inc(self.root_in, 16)

            def gpsimd_stores(self, e):
                e.wait_ge(self.step, 1 + 2 + 4)
                for l in range(2):
                    e.dma_start(mixed_d[l][RELS].rearrange("(c p) o -> p c o", p=P), self.root[l][:, :, :]).then_inc(self.root_kept, 16)
                e.wait_ge(self.root_kept, 32)

            def vector(self, e):
                v, S = nc.vector, self.S
                v.memset(self.zeros[:, :], 0.0).then_inc(self.zeroed, 1)
                v.reduce_sum(self.same_s[:, :], ident[:, :].rearrange("p (b s) -> p s b", s=S), AX.X).then_inc(self.step, 1)
                e.wait_ge(self.step, 1)
                e.wait_ge(self.att_in, 16 * 2 * BASES)
                for l in range(2):
                    v.tensor_tensor(self.spread_att[l][:, :, :], self.att[l][:, :].unsqueeze(2).to_broadcast([P, RELS, S]),
                                    self.same_s[:, :].unsqueeze(1).to_broadcast([P, RELS, S]), ALU.mult).then_inc(self.step, 1)
                e.wait_ge(self.root_in, 32)
                for l in range(2):
                    for c in range(2):
                        part = self.root[l][:, c, c * P:(c + 1) * P]
                        v.tensor_tensor(part, part, ident[:, :], ALU.add).then_inc(self.step, 1)

            def tensor(self, e):
                e.wait_ge(self.step, 3)
                for l in range(2):
                    e.wait_ge(self.basis_in[l], 16 * BASES)
                    for h in range(2):
                        for b in range(self.BLOCKS // 2):
                            m = self.piece(l, h, b)
                            if m >= 4:
                                e.wait_ge(self.copied, m - 3)
                            nc.tensor.matmul(self.ps[m % 4][:, :], self.spread_att[l][:, h * self.HALF_R:(h + 1) * self.HALF_R, :].rearrange("p r s -> p (r s)"),
                                             self.basis[l][:, 2 * b:2 * b + 2, :].rearrange("p k o -> p (k o)"),
                                             start=True, stop=True).then_inc(self.product, 1)

            def scalar(self, e):
                for l in range(2):
                    for h in range(2):
                        if l:
                            e.wait_ge(self.stored[h], 16 * self.HALF_R)
                        for b in range(self.BLOCKS // 2):
                            m = self.piece(l, h, b)
                            e.wait_ge(self.product, m + 1)
                            nc.scalar.activation(self.mixed[h][:, 2 * b:2 * b + 2, :].rearrange("p k o -> p (k o)"), self.ps[m % 4][:, :],
                                                 ACT.Copy).then_inc(self.copied, 1)

        class Products:
            CH = 9
            HALVES = 2 * CH
            PLACES = 2 * (HALVES + 1)

            def __init__(self, tag, sc, l, ps_turn, banks):
                self.l, self.psT = l, ps_turn
                self.weights = [sb(f"{tag}_weights{c}", [P, RELS + 1, D], F32, sc) for c in range(2)]
                self.h_new = [sb(f"{tag}_h_new{k}", [P, D], F32, sc) for k in range(2)]
                self.hT = [sb(f"{tag}_hT{k}", [P, 2, P], F32, sc) for k in range(2)]
                self.prod = [sb(f"{tag}_prod{k}", [P, RELS + 1, D], F32, sc) for k in range(2)]
                self.psP = [sc.enter_context(nc.psum_tensor(f"{tag}_psP{q}", [P, 512], F32)) for q in range(banks)]
                self.banks = banks
                self.h_turned, self.hT_ready, self.product, self.evacuated, self.held, self.w_in = (
                    sem(f"{tag}_{n}") for n in ("h_turned", "hT_ready", "product", "evacuated", "prod_held", "w_in"))
                self.kept = [sem(f"{tag}_kept{k}") for k in range(2)]

            def load_weights(self, e):
                for c in range(2):
                    e.dma_start(self.weights[c][:, :, :], mixed_d[self.l][:, c * P:(c + 1) * P, :].rearrange("r p o -> p r o")).then_inc(self.w_in, 16)

            def h_free(self, e, i, k):
                if later(i):
                    e.wait_ge(self.h_turned, 2 * i + k - 1)

            def turn(self, e, i, k):
                n = 2 * i + k
                if later(i) or k:
                    e.wait_ge(self.hT_ready, n)
                for c in range(2):
                    m = nc.tensor.transpose(self.psT[:, c * P:(c + 1) * P], self.h_new[k][:, c * P:(c + 1) * P], ident[:, :])
                m.then_inc(self.h_turned, 1)

            def multiply(self, e, i, k, between, turn_next):
                n, CH = 2 * i + k, self.CH
                n_odd = k
                between(k * (self.HALVES + 1))
                e.wait_ge(self.hT_ready, n + 1)
                for q in range(CH):
                    if later(i) or k or q >= self.banks:
                        e.wait_ge(self.evacuated, n * CH + q - self.banks + 1)
                    w = 512 if q < CH - 1 else D
                    for c in range(2):
                        m = nc.tensor.matmul(self.psP[(n_odd * CH + q) % self.banks][:, 0:w], self.hT[k][:, c, :],
                                             self.weights[c][:, 2 * q:2 * q + w // D, :].rearrange("p r o -> p (r o)"),
                                             start=(c == 0), stop=(c == 1))
                        if c:
                            m.then_inc(self.product, 1)
                        between(k * (self.HALVES + 1) + 1 + 2 * q + c)
                    if q == CH - 2:
                        turn_next()

            def take(self, e, i, k):
                n, CH = 2 * i + k, self.CH
                e.wait_ge(self.h_turned, n + 1)
                if later(i):
                    e.wait_ge(self.product, (n - 1) * CH)
                nc.scalar.activation(self.hT[k][:, :, :].rearrange("p c n -> p (c n)"), self.psT[:, 0:2 * P], ACT.Copy).then_inc(self.hT_ready, 1)

            def evacuate(self, e, i, k, between, take_next):
                n, CH = 2 * i + k, self.CH
                n_odd = k
                between(k * (self.HALVES + 1))
                if later(i):
                    e.wait_ge(self.kept[k], 32 * i)
                for q in range(CH):
                    between(k * (self.HALVES + 1) + 1 + 2 * q)
                    e.wait_ge(self.product, n * CH + q + 1)
                    w = 512 if q < CH - 1 else D
                    nc.scalar.activation(self.prod[k][:, 2 * q:2 * q + w // D, :].rearrange("p r o -> p (r o)"),
                                         self.psP[(n_odd * CH + q) % self.banks][:, 0:w], ACT.Copy).then_inc(self.evacuated, 1)
                    between(k * (self.HALVES + 1) + 2 + 2 * q)
                    if q == CH - 2:
                        take_next()
                e.wait_ge(self.evacuated, (n + 1) * CH)
                e.sem_inc(self.held, 1)
                e.dma_start(table[self.l][bass.ds(n * P, P), :], self.prod[k][:, 0:RELS, :].rearrange("p r o -> p (r o)")).then_inc(self.kept[k], 16)
                e.dma_start(rooted[self.l][bass.ds(n * P, P), :], self.prod[k][:, RELS, :]).then_inc(self.kept[k], 16)

            def all_kept(self, e):
                for k in range(2):
                    e.wait_ge(self.kept[k], 32 * ((NT + 1 - k) // 2))

        HEAD_STEPS = 8

        def inverse_root(e, rs, ve, rooted):
            e.tensor_tensor(rs[:, :], ve[:, :], minus_half[:, :], ALU.pow).then_inc(rooted, 1)

        class Tail:

            MASKS = 2

            def __init__(self, tag, sc, layer, per, gap, psC):
                self.layer, self.per, self.gap = layer, per, gap
                two = lambda name, shape, dt=F32: [sb(f"{tag}_{name}{k}", shape, dt, sc) for k in range(2)]
                self.rows, self.own, self.root, self.end = two("rows", [P, 2, P]), two("own", [P, D]), two("root", [P, D]), two("end", [P, D])
                self.idx, self.cross, self.below, self.acc = two("idx", [P, 1], I32), two("cross", [P, P]), two("below", [P, P]), two("acc", [P, D])
                self.stats, self.mv, self.ve, self.rs = two("stats", [P, 6]), two("mv", [P, 2]), two("ve", [P, 1]), two("rs", [P, 1])
                self.vectors = {n: sb(f"{tag}_{n}", [P, D], F32, sc) for n in ("bias", "gain", "shift")}
                self.psC = psC
                self.vec_in = sem(f"{tag}_vec_in")
                self.held = sem(f"{tag}_tail_held")
                self.rows_in, self.loaded, self.end_in, self.step, self.crossed, self.biased, self.idx_set, self.rooted = (
                    [sem(f"{tag}_{n}{k}") for k in range(2)] for n in ("rows_in", "loaded", "end_in", "step", "crossed", "biased", "idx_set", "rooted"))

            def at(self, i, steps):
                return i * self.per + steps + (self.gap if steps > self.MASKS else 0)

            def load_vectors(self, e):
                l = self.layer
                for n, arr in (("bias", f"L0_gnn_bias{l}"), ("gain", f"L0_gnn_ln{l}_g"), ("shift", f"L0_gnn_ln{l}_b")):
                    e.dma_start(self.vectors[n][:, :], a[arr].unsqueeze(0).to_broadcast([P, D])).then_inc(self.vec_in, 16)

            def load_rows(self, e, i, k):
                if later(i):
                    e.wait_ge(self.step[k], self.at(i - 1, self.MASKS))
                    e.sem_inc(self.held, 1)
                e.dma_start(self.rows[k][:, :, :], bounds_gnn[:, bass.ds((2 * i + k) * P, P)].unsqueeze(0).to_broadcast([P, 2, P])).then_inc(self.rows_in[k], 16)

            def load(self, e, i, k):
                n, l = 2 * i + k, self.layer
                if later(i):
                    e.wait_ge(self.step[k], self.at(i - 1, 5))
                    e.sem_inc(self.held, 1)
                e.dma_start(self.own[k][:, :], table[l - 1][bass.ds(n * P, P), (RELS - 1) * D:RELS * D]).then_inc(self.loaded[k], 16)
                e.dma_start(self.root[k][:, :], rooted[l - 1][bass.ds(n * P, P), :]).then_inc(self.loaded[k], 16)

            def fetch(self, e, i, k):
                n = 2 * i + k
                if later(i):
                    e.wait_ge(self.step[k], self.at(i - 1, 5))
                else:
                    e.wait_ge(self.vec_in, 16 * 3)
                e.sem_inc(self.held, 1)
                e.tensor_copy(self.idx[k][:, :], last_gnn_i[:, bass.ds(n, 1)]).then_inc(self.idx_set[k], 1)
                e.wait_ge(self.idx_set[k], i + 1)
                e.sem_inc(self.held, 1)
                e.indirect_dma_start(out=self.end[k][:, :], out_offset=None, in_=run_d[:, :],
                                     in_offset=bass.IndirectOffsetOnAxis(ap=self.idx[k][:, 0:1], axis=0)).then_inc(self.end_in[k], 16)

            def add_bias(self, e, i, k):
                e.wait_ge(self.loaded[k], 32 * (i + 1))
                e.tensor_tensor(self.root[k][:, :], self.root[k][:, :], self.vectors["bias"][:, :], ALU.add).then_inc(self.biased[k], 1)

            def inverse_root(self, e, i, k):
                e.wait_ge(self.step[k], self.at(i, HEAD_STEPS))
                inverse_root(e, self.rs[k], self.ve[k], self.rooted[k])

            def cross_product(self, e, i, k):
                e.wait_ge(self.step[k], self.at(i, self.MASKS))
                nc.tensor.matmul(self.psC[k], self.cross[k][:, :], carry[:, :], start=True, stop=True).then_inc(self.crossed[k], 1)

            def vectors_ready(self, e):
                e.wait_ge(self.vec_in, 16 * 3)

            def steps(self, e, i, slots, done):
                counters = {k: Steps(e, self.step[k], i, self.per, done) for k in slots}

                def each(op):
                    for k in slots:
                        counters[k].wait()
                        counters[k](op(k))
                return each

            def masks(self, e, each, i, slots):
                v = nc.vector
                for k in slots:
                    e.wait_ge(self.rows_in[k], 16 * (i + 1))
                    if later(i):
                        e.wait_ge(self.crossed[k], i)
                each(lambda k: v.tensor_scalar(self.below[k][:, :], self.rows[k][:, 0, :], split_gnn[:, :], None, ALU.is_lt))
                each(lambda k: v.scalar_tensor_tensor(out=self.cross[k][:, :], in0=self.rows[k][:, 1, :], scalar=split_gnn[:, :],
                                                      in1=self.below[k][:, :], op0=ALU.is_gt, op1=ALU.mult))

            def sums(self, e, each, i, slots):
                v, n = nc.vector, {k: 2 * i + k for k in slots}
                for k in slots:
                    e.wait_ge(self.loaded[k], 32 * (i + 1))
                    e.wait_ge(self.end_in[k], 16 * (i + 1))
                each(lambda k: v.scalar_tensor_tensor(out=self.acc[k][:, :], in0=self.end[k][:, :], scalar=has_gnn[:, bass.ds(n[k], 1)],
                                                      in1=self.own[k][:, :], op0=ALU.mult, op1=ALU.add))
                for k in slots:
                    e.wait_ge(self.crossed[k], i + 1)
                each(lambda k: v.tensor_tensor(self.acc[k][:, :], self.acc[k][:, :], self.psC[k], ALU.add))
                for k in slots:
                    e.wait_ge(self.biased[k], i + 1)
                each(lambda k: v.scalar_tensor_tensor(out=self.acc[k][:, :], in0=self.acc[k][:, :], scalar=inv_gnn[:, bass.ds(n[k], 1)],
                                                      in1=self.root[k][:, :], op0=ALU.mult, op1=ALU.add))
                layer_stats(e, each, self.acc, self.stats, self.mv, self.ve, self.held)

            def gain_and_shift(self, e, each, i, slots):
                v = nc.vector
                each(lambda k: v.scalar_tensor_tensor(out=self.acc[k][:, :], in0=self.acc[k][:, :], scalar=self.mv[k][:, 0:1],
                                                      in1=self.vectors["gain"][:, :], op0=ALU.subtract, op1=ALU.mult))
                for k in slots:
                    e.wait_ge(self.rooted[k], i + 1)
                each(lambda k: v.scalar_tensor_tensor(out=self.acc[k][:, :], in0=self.acc[k][:, :], scalar=self.rs[k][:, :],
                                                      in1=self.vectors["shift"][:, :], op0=ALU.mult, op1=ALU.add))

        def layer_stats(e, each, src, stats, mv, ve, held):
            v = nc.vector
            each(lambda k: v.bn_stats(stats[k][:, :], src[k][:, :]))

            def aggregate(k):
                e.sem_inc(held, 1)
                return v.bn_aggr(mv[k][:, :], stats[k][:, :])
            each(aggregate)
            each(lambda k: v.tensor_scalar(ve[k][:, :], mv[k][:, 1:2], EPS, None, ALU.add))

        class Sender:
            SLOTS, G = 4, EDGE_SORT[1]

            def __init__(self, tag, sc):
                self.place, self.pair = ([sb(f"{tag}_sent_{n}{j}", [P, self.G] + w, I32, sc) for j in range(self.SLOTS)]
                                         for n, w in (("place", []), ("pair", [2])))
                self.held, self.copied = sem(f"{tag}_send_held"), sem(f"{tag}_send_copied")
                self.sent = [[sem(f"{tag}_sent{j}_{g}") for g in range(self.G)] for j in range(self.SLOTS)]

            def send(self, e, i, j):
                gl, G = i * self.SLOTS + j, self.G
                if later(i):
                    for g in range(G):
                        e.wait_ge(self.sent[j][g], 16 * i)
                e.sem_inc(self.held, 1)
                e.tensor_copy(self.place[j][:, :], place_kept[:, bass.ds(gl * G, G)]).then_inc(self.copied, 1)
                e.tensor_copy(self.pair[j][:, :, :], edge_pair[:, bass.ds(gl * G + EDGE_BASE, G), :]).then_inc(self.copied, 1)
                e.wait_ge(self.copied, 2 * gl + 2)
                e.sem_inc(self.held, 1)
                for g in range(G):
                    e.indirect_dma_start(out=sorted_d[:, :], out_offset=bass.IndirectOffsetOnAxis(ap=self.place[j][:, g:g + 1], axis=0),
                                         in_=self.pair[j][:, g, :], in_offset=None).then_inc(self.sent[j][g], 16)

            def send_rest(self, e, turns):
                rest = PLACED // self.G - turns * self.SLOTS
                assert 0 <= rest <= self.SLOTS and PLACED % self.G == 0
                for j in range(rest):
                    self.send(e, turns, j)
                for j in range(self.SLOTS):
                    for g in range(self.G):
                        e.wait_ge(self.sent[j][g], 16 * (turns + int(j < rest)))

        def node_loop(weights):
            CH = 9
            with phase() as sc:
                h_new = [sb(f"n_h_new{k}", [P, D], F32, sc) for k in range(2)]
                hT = [sb(f"n_hT{k}", [P, 2, P], F32, sc) for k in range(2)]
                prod = [sb(f"n_prod{k}", [P, RELS + 1, D], F32, sc) for k in range(2)]
                psT = [sc.enter_context(nc.psum_tensor(f"n_psT{k}", [P, 512], F32)) for k in range(2)]
                psP = [sc.enter_context(nc.psum_tensor(f"n_psP{j}", [P, 512], F32)) for j in range(3)]
                S = {n: sem(f"n_{n}") for n in ("turned", "hT_ready", "product", "evacuated")}
                t_kept = [sem(f"n_t_kept{k}") for k in range(2)]
                psC = [sc.enter_context(nc.psum_tensor(f"n_psC{k}", [P, 512], F32)) for k in range(2)]
                tail = Tail("n", sc, 1, HEAD_STEPS + 3, 0, [p[:, 0:D] for p in psC])
                sender = Sender("n", sc)
                with nc.Block() as block:
                    @block.sync
                    def _(e):
                        tail.load_vectors(e)
                        over_tiles(e, lambda i, k: (tail.load_rows(e, i, k), tail.load(e, i, k)))

                    @block.vector
                    def _(e):
                        v = nc.vector
                        tail.vectors_ready(e)

                        def body(i, k):
                            each = tail.steps(e, i, (k,), 0)
                            tail.masks(e, each, i, (k,))
                            tail.sums(e, each, i, (k,))
                            tail.gain_and_shift(e, each, i, (k,))
                            if later(i):
                                e.wait_ge(S["turned"], 2 * i + k - 1)
                            each(lambda k: v.tensor_relu(h_new[k][:, :], tail.acc[k][:, :]))
                        over_tiles(e, body)

                    @block.tensor
                    def _(e):
                        def turn(i, k):
                            e.wait_ge(tail.step[k], (i + 1) * tail.per)
                            if later(i):
                                e.wait_ge(S["hT_ready"], 2 * i + k - 1)
                            for c in range(2):
                                m = nc.tensor.transpose(psT[k][:, c * P:(c + 1) * P], h_new[k][:, c * P:(c + 1) * P], ident[:, :])
                            m.then_inc(S["turned"], 1)
                        tail.cross_product(e, 0, 0)
                        turn(0, 0)

                        def body(i, k):
                            n = 2 * i + k
                            e.wait_ge(S["hT_ready"], n + 1)
                            for q in range(CH):
                                if later(i) or k or q >= 3:
                                    e.wait_ge(S["evacuated"], n * CH + q - 2)
                                w = 512 if q < CH - 1 else D
                                for c in range(2):
                                    m = nc.tensor.matmul(psP[q % 3][:, 0:w], hT[k][:, c, :],
                                                         weights[c][:, 2 * q:2 * q + w // D, :].rearrange("p r o -> p (r o)"),
                                                         start=(c == 0), stop=(c == 1))
                                m.then_inc(S["product"], 1)
                                if has_next(i, k) and q == 0:
                                    tail.cross_product(e, *next_tile(i, k))
                                if has_next(i, k) and q == 7:
                                    turn(*next_tile(i, k))
                        over_tiles(e, body)

                    @block.scalar
                    def _(e):
                        def take(i, k):
                            n = 2 * i + k
                            e.wait_ge(S["turned"], n + 1)
                            if later(i):
                                e.wait_ge(S["product"], (n - 1) * CH)
                            nc.scalar.activation(hT[k][:, :, :].rearrange("p c n -> p (c n)"), psT[k][:, 0:2 * P], ACT.Copy).then_inc(S["hT_ready"], 1)
                        take(0, 0)

                        def body(i, k):
                            n = 2 * i + k
                            if later(i):
                                e.wait_ge(t_kept[k], 32 * i)
                            for q in range(CH):
                                if q == 8 and has_next(i, k):
                                    take(*next_tile(i, k))
                                e.wait_ge(S["product"], n * CH + q + 1)
                                w = 512 if q < CH - 1 else D
                                nc.scalar.activation(prod[k][:, 2 * q:2 * q + w // D, :].rearrange("p r o -> p (r o)"),
                                                     psP[q % 3][:, 0:w], ACT.Copy).then_inc(S["evacuated"], 1)
                            e.wait_ge(S["evacuated"], (n + 1) * CH)
                            e.dma_start(table[1][bass.ds(n * P, P), :], prod[k][:, 0:RELS, :].rearrange("p r o -> p (r o)")).then_inc(t_kept[k], 16)
                            e.dma_start(rooted[1][bass.ds(n * P, P), :], prod[k][:, RELS, :]).then_inc(t_kept[k], 16)
                        over_tiles(e, body)
                        for k in range(2):
                            e.wait_ge(t_kept[k], 32 * (NT // 2 + (NT % 2 if k == 0 else 0)))

                    @block.gpsimd
                    def _(e):
                        tail.fetch(e, 0, 0)
                        tail.add_bias(e, 0, 0)
                        tail.inverse_root(e, 0, 0)
                        tail.fetch(e, 0, 1)
                        tail.add_bias(e, 0, 1)

                        def body(i):
                            for k in range(2):
                                sender.send(e, i, 2 * k)
                                tail.inverse_root(e, *next_tile(i, k))
                                sender.send(e, i, 2 * k + 1)
                                if not isinstance(i, int) or 2 * (i + 1) + k < NT:
                                    tail.fetch(e, i + 1, k)
                                    tail.add_bias(e, i + 1, k)
                        body(0)
                        with e.Fori(1, NT // 2 - 1) as i:
                            body(i)
                        body(NT // 2 - 1)
                        sender.send_rest(e, NT // 2)

        stats = [sb(f"stats{k}", [P, 6]) for k in range(2)]
        mvs = [sb(f"mv{k}", [P, 2]) for k in range(2)]
        rss = [sb(f"rstd{k}", [P, 1]) for k in range(2)]
        ves = [sb(f"var_eps{k}", [P, 1]) for k in range(2)]

        def edge_loop(l, sort=False, next_weights=None):
            with phase() as sc:
                tag = f"e{l}"
                if sort:
                    assert EDGE_SORT[0] == 2 and EDGE_SORT[1] == 6
                    so = Sorter("es", sc, *EDGE_SORT, EDGE_BASE, gat_running, place_kept, banks=4)
                    TILE_AFTER = {1: 0, 2: 1, 3: 2, 5: 3, 6: 4, 7: 5}

                def over_edge_turns(e, body):
                    body(0, True)
                    with e.Fori(1, turns - int(sort)) as i:
                        body(i, False)
                    if sort:
                        body(turns - 1, False)

                def next_group(i, h):
                    i2, h2 = (i, 1) if h == 0 else (i + 1, 0)
                    return None if isinstance(i2, int) and i2 == turns else (i2, h2)
                H = U // 2
                got = sb(f"{tag}_got", [P, U, D], F32, sc)
                msg = sb(f"{tag}_msg", [P, U, D], F32, sc)
                run = sb(f"{tag}_run", [P, U, D], F32, sc)
                idx = [sb(f"{tag}_idx{h}", [P, H], I32, sc) for h in range(2)]
                ea_s = sb(f"{tag}_ea", [P, U], F32, sc)
                keep_s = sb(f"{tag}_keep", [P, U], F32, sc)
                idx_set, held, weighted, summed, ea_set, keep_set = (
                    sem(f"{tag}_{n}") for n in ("idx_set", "held", "weighted", "summed", "ea_set", "keep_set"))
                arrived = [sem(f"{tag}_arrived{j}") for j in range(U)]
                weights_in = sem(f"{tag}_weights_in")
                run_kept = [sem(f"{tag}_run_kept{h}") for h in range(2)]
                turns = T_GNN // U
                rows = table[l][:, :].rearrange("n (r o) -> (n r) o", o=D)
                run_view = run_d[:, :].rearrange("(p t) o -> p t o", t=T_GNN)
                with nc.Block() as block:
                    @block.gpsimd
                    def _(e):
                        def body(i, first):
                            for h in range(2):
                                if not first:
                                    e.wait_ge(weighted, (i - 1) * U + (h + 1) * H)
                                    for j in range(h * H, (h + 1) * H):
                                        e.wait_ge(arrived[j], 16 * i)
                                e.sem_inc(held, 1)
                                e.tensor_copy(idx[h][:, :], hidx[:, bass.ds(i * U + h * H, H)]).then_inc(idx_set, 1)
                                e.wait_ge(idx_set, 2 * i + h + 1)
                                e.sem_inc(held, 1)
                                for j in range(h * H, (h + 1) * H):
                                    e.indirect_dma_start(out=got[:, j, :], out_offset=None, in_=rows,
                                                         in_offset=bass.IndirectOffsetOnAxis(ap=idx[h][:, j - h * H:j - h * H + 1], axis=0)).then_inc(arrived[j], 16)
                        over_edge_turns(e, body)

                    @block.scalar
                    def _(e):
                        def copy_next(i, h, g):
                            at = (i, h) if g + 1 < so.G else next_group(i, h)
                            if at:
                                so.copy_tile(e, *at, (g + 1) % so.G)
                        if sort:
                            so.copy_tile(e, 0, 0, 0)

                        def body(i, first):
                            if not first:
                                e.wait_ge(weighted, i * U)
                                e.sem_inc(held, 1)
                            nc.scalar.activation(ea_s[:, :], ea[:, bass.ds(i * U, U)], ACT.Copy).then_inc(ea_set, 1)
                            e.wait_ge(ea_set, i + 1)
                            for j in range(U):
                                e.wait_ge(arrived[j], 16 * (i + 1))
                                if not first:
                                    e.wait_ge(summed, (i - 1) * U + j + 2)
                                nc.scalar.activation(msg[:, j, :], got[:, j, :], ACT.Copy, scale=ea_s[:, j:j + 1]).then_inc(weighted, 1)
                                if sort and j % H in TILE_AFTER:
                                    copy_next(i, j // H, TILE_AFTER[j % H])
                        over_edge_turns(e, body)
                        if sort:
                            so.keep_running(e, PLACED)

                    @block.vector
                    def _(e):
                        v = nc.vector
                        v.memset(run[:, U - 1, :], 0.0).then_inc(summed, 1)
                        if sort:
                            so.masks(e, 0, 0)
                            for g in range(so.G):
                                so.rank_tile(e, 0, 0, g)

                        def body(i, first):
                            if not first:
                                e.wait_ge(summed, i * U + 1)
                                e.sem_inc(held, 1)
                            v.tensor_copy(keep_s[:, :], keep[:, bass.ds(i * U, U)]).then_inc(keep_set, 1)
                            e.wait_ge(keep_set, i + 1)
                            for j in range(U):
                                nxt = next_group(i, j // H)
                                if sort and j % H == 0 and nxt:
                                    so.masks(e, *nxt)
                                if j % H == 0 and not first:
                                    e.wait_ge(run_kept[j // H], 16 * i)
                                e.wait_ge(weighted, i * U + j + 1)
                                e.wait_ge(summed, i * U + j + 1)
                                v.scalar_tensor_tensor(out=run[:, j, :], in0=run[:, (j - 1) % U, :], scalar=keep_s[:, j:j + 1],
                                                       in1=msg[:, j, :], op0=ALU.mult, op1=ALU.add).then_inc(summed, 1)
                                if sort and j % H in TILE_AFTER:
                                    so.place_tile(e, i, j // H, TILE_AFTER[j % H])
                                    if nxt:
                                        so.rank_tile(e, *nxt, TILE_AFTER[j % H])
                                if sort and j % H == H - 1:
                                    so.finish_group(e, i, j // H)
                        over_edge_turns(e, body)
                        e.wait_ge(summed, T_GNN + 1)
                        v.tensor_copy(carry[:, :], run[:, U - 1, :])

                    @block.tensor
                    def _(e):
                        if not sort:
                            return
                        so.seed(e)

                        def body(i, first):
                            for h in range(2):
                                for g in range(so.G):
                                    so.use_tile(e, i, h, g)
                                    at = (i, h) if g + 1 < so.G else next_group(i, h)
                                    if at:
                                        so.turn_tile(e, *at, (g + 1) % so.G)
                        over_edge_turns(e, body)

                    @block.sync
                    def _(e):
                        if sort:
                            for j in range(2):
                                so.load_rows(e, 0, j)
                        if next_weights:
                            for c in range(2):
                                e.dma_start(next_weights[c][:, :, :], mixed_d[l + 1][:, c * P:(c + 1) * P, :].rearrange("r p o -> p r o")).then_inc(weights_in, 16)

                        def body(i, first):
                            for h in range(2):
                                if sort and not (isinstance(i, int) and i == turns - 1):
                                    so.load_rows(e, i + 1, h)
                                e.wait_ge(summed, i * U + (h + 1) * H + 1)
                                e.dma_start(run_view[:, bass.ds(i * U + h * H, H), :], run[:, h * H:(h + 1) * H, :]).then_inc(run_kept[h], 16)
                        over_edge_turns(e, body)
                        for h in range(2):
                            e.wait_ge(run_kept[h], 16 * turns)
                        if next_weights:
                            e.wait_ge(weights_in, 32)


        def gate_rows():
            with phase() as sc:
                MID, END = 6, 1
                PAIRS = NT // 2
                assert NT % 2
                wg = sb("wg", [P, 2, HEADS * EXPERTS], F32, sc)
                x_in, x_new, h_new = ([sb(f"g_{n}{k}", [P, D], F32, sc) for k in range(2)] for n in ("x_in", "x_new", "h_new"))
                stats2, mv2, ve2, rs2 = ([sb(f"g_{n}{k}", [P, w], F32, sc) for k in range(2)] for n, w in (("stats2", 6), ("mv2", 2), ("ve2", 1), ("rs2", 1)))
                hT = [sb(f"g_hT{k}", [P, 2, P], F32, sc) for k in range(2)]
                psT = [sc.enter_context(nc.psum_tensor(f"g_psT{k}", [P, 512], F32)) for k in range(2)]
                psG = [sc.enter_context(nc.psum_tensor(f"g_psG{k}", [P, 512], F32)) for k in range(2)]
                S = {n: sem(f"g_{n}") for n in ("turned", "hT_ready", "product", "evacuated", "held", "wg_in")}
                x_full, x_kept, h_kept, rooted2 = ([sem(f"g_{n}{k}") for k in range(2)] for n in ("x_full", "x_kept", "h_kept", "rooted2"))
                psC = [sc.enter_context(nc.psum_tensor(f"g_psC{k}", [P, 512], F32)) for k in range(2)]
                tail = Tail("g", sc, 2, HEAD_STEPS + MID + END, MID, [p[:, 0:D] for p in psC])
                PER = HEAD_STEPS + MID + END
                MID_BEGUN = PER + Tail.MASKS
                MID_DONE = MID_BEGUN + MID
                SUMS = HEAD_STEPS - Tail.MASKS
                END_DONE = MID_DONE + SUMS + END

                def at(i, steps):
                    return i * PER + steps

                def over_pairs_ahead(e, before, body):
                    before(0, (0, 1))
                    body(0, (0, 1), (0, 1))
                    with e.Fori(1, PAIRS - 1) as i:
                        body(i, (0, 1), (0, 1))
                    body(PAIRS - 1, (0, 1), (0,))
                    body(PAIRS, (0,), ())

                def over_pairs_two_ahead(e, before, body):
                    before(0, (0, 1))
                    body(0, (0, 1), (0, 1))
                    with e.Fori(1, PAIRS - 2) as i:
                        body(i, (0, 1), (0, 1))
                    body(PAIRS - 2, (0, 1), (0, 1))
                    body(PAIRS - 1, (0, 1), (0,))
                    body(PAIRS, (0,), ())

                with nc.Block() as block:
                    @block.sync
                    def _(e):
                        def load_x(i, slots):
                            for k in slots:
                                if later(i):
                                    e.wait_ge(tail.step[k], at(i - 1, MID_DONE - 3))
                                    e.sem_inc(S["held"], 1)
                                e.dma_start(x_in[k][:, :], x_pad[bass.ds((2 * i + k) * P, P), :]).then_inc(x_full[k], 16)

                        def before(i, slots):
                            for k in slots:
                                tail.load_rows(e, i, k)
                                tail.load(e, i, k)
                            for k in slots:
                                tail.load_rows(e, i + 1, k)

                        def body(i, slots, nexts):
                            load_x(i, slots)
                            for k in nexts:
                                tail.load(e, i + 1, k)
                            for k in nexts:
                                if not isinstance(i, int) or 2 * (i + 2) + k < NT:
                                    tail.load_rows(e, i + 2, k)
                        tail.load_vectors(e)
                        e.dma_start(wg[:, :, :], a["L0_ffn_W_gat"].rearrange("(c p) m -> p c m", p=P)).then_inc(S["wg_in"], 16)
                        over_pairs_two_ahead(e, before, body)

                    @block.vector
                    def _(e):
                        v = nc.vector
                        tail.vectors_ready(e)

                        def masks(i, slots):
                            tail.masks(e, tail.steps(e, i, slots, 0), i, slots)

                        def sums(i, slots):
                            tail.sums(e, tail.steps(e, i, slots, Tail.MASKS + MID), i, slots)

                        def before(i, slots):
                            masks(i, slots)
                            for k in slots:
                                e.wait_ge(tail.step[k], Tail.MASKS)
                                e.sem_inc(tail.step[k], MID)
                            sums(i, slots)
                            for k in slots:
                                e.wait_ge(tail.step[k], HEAD_STEPS + MID)
                                e.sem_inc(tail.step[k], END)

                        def body(i, slots, nexts):
                            for k in slots:
                                if k not in nexts:
                                    e.wait_ge(tail.step[k], at(i, PER))
                                    e.sem_inc(tail.step[k], Tail.MASKS)
                            if nexts:
                                masks(i + 1, nexts)
                            each = tail.steps(e, i, slots, MID_BEGUN)
                            tail.gain_and_shift(e, each, i, slots)
                            for k in slots:
                                e.wait_ge(x_full[k], 16 * (i + 1))
                                if later(i):
                                    e.wait_ge(x_kept[k], 16 * i)
                            each(lambda k: v.scalar_tensor_tensor(out=x_new[k][:, :], in0=tail.acc[k][:, :], scalar=0.0, in1=x_in[k][:, :],
                                                                  op0=ALU.max, op1=ALU.add))
                            layer_stats(e, each, x_new, stats2, mv2, ve2, S["held"])
                            if nexts:
                                sums(i + 1, nexts)
                            for k in slots:
                                if k not in nexts:
                                    e.wait_ge(tail.step[k], at(i, MID_DONE))
                                    e.sem_inc(tail.step[k], SUMS)
                                e.wait_ge(rooted2[k], i + 1)
                                if later(i):
                                    e.wait_ge(h_kept[k], 16 * i)
                                    e.wait_ge(S["turned"], 2 * i + k - 1)
                            each = tail.steps(e, i, slots, MID_DONE + SUMS)
                            each(lambda k: v.tensor_scalar(h_new[k][:, :], x_new[k][:, :], mv2[k][:, 0:1], rs2[k][:, :], ALU.subtract, ALU.mult))
                        over_pairs_ahead(e, before, body)

                    @block.tensor
                    def _(e):
                        e.wait_ge(S["wg_in"], 16)

                        def before(i, slots):
                            for k in slots:
                                tail.cross_product(e, i, k)

                        def body(i, slots, nexts):
                            before(i + 1, nexts)
                            for k in slots:
                                n = 2 * i + k
                                e.wait_ge(tail.step[k], at(i, END_DONE))
                                if later(i):
                                    e.wait_ge(S["hT_ready"], n - 1)
                                for c in range(2):
                                    m = nc.tensor.transpose(psT[k][:, c * P:(c + 1) * P], h_new[k][:, c * P:(c + 1) * P], ident[:, :])
                                m.then_inc(S["turned"], 1)
                                e.wait_ge(S["hT_ready"], n + 1)
                                if later(i):
                                    e.wait_ge(S["evacuated"], n - 1)
                                for c in range(2):
                                    m = nc.tensor.matmul(psG[k][:, 0:16], hT[k][:, c, :], wg[:, c, :], start=(c == 0), stop=(c == 1))
                                m.then_inc(S["product"], 1)
                        over_pairs_ahead(e, before, body)

                    @block.scalar
                    def _(e):
                        def body(i, slots, nexts):
                            for k in slots:
                                e.wait_ge(tail.step[k], at(i, MID_DONE - 3))
                                e.sem_inc(S["held"], 1)
                                e.dma_start(x2_d[bass.ds((2 * i + k) * P, P), :], x_new[k][:, :]).then_inc(x_kept[k], 16)
                            for k in slots:
                                n = 2 * i + k
                                e.wait_ge(tail.step[k], at(i, END_DONE))
                                e.sem_inc(S["held"], 1)
                                e.dma_start(xf_d[bass.ds(n * P, P), :], h_new[k][:, :]).then_inc(h_kept[k], 16)
                                e.wait_ge(S["turned"], n + 1)
                                nc.scalar.activation(hT[k][:, :, :].rearrange("p c n -> p (c n)"), psT[k][:, 0:2 * P], ACT.Copy).then_inc(S["hT_ready"], 1)
                                e.wait_ge(S["product"], n + 1)
                                e.sem_inc(S["held"], 1)
                                nc.scalar.activation(proj[:, bass.ds(n, 1), :].rearrange("p a m -> p (a m)"), psG[k][:, 0:16], ACT.Copy).then_inc(S["evacuated"], 1)
                        over_pairs_ahead(e, lambda i, slots: None, body)
                        e.wait_ge(S["evacuated"], NT)
                        for k in range(2):
                            e.wait_ge(x_kept[k], 16 * (PAIRS + 1 - k))
                            e.wait_ge(h_kept[k], 16 * (PAIRS + 1 - k))

                    @block.gpsimd
                    def _(e):
                        def before(i, slots):
                            for k in slots:
                                tail.fetch(e, i, k)
                            for k in slots:
                                tail.add_bias(e, i, k)
                            for k in slots:
                                tail.inverse_root(e, i, k)
                            for k in slots:
                                tail.fetch(e, i + 1, k)
                            for k in slots:
                                tail.add_bias(e, i + 1, k)

                        def body(i, slots, nexts):
                            for k in slots:
                                e.wait_ge(tail.step[k], at(i, MID_DONE))
                                inverse_root(e, rs2[k], ve2[k], rooted2[k])
                            for k in nexts:
                                tail.inverse_root(e, i + 1, k)
                            ahead = [k for k in nexts if not isinstance(i, int) or 2 * (i + 2) + k < NT]
                            for k in ahead:
                                tail.fetch(e, i + 2, k)
                            for k in ahead:
                                tail.add_bias(e, i + 2, k)
                        over_pairs_two_ahead(e, before, body)

        def gat_keys():
            C = T_GAT // P
            with phase() as sc:
                raw = [sb(f"raw{r}", [P, T_GAT], I32, sc) for r in range(2)]
                rawf = [sb(f"rawf{r}", [P, T_GAT], F32, sc) for r in range(2)]
                part = [sb(f"gat_part{r}", [P, T_GAT], I32, sc) for r in range(2)]
                ps = [[sc.enter_context(nc.psum_tensor(f"k_ps{r}{h}", [P, 512], F32)) for h in range(2)] for r in range(2)]
                k_in, k_step, k_turned = sem("k_in"), sem("k_step"), sem("k_turned")
                with nc.Block() as block:
                    @block.sync
                    def _(e):
                        for r in range(2):
                            e.dma_start(raw[r][:, :], a["L0_ffn_edge_index"][r, :].rearrange("(p t) -> p t", t=T_GAT)).then_inc(k_in, 16)
                        e.wait_ge(k_in, 32)

                    @block.tensor
                    def _(e):
                        e.wait_ge(k_step, 2)
                        for r in range(2):
                            for c in range(C):
                                m = nc.tensor.transpose(ps[r][c // 4][:, (c % 4) * P:(c % 4 + 1) * P], rawf[r][:, c * P:(c + 1) * P], ident[:, :])
                        m.then_inc(k_turned, 1)

                    @block.vector
                    def _(e):
                        v = nc.vector
                        st = Steps(e, k_step, 0, 99)
                        e.wait_ge(k_in, 32)
                        st(v.tensor_scalar(rawf[0][:, :], raw[0][:, :], float(N - 1), None, ALU.min))
                        st(v.tensor_copy(rawf[1][:, :], raw[1][:, :]))
                        e.wait_ge(k_turned, 1)
                        for h in range(2):
                            for r in range(2):
                                view = edge_pair[:, :, r].rearrange("p (q c) -> p c q", c=C)[:, 4 * h:4 * h + 4, :]
                                st(v.tensor_copy(view, ps[r][h][:, :].rearrange("p (j q) -> p j q", j=4)))
                            view = gat_dst[:, :].rearrange("p (q c) -> p c q", c=C)[:, 4 * h:4 * h + 4, :]
                            st(v.tensor_copy(view, ps[1][h][:, :].rearrange("p (j q) -> p j q", j=4)))
                        st.wait()
                        st(v.tensor_single_scalar(part[0][:, :], edge_pair[:, :, 1], P - 1, ALU.bitwise_and))
                        st(v.tensor_single_scalar(part[1][:, :], edge_pair[:, :, 1], 7, ALU.logical_shift_right))
                        st.wait()
                        st(v.tensor_copy(gat_lo[:, :], part[0][:, :]))
                        st(v.tensor_copy(gat_hi[:, :], part[1][:, :]))
                        st.wait()

        def finish_gat(v, st, cnt):
            st(v.tensor_scalar(gat_has[:, :], cnt[:, :], 1.0, None, ALU.min))
            st(v.tensor_scalar(gat_last_i[:, :], gat_after[:, :], -1.0, 0.0, ALU.add, ALU.max))
            st.wait()
            st(v.tensor_scalar(gat_tmp[:, :], gat_has[:, :], -1.0, 1.0, ALU.mult, ALU.add))
            st(v.tensor_tensor(gat_tmp2[:, :], gat_first[:, :], gat_has[:, :], ALU.mult))
            st.wait()
            st(v.tensor_tensor(gat_tmp[:, :], gat_tmp[:, :], gat_spare[:, :], ALU.mult))
            st.wait()
            st(v.tensor_tensor(gat_tmp[:, :], gat_tmp[:, :], gat_tmp2[:, :], ALU.add))
            st.wait()
            st(v.tensor_copy(gat_start_i[:, :], gat_tmp[:, :]))
            st.wait()

        class Sorter:

            def __init__(self, tag, sc, slots, G, base, start, kept=None, banks=2):
                self.SG, self.G, self.base_tile, self.start, self.kept = slots, G, base, start, kept
                self.banks = banks
                assert G % 2 == 0 and slots * G % banks == 0
                self.eq_lo = [sb(f"{tag}_eq_lo{j}", [P, G, P], BF16, sc) for j in range(slots)]
                self.eq_hi = [sb(f"{tag}_eq_hi{j}", [P, G, KH], BF16, sc) for j in range(slots)]
                self.rows = [sb(f"{tag}_rows{j}", [P, G * P], I32, sc) for j in range(slots)]
                self.dst_s = [sb(f"{tag}_dst{j}", [P, G], F32, sc) for j in range(slots)]
                self.rank = [sb(f"{tag}_rank{j}", [P, G], F32, sc) for j in range(slots)]
                self.place = [sb(f"{tag}_place{j}", [P, G], F32, sc) for j in range(slots)]
                self.place_i = [sb(f"{tag}_place_i{j}", [P, G], I32, sc) for j in range(slots)]
                self.pair_s = [sb(f"{tag}_pair{j}", [P, G, 2], I32, sc) for j in range(slots)]
                self.eqT = [sb(f"{tag}_eqT{j}", [P, P], F32, sc) for j in range(2)]
                self.base = [sb(f"{tag}_base{j}", [P, KH], F32, sc) for j in range(2)]
                self.junk = sb(f"{tag}_junk", [P, P], F32, sc)
                self.junk2 = sb(f"{tag}_junk2", [P, KH], F32, sc)
                self.psT = sc.enter_context(nc.psum_tensor(f"{tag}_psT", [P, 1024], BF16))
                self.psB = [sc.enter_context(nc.psum_tensor(f"{tag}_psB{j}", [P, 512], F32)) for j in range(banks)]
                self.psR = sc.enter_context(nc.psum_tensor(f"{tag}_psR", [P, 512], F32))
                (self.eq_ready, self.turned, self.eqT_ready, self.based, self.looked, self.added, self.dst_set, self.ranked,
                 self.placed, self.placed_i, self.pair_set, self.held) = (
                    sem(f"{tag}_{n}") for n in ("eq_ready", "turned", "eqT_ready", "based", "looked", "added", "dst_set", "ranked",
                                                "placed", "placed_i", "pair_set", "held"))
                self.rows_in = [sem(f"{tag}_rows_in{j}") for j in range(slots)]
                if kept is None:
                    self.sent = [[sem(f"{tag}_sent{j}_{g}") for g in range(G)] for j in range(slots)]

            def after(self, i, j, g=None):
                if g is not None and g + 1 < self.G:
                    return i, j, g + 1
                at = (i, j + 1) if j + 1 < self.SG else (i + 1, 0)
                return at if g is None else (*at, 0)

            def load_rows(self, e, i, j):
                gl, G = i * self.SG + j, self.G
                if later(i):
                    e.wait_ge(self.ranked, (gl - self.SG + 1) * G)
                    e.sem_inc(self.held, 1)
                src = a["L0_ffn_edge_index"][1, bass.ds((gl * G + self.base_tile) * P, G * P)]
                e.dma_start(self.rows[j][:, :], src.unsqueeze(0).to_broadcast([P, G * P])).then_inc(self.rows_in[j], 16)

            def masks(self, e, i, j):
                gl, G, v = i * self.SG + j, self.G, nc.vector
                if later(i):
                    e.wait_ge(self.added, (gl - self.SG + 1) * G + 1)
                    e.wait_ge(self.placed, (gl - self.SG + 1) * G)
                    e.wait_ge(self.placed_i, gl - self.SG + 1)
                at = bass.ds(gl * G + self.base_tile, G)
                v.tensor_tensor(self.eq_lo[j][:, :, :], gat_lo[:, at].unsqueeze(2).to_broadcast([P, G, P]),
                                iota_row[:, :].unsqueeze(1).to_broadcast([P, G, P]), ALU.is_equal).then_inc(self.eq_ready, 1)
                v.tensor_tensor(self.eq_hi[j][:, :, :], gat_hi[:, at].unsqueeze(2).to_broadcast([P, G, KH]),
                                iota_row[:, 0:KH].unsqueeze(1).to_broadcast([P, G, KH]), ALU.is_equal).then_inc(self.eq_ready, 1)
                if later(i):
                    e.wait_ge(self.ranked, (gl - self.SG + 1) * G)
                    e.sem_inc(self.held, 1)
                v.tensor_copy(self.dst_s[j][:, :], gat_dst[:, at]).then_inc(self.dst_set, 1)
                e.wait_ge(self.dst_set, gl + 1)
                e.wait_ge(self.rows_in[j], 16 * (i + 1))

            def rank_tile(self, e, i, j, g):
                t = (i * self.SG + j) * self.G + g
                if later(i) or j or g:
                    e.wait_ge(self.ranked, t)
                nc.vector.scalar_tensor_tensor(out=self.junk[:, :], in0=self.rows[j][:, g * P:(g + 1) * P], scalar=self.dst_s[j][:, g:g + 1],
                                               in1=earlier[:, :], op0=ALU.is_equal, op1=ALU.mult,
                                               accum_out=self.rank[j][:, g:g + 1]).then_inc(self.ranked, 1)

            def place_tile(self, e, i, j, g):
                gl = i * self.SG + j
                t = gl * self.G + g
                if g == 0:
                    e.wait_ge(self.ranked, (gl + 1) * self.G)
                    e.wait_ge(self.eq_ready, 2 * gl + 2)
                e.wait_ge(self.looked, t + 1)
                if later(i) or j or g:
                    e.wait_ge(self.placed, t)
                nc.vector.scalar_tensor_tensor(out=self.junk2[:, :], in0=self.psB[(j * self.G + g) % self.banks][:, 0:KH], scalar=self.rank[j][:, g:g + 1],
                                               in1=self.eq_hi[j][:, g, :], op0=ALU.add, op1=ALU.mult,
                                               accum_out=self.place[j][:, g:g + 1]).then_inc(self.placed, 1)

            def finish_group(self, e, i, j):
                gl = i * self.SG + j
                e.wait_ge(self.placed, (gl + 1) * self.G)
                if self.kept is not None:
                    e.sem_inc(self.held, 1)
                    nc.vector.tensor_copy(self.kept[:, bass.ds(gl * self.G, self.G)], self.place[j][:, :]).then_inc(self.placed_i, 1)
                    return
                if later(i):
                    for g in range(self.G):
                        e.wait_ge(self.sent[j][g], 16 * i)
                nc.vector.tensor_copy(self.place_i[j][:, :], self.place[j][:, :]).then_inc(self.placed_i, 1)

            def seed(self, e):
                nc.tensor.matmul(self.psR[:, 0:KH], ident[:, :], self.start[:, :], start=True, stop=True).then_inc(self.added, 1)
                self.turn_tile(e, 0, 0, 0)

            def turn_tile(self, e, i, j, g):
                gl = i * self.SG + j
                if g == 0:
                    e.wait_ge(self.eq_ready, 2 * gl + 2)
                if later(i) or j or g:
                    e.wait_ge(self.eqT_ready, gl * self.G + g)
                nc.tensor.transpose(self.psT[:, 0:P], self.eq_lo[j][:, g, :], identb[:, :]).then_inc(self.turned, 1)

            def use_tile(self, e, i, j, g):
                t = (i * self.SG + j) * self.G + g
                e.wait_ge(self.eqT_ready, t + 1)
                e.wait_ge(self.based, t + 1)
                if later(i) or j * self.G + g >= self.banks:
                    e.wait_ge(self.placed, t - self.banks + 1)
                nc.tensor.matmul(self.psB[(j * self.G + g) % self.banks][:, 0:KH], self.eqT[g % 2][:, :], self.base[g % 2][:, :], start=True, stop=True).then_inc(self.looked, 1)
                nc.tensor.matmul(self.psR[:, 0:KH], self.eq_lo[j][:, g, :], self.eq_hi[j][:, g, :], start=False, stop=True,
                                 skip_group_check=True).then_inc(self.added, 1)

            def copy_tile(self, e, i, j, g):
                t = (i * self.SG + j) * self.G + g
                if later(i) or j or g >= 2:
                    e.wait_ge(self.looked, t - 1)
                e.wait_ge(self.turned, t + 1)
                nc.scalar.activation(self.eqT[g % 2][:, :], self.psT[:, 0:P], ACT.Copy).then_inc(self.eqT_ready, 1)
                e.wait_ge(self.added, t + 1)
                nc.scalar.activation(self.base[g % 2][:, :], self.psR[:, 0:KH], ACT.Copy).then_inc(self.based, 1)

            def keep_running(self, e, tiles):
                e.wait_ge(self.added, tiles + 1)
                nc.scalar.activation(gat_running[:, :], self.psR[:, 0:KH], ACT.Copy).then_inc(self.held, 1)

            def send_group(self, e, i, j):
                gl, G = i * self.SG + j, self.G
                if later(i):
                    for g in range(G):
                        e.wait_ge(self.sent[j][g], 16 * i)
                    e.sem_inc(self.held, 1)
                e.tensor_copy(self.pair_s[j][:, :, :], edge_pair[:, bass.ds(gl * G + self.base_tile, G), :]).then_inc(self.pair_set, 1)
                e.wait_ge(self.pair_set, gl + 1)
                e.wait_ge(self.placed_i, gl + 1)
                e.sem_inc(self.held, 1)
                for g in range(G):
                    e.indirect_dma_start(out=sorted_d[:, :], out_offset=bass.IndirectOffsetOnAxis(ap=self.place_i[j][:, g:g + 1], axis=0),
                                         in_=self.pair_s[j][:, g, :], in_offset=None).then_inc(self.sent[j][g], 16)

            def all_sent(self, e, turns):
                for j in range(self.SG):
                    for g in range(self.G):
                        e.wait_ge(self.sent[j][g], 16 * turns)

        def over_turns(eng, turns, body):
            body(0)
            if turns > 1:
                with eng.Fori(1, turns) as i:
                    body(i)

        def sort_rest(base):
            G = 2
            turns = (T_GAT - base) // (2 * G)
            assert turns * 2 * G == T_GAT - base
            with phase() as sc:
                so = Sorter("s", sc, 2, G, base, gat_running)
                with nc.Block() as block:
                    @block.sync
                    def _(e):
                        over_turns(e, turns, lambda i: [so.load_rows(e, i, j) for j in range(2)])

                    @block.vector
                    def _(e):
                        def body(i):
                            for j in range(2):
                                so.masks(e, i, j)
                                for g in range(G):
                                    so.rank_tile(e, i, j, g)
                                for g in range(G):
                                    so.place_tile(e, i, j, g)
                                so.finish_group(e, i, j)
                        over_turns(e, turns, body)

                    @block.tensor
                    def _(e):
                        nc.tensor.matmul(so.psR[:, 0:KH], ident[:, :], so.start[:, :], start=True, stop=True).then_inc(so.added, 1)

                        def body(i):
                            for j in range(2):
                                for g in range(G):
                                    so.turn_tile(e, i, j, g)
                                    so.use_tile(e, i, j, g)
                        over_turns(e, turns, body)

                    @block.scalar
                    def _(e):
                        over_turns(e, turns, lambda i: [so.copy_tile(e, i, j, g) for j in range(2) for g in range(G)])

                    @block.gpsimd
                    def _(e):
                        over_turns(e, turns, lambda i: [so.send_group(e, i, j) for j in range(2)])
                        so.all_sent(e, turns)

        def spread_evenly(tiles):
            return [range(p * tiles // Products.PLACES, (p + 1) * tiles // Products.PLACES) for p in range(Products.PLACES)]

        class Histogram:
            G, CHUNKS = 4, 8

            def __init__(self, sc):
                self.ps = sc.enter_context(nc.psum_tensor("h_ps", [P, 512], F32))
                self.eq_lo = [sb(f"h_eq_lo{j}", [P, self.G, P], BF16, sc) for j in range(2)]
                self.eq_hi = [sb(f"h_eq_hi{j}", [P, self.G, KH], BF16, sc) for j in range(2)]
                self.zb = sb("h_zb", [P, P], BF16, sc)
                self.zero_set, self.masked, self.used, self.counted = (sem(f"h_{n}") for n in ("zero_set", "masked", "used", "counted"))
                self.positions = Positions("h", sc, self.counted, self.ps[:, 0:KH], self.ps[:, KH:2 * KH], first_gnn, after_gnn, bounds_gnn, finish_gnn)

            def zero(self, e):
                nc.vector.memset(self.zb[:, :], 0.0).then_inc(self.zero_set, 1)

            def masks(self, e, i, c):
                m, G, v, j = i * self.CHUNKS + c, self.G, nc.vector, c % 2
                if later(i) or c >= 2:
                    e.wait_ge(self.used, m - 1)
                at = bass.ds(m * G, G)
                v.tensor_tensor(self.eq_lo[j][:, :, :], lo_gnn[:, at].unsqueeze(2).to_broadcast([P, G, P]),
                                iota_row[:, :].unsqueeze(1).to_broadcast([P, G, P]), ALU.is_equal).then_inc(self.masked, 1)
                v.tensor_tensor(self.eq_hi[j][:, :, :], hi_gnn[:, at].unsqueeze(2).to_broadcast([P, G, KH]),
                                iota_row[:, 0:KH].unsqueeze(1).to_broadcast([P, G, KH]), ALU.is_equal).then_inc(self.masked, 1)

            def begin(self, e):
                e.wait_ge(self.zero_set, 1)
                nc.tensor.matmul(self.ps[:, 0:KH], self.zb[:, :], self.zb[:, 0:KH], start=True, stop=False)

            def add(self, e, i, c):
                j = c % 2
                e.wait_ge(self.masked, 2 * (i * self.CHUNKS + c + 1))
                for g in range(self.G):
                    m = nc.tensor.matmul(self.ps[:, 0:KH], self.eq_lo[j][:, g, :], self.eq_hi[j][:, g, :], start=False, stop=False)
                m.then_inc(self.used, 1)

            def end(self, e):
                nc.tensor.matmul(self.ps[:, 0:KH], self.zb[:, :], self.zb[:, 0:KH], start=False, stop=True).then_inc(self.counted, 1)

            def left(self, turns):
                rest = T_GNN // self.G - turns * self.CHUNKS
                assert 0 <= rest <= self.CHUNKS and T_GNN % self.G == 0
                return range(rest)

        def first_nodes_and_sort():
            TURNS = NT // 2
            SG, G = SORT
            with phase() as sc:
                psT = sc.enter_context(nc.psum_tensor("m_psTh", [P, 512], F32))
                pr = Products("m", sc, 0, psT, 2)
                hist = Histogram(sc)
                so = Sorter("m", sc, SG, G, 0, gat_first)
                h_in, stats, mv, ve, rs = ([sb(f"m_{n}{k}", [P, w], F32, sc) for k in range(2)]
                                           for n, w in (("h_in", D), ("stats", 6), ("mv", 2), ("ve", 1), ("rs", 1)))
                step, held, rooted1 = sem("m_step"), sem("m_held2"), sem("m_rooted")
                h_full = [sem(f"m_h_full{k}") for k in range(2)]
                PER = 4
                tiles_at = spread_evenly(SG * G)

                def load(e, i, k):
                    n = 2 * i + k
                    if later(i):
                        e.wait_ge(step, (n - 1) * PER)
                        e.sem_inc(held, 1)
                    e.dma_start(h_in[k][:, :], x_pad[bass.ds(n * P, P), :]).then_inc(h_full[k], 16)

                def norm_begin(e, i, k):
                    e.wait_ge(h_full[k], 16 * (i + 1))
                    st = Steps(e, step, 2 * i + k, PER)
                    st(nc.vector.bn_stats(stats[k][:, :], h_in[k][:, :]))
                    st.wait()
                    e.sem_inc(held, 1)
                    st(nc.vector.bn_aggr(mv[k][:, :], stats[k][:, :]))
                    st.wait()
                    st(nc.vector.tensor_scalar(ve[k][:, :], mv[k][:, 1:2], EPS, None, ALU.add))

                def root(e, i, k):
                    e.wait_ge(step, (2 * i + k) * PER + 3)
                    inverse_root(e, rs[k], ve[k], rooted1)

                def norm_end(e, i, k):
                    e.wait_ge(rooted1, 2 * i + k + 1)
                    pr.h_free(e, i, k)
                    nc.vector.tensor_scalar(pr.h_new[k][:, :], h_in[k][:, :], mv[k][:, 0:1], rs[k][:, :], ALU.subtract, ALU.mult).then_inc(step, 1)

                with nc.Block() as block:
                    @block.sync
                    def _(e):
                        for k in range(2):
                            load(e, 0, k)
                        so.load_rows(e, 0, 0)
                        pr.load_weights(e)

                        def body(i):
                            for j in range(SG):
                                if j in (0, SG // 2):
                                    load(e, i + 1, int(j > 0))
                                so.load_rows(e, *so.after(i, j))
                        over_turns(e, TURNS, body)
                        hist.positions.sync(e)

                    @block.vector
                    def _(e):
                        hist.zero(e)
                        for k in range(2):
                            norm_begin(e, 0, k)
                            norm_end(e, 0, k)
                        so.masks(e, 0, 0)
                        for g in range(G):
                            so.rank_tile(e, 0, 0, g)

                        def body(i):
                            for j in range(SG):
                                nxt = so.after(i, j)
                                so.masks(e, *nxt)
                                if j in (0, SG // 2):
                                    norm_begin(e, i + 1, int(j > 0))
                                for g in range(G):
                                    so.place_tile(e, i, j, g)
                                    so.rank_tile(e, *nxt, g)
                                    t = j * G + g
                                    if t % 2 and t // 2 < hist.CHUNKS:
                                        hist.masks(e, i, t // 2)
                                so.finish_group(e, i, j)
                                if j in (0, SG - 1):
                                    norm_end(e, i + 1, int(j == SG - 1))
                        over_turns(e, TURNS, body)
                        for c in hist.left(TURNS):
                            hist.masks(e, TURNS, c)
                        hist.positions.vector(e)

                    @block.tensor
                    def _(e):
                        hist.begin(e)
                        so.seed(e)
                        e.wait_ge(pr.w_in, 32)

                        def turn(i, k):
                            e.wait_ge(step, (2 * i + k + 1) * PER)
                            pr.turn(e, i, k)
                        turn(0, 0)

                        def body(i):
                            def sorting(place):
                                for t in tiles_at[place]:
                                    so.use_tile(e, i, *divmod(t, G))
                                    so.turn_tile(e, *so.after(i, *divmod(t, G)))
                                    if t % 2 and 0 <= t // 2 - 1 < hist.CHUNKS:
                                        hist.add(e, i, t // 2 - 1)
                            for k in range(2):
                                pr.multiply(e, i, k, sorting, lambda: turn(*next_tile(i, k)))
                        over_turns(e, TURNS, body)
                        for c in hist.left(TURNS):
                            hist.add(e, TURNS, c)
                        hist.end(e)
                        pr.multiply(e, TURNS, 0, lambda place: None, lambda: None)
                        hist.positions.tensor(e)

                    @block.scalar
                    def _(e):
                        so.copy_tile(e, 0, 0, 0)
                        pr.take(e, 0, 0)

                        def body(i):
                            def sorting(place):
                                for t in tiles_at[place]:
                                    so.copy_tile(e, *so.after(i, *divmod(t, G)))
                            for k in range(2):
                                pr.evacuate(e, i, k, sorting, lambda: pr.take(e, *next_tile(i, k)))
                        over_turns(e, TURNS, body)
                        pr.evacuate(e, TURNS, 0, lambda place: None, lambda: None)
                        so.keep_running(e, TURNS * SG * G)
                        pr.all_kept(e)

                    @block.gpsimd
                    def _(e):
                        for k in range(2):
                            root(e, 0, k)

                        def body(i):
                            for j in range(SG):
                                if j in (0, SG // 2):
                                    root(e, i + 1, int(j > 0))
                                so.send_group(e, i, j)
                        over_turns(e, TURNS, body)
                        so.all_sent(e, TURNS)

        EDGE_BASE = NT // 2 * SORT[0] * SORT[1]
        PLACED = T_GNN // U * EDGE_SORT[0] * EDGE_SORT[1]
        x2_d, xf_d = dram("x2_d", (NP, D)), dram("xf_d", (NP, D))
        sorted_d = dram("sorted_d", (E_GAT, 2), I32)
        y_d = dram("y_d", (NP, EXPERTS, D))
        bounds_gat = dram("bounds_gat", (2, KEYS))
        proj = sb("proj", [P, NT, HEADS * EXPERTS])
        gat_first, gat_after, gat_has, gat_tmp, gat_tmp2, gat_spare = (
            sb(n, [P, KH]) for n in ("gat_first", "gat_after", "gat_has", "gat_tmp", "gat_tmp2", "gat_spare"))
        gat_last_i, gat_start_i, spare_i = (sb(n, [P, KH], I32) for n in ("gat_last_i", "gat_start_i", "spare_i"))
        split_gat, split_gat_i = sb("split_gat", [P, 1]), sb("split_gat_i", [P, 1], I32)
        earlier = sb("earlier", [P, P])
        identb = sb("identb", [P, P], BF16)
        gat_running = sb("gat_running", [P, KH])

        def gat_constants(gk):
            c_made, c_cast = sem("c_made"), sem("c_cast")
            with nc.Block() as block:
                @block.gpsimd
                def _(e):
                    e.iota(spare_i[:, :], pattern=[[P, KH]], base=E_GAT, channel_multiplier=1).then_inc(c_made, 1)
                    e.iota(split_gat_i[:, :], pattern=[[0, 1]], base=T_GAT, channel_multiplier=T_GAT).then_inc(c_made, 1)
                    e.affine_select(out=earlier[:, :], in_=ones[:, :], compare_op=ALU.is_gt, fill=0.0, base=0,
                                    pattern=[[-1, P]], channel_multiplier=1).then_inc(c_made, 1)
                    e.wait_ge(c_made, 3)

                @block.vector
                def _(e):
                    e.wait_ge(c_made, 2)
                    nc.vector.tensor_copy(gat_spare[:, :], spare_i[:, :]).then_inc(c_cast, 1)
                    nc.vector.tensor_copy(split_gat[:, :], split_gat_i[:, :]).then_inc(c_cast, 1)
                    nc.vector.tensor_copy(identb[:, :], ident[:, :]).then_inc(c_cast, 1)
                    e.wait_ge(c_cast, 3)

        with phase() as gk:
            gat_constants(gk)
            edge_pair = sb("edge_pair", [P, T_GAT, 2], I32, gk)
            gat_dst, gat_lo, gat_hi = (sb(n, [P, T_GAT], F32, gk) for n in ("gat_dst", "gat_lo", "gat_hi"))
            gat_keys()
            count("gat", gat_lo, gat_hi, T_GAT, gat_first, gat_after, bounds_gat, finish_gat, Mix)
            first_nodes_and_sort()
            place_kept = sb("place_kept", [P, PLACED], I32, gk)
            weights1 = [sb(f"n_weights{c}", [P, RELS + 1, D], F32, gk) for c in range(2)]
            edge_loop(0, sort=True, next_weights=weights1)
            sort_rest(EDGE_BASE + PLACED)
            node_loop(weights1)
        edge_loop(1)
        gate_rows()

        REDUCE_LAST = AX.X
        BIG = 1e30
        gat_table = dram("gat_table", (NP, REC))
        mx_d = dram("mx_d", (E_GAT, HEADS))
        start_d = dram("start_d", (E_GAT + KEYS, 2 * HEADS))
        node_d = dram("node_d", (NP, 2 * HEADS))
        run20_d = dram("run20_d", (E_GAT, REC))
        a_src, a_dst = (sb(n, [P, NT, HEADS]) for n in ("a_src", "a_dst"))
        gates = sb("gates", [P, NT, EXPERTS])
        C16 = HEADS * EXPERTS

        def spread(ap, shape):
            return ap.unsqueeze(len(shape) - 1).to_broadcast(shape)

        def gat_records(sc, srt):
            rec = sb("rec_all", [P, NT, REC], F32, sc)
            att = [sb(f"att_v{r}", [P, C16], F32, sc) for r in range(2)]
            tmp = [sb(f"att_tmp{r}", [P, NT, C16], F32, sc) for r in range(2)]
            att_in, r_step, rec_out, srt_in = sem("att_in"), sem("r_step"), sem("rec_out"), sem("srt_in")
            with nc.Block() as block:
                @block.sync
                def _(e):
                    for r, n in enumerate(("L0_ffn_att_src", "L0_ffn_att_dst")):
                        e.dma_start(att[r][:, :], a[n].rearrange("h x -> (h x)").unsqueeze(0).to_broadcast([P, C16])).then_inc(att_in, 16)
                    e.dma_start(srt[:, :, :], sorted_d[:, :].rearrange("(p t) c -> p t c", t=T_GAT)).then_inc(srt_in, 16)
                    e.wait_ge(r_step, 6)
                    e.dma_start(gat_table[:, :].rearrange("(t p) c -> p t c", p=P), rec[:, :, :]).then_inc(rec_out, 16)
                    e.wait_ge(rec_out, 16)
                    e.wait_ge(srt_in, 16)

                @block.vector
                def _(e):
                    v = nc.vector
                    st = Steps(e, r_step, 0, 99)
                    e.wait_ge(att_in, 32)
                    for r in range(2):
                        st(v.tensor_tensor(tmp[r][:, :, :], proj[:, :, :], att[r][:, :].unsqueeze(1).to_broadcast([P, NT, C16]), ALU.mult))
                    for r, dst in enumerate((a_src, a_dst)):
                        st.wait()
                        st(v.reduce_sum(dst[:, :, :].rearrange("p n h -> p (n h)"),
                                        tmp[r][:, :, :].rearrange("p n (h x) -> p (n h) x", x=EXPERTS), REDUCE_LAST))
                    st.wait()
                    st(v.tensor_copy(rec[:, :, 0:HEADS], a_src[:, :, :]))
                    st(v.tensor_copy(rec[:, :, HEADS:REC], proj[:, :, :]))

        def gat_gather(srt, rec, sc):
            H = U // 2
            turns = T_GAT // U
            got = sb("t_got", [P, U, REC], F32, sc)
            idx = [sb(f"t_idx{h}", [P, H], I32, sc) for h in range(2)]
            idx_set, held, taken = sem("t_idx_set"), sem("t_held"), sem("t_taken")
            arrived = [sem(f"t_arrived{j}") for j in range(U)]

            def fetch(e):
                def body(i):
                    for h in range(2):
                        if later(i):
                            e.wait_ge(taken, (i - 1) * 2 + h + 1)
                            for j in range(h * H, (h + 1) * H):
                                e.wait_ge(arrived[j], 16 * i)
                        e.sem_inc(held, 1)
                        e.tensor_copy(idx[h][:, :], srt[:, bass.ds(i * U + h * H, H), 0]).then_inc(idx_set, 1)
                        e.wait_ge(idx_set, 2 * i + h + 1)
                        e.sem_inc(held, 1)
                        for j in range(h * H, (h + 1) * H):
                            e.indirect_dma_start(out=got[:, j, :], out_offset=None, in_=gat_table[:, :],
                                                 in_offset=bass.IndirectOffsetOnAxis(ap=idx[h][:, j - h * H:j - h * H + 1], axis=0)).then_inc(arrived[j], 16)
                body(0)
                with e.Fori(1, turns) as i:
                    body(i)

            def file(e):
                with e.Fori(0, turns) as i:
                    for h in range(2):
                        for j in range(h * H, (h + 1) * H):
                            e.wait_ge(arrived[j], 16 * (i + 1))
                        e.sem_inc(held, 1)
                        nc.vector.tensor_copy(rec[:, bass.ds(i * U + h * H, H), :], got[:, h * H:(h + 1) * H, :]).then_inc(taken, 1)
                e.wait_ge(taken, 2 * turns)
            return fetch, file

        def gat_softmax(srt, rec, sc):
            T = T_GAT
            PARTS = 4
            mx = sb("mx", [P, T, HEADS], F32, sc)
            fill = sb("fill", [P, T, 2 * HEADS], F32, sc)
            keep_t = sb("keep_t", [P, T], F32, sc)
            pen = sb("pen", [P, T], F32, sc)
            cols = sb("edge_cols", [P, 3 * HEADS], F32, sc)
            rows = sb("edge_rows", [HEADS, 3, P], F32, sc)
            link, thru, thru_pen, link_pen, c_out, c_in = (
                sb(n, [HEADS, P], F32, sc) for n in ("link", "thru", "thru_pen", "link_pen", "c_out", "c_in"))
            c_col = sb("c_col", [P, HEADS], F32, sc)
            mx_end = sb("mx_end", [P, NT, HEADS], F32, sc)
            zz = sb("zz", [P, NT, HEADS], F32, sc)
            pen_n = sb("pen_n", [P, NT], F32, sc)
            first_node = sb("first_node", [P, 1], I32, sc)
            init = sb("init", [P, 2 * HEADS], F32, sc)
            ps = sc.enter_context(nc.psum_tensor("m_ps", [P, 512], F32))
            ps2 = sc.enter_context(nc.psum_tensor("m_ps2", [P, 512], F32))
            d, t1, t2, mx_out, ends_in, zeroed, node_out, started, init_in, fill_in, z_set, ex_done, run_out, run_in = (
                sem(f"m_{n}") for n in ("d", "t1", "t2", "mx_out", "ends_in", "zeroed", "node_out", "started", "init_in", "fill_in",
                                        "z_set", "ex_done", "run_out", "run_in"))
            mark = {}
            with nc.Block() as block:
                @block.vector
                def _(e):
                    v = nc.vector
                    st = Steps(e, d, 0, 999)
                    dst = srt[:, :, 1]
                    st(v.memset(keep_t[:, 0:1], 1.0))
                    st(v.tensor_tensor(keep_t[:, 1:T], dst[:, 1:T], dst[:, 0:T - 1], ALU.is_equal))
                    st.wait()
                    st(v.tensor_scalar(pen[:, :], keep_t[:, :], -1.0, BIG, ALU.add, ALU.mult))
                    st(v.tensor_copy(cols[:, HEADS:2 * HEADS], dst[:, 0:1].to_broadcast([P, HEADS])))
                    st(v.tensor_copy(cols[:, 2 * HEADS:3 * HEADS], dst[:, T - 1:T].to_broadcast([P, HEADS])))
                    st(v.tensor_scalar(first_node[:, :], dst[:, 0:1], float(NP - 1), None, ALU.min))
                    st.wait()
                    for h in range(HEADS):
                        st(v.tensor_tensor_scan(mx[:, :, h], pen[:, :], rec[:, :, h], -BIG, ALU.add, ALU.max))
                    st.wait()
                    st(v.tensor_copy(cols[:, 0:HEADS], mx[:, T - 1, :]))
                    mark["cols"] = st.k
                    e.wait_ge(t1, 1)
                    st(v.tensor_copy(rows[:, :, :].rearrange("h c p -> h (c p)"), ps[0:HEADS, 0:3 * P]))
                    st.wait()
                    st(v.memset(link[:, 0:1], 0.0))
                    st(v.tensor_tensor(link[:, 1:P], rows[:, 1, 1:P], rows[:, 2, 0:P - 1], ALU.is_equal))
                    st(v.tensor_tensor(thru[:, :], rows[:, 1, :], rows[:, 2, :], ALU.is_equal))
                    st.wait()
                    st(v.tensor_tensor(thru[:, :], thru[:, :], link[:, :], ALU.mult))
                    st.wait()
                    st(v.tensor_scalar(thru_pen[:, :], thru[:, :], -1.0, BIG, ALU.add, ALU.mult))
                    st(v.tensor_scalar(link_pen[:, :], link[:, :], -1.0, BIG, ALU.add, ALU.mult))
                    st.wait()
                    st(v.tensor_tensor_scan(c_out[:, :], thru_pen[:, :], rows[:, 0, :], -BIG, ALU.add, ALU.max))
                    st.wait()
                    st(v.memset(c_in[:, 0:1], -BIG))
                    st(v.tensor_tensor(c_in[:, 1:P], c_out[:, 0:P - 1], link_pen[:, 1:P], ALU.add))
                    mark["c_in"] = st.k
                    e.wait_ge(t2, 1)
                    st(v.tensor_copy(c_col[:, :], ps2[:, 0:HEADS]))
                    st.wait()
                    for h in range(HEADS):
                        st(v.tensor_tensor_scan(mx[:, :, h], pen[:, :], rec[:, :, h], c_col[:, h:h + 1], ALU.add, ALU.max))
                    mark["mx"] = st.k
                    st(v.memset(fill[:, :, :], 0.0))
                    mark["zero"] = st.k
                    st(v.tensor_scalar(pen_n[:, :], gat_has[:, 0:NT], -1.0, BIG, ALU.add, ALU.mult))
                    e.wait_ge(ends_in, 16 * NT)
                    st.wait()
                    st(v.tensor_tensor(mx_end[:, :, :], mx_end[:, :, :], spread(pen_n[:, :], [P, NT, HEADS]), ALU.add))
                    st.wait()
                    st(v.tensor_tensor(mx_end[:, :, :], mx_end[:, :, :], a_src[:, :, :], ALU.max))
                    st.wait()
                    st(v.tensor_tensor(zz[:, :, :], mx_end[:, :, :], a_dst[:, :, :], ALU.add))
                    st.wait()
                    st(v.scalar_tensor_tensor(out=node8[:, :, HEADS:2 * HEADS], in0=zz[:, :, :], scalar=0.2, in1=zz[:, :, :],
                                              op0=ALU.mult, op1=ALU.max))
                    st(v.tensor_copy(node8[:, :, 0:HEADS], a_dst[:, :, :]))
                    mark["node8"] = st.k
                    e.wait_ge(fill_in, 16)
                    e.wait_ge(init_in, 16)
                    st(v.memset(fill[:, 0:1, :], 0.0))
                    st.wait()
                    for c in range(2 * HEADS):
                        st(v.tensor_tensor_scan(fill[:, :, c], keep_t[:, :], fill[:, :, c], init[:, c:c + 1], ALU.mult, ALU.add))
                    st.wait()
                    z = rec[:, :, 0:HEADS]
                    st(v.tensor_tensor(z, z, fill[:, :, 0:HEADS], ALU.add))
                    st.wait()
                    st(v.scalar_tensor_tensor(out=z, in0=z, scalar=0.2, in1=z, op0=ALU.mult, op1=ALU.max))
                    st.wait()
                    st(v.tensor_tensor(z, z, fill[:, :, HEADS:2 * HEADS], ALU.subtract))
                    st.wait()
                    st(v.tensor_scalar(z, z, 0.0, None, ALU.min))
                    mark["z"] = st.k
                    e.wait_ge(ex_done, 1)
                    for h in range(HEADS):
                        cells = rec[:, :, HEADS + EXPERTS * h:HEADS + EXPERTS * (h + 1)]
                        st(v.tensor_tensor(cells, cells, rec[:, :, h:h + 1].to_broadcast([P, T, EXPERTS]), ALU.mult))
                    st.wait()
                    for q in range(PARTS):
                        part = slice(q * T // PARTS, (q + 1) * T // PARTS)
                        for c in range(REC):
                            before = rec[:, part.start - 1, c:c + 1] if q else 0.0
                            st(v.tensor_tensor_scan(rec[:, part, c], keep_t[:, part], rec[:, part, c], before, ALU.mult, ALU.add))
                        st.wait()
                        mark["run", q] = st.k
                    st(v.tensor_copy(carry[:, 0:REC], rec[:, T - 1, :]))
                    st.wait()

                @block.tensor
                def _(e):
                    e.wait_ge(d, mark["cols"])
                    for c in range(3):
                        m = nc.tensor.transpose(ps[0:HEADS, c * P:(c + 1) * P], cols[:, c * HEADS:(c + 1) * HEADS], ident[:, :])
                    m.then_inc(t1, 1)
                    e.wait_ge(d, mark["c_in"])
                    nc.tensor.transpose(ps2[:, 0:HEADS], c_in[:, :], ident[0:HEADS, 0:HEADS]).then_inc(t2, 1)

                @block.scalar
                def _(e):
                    e.wait_ge(d, mark["z"])
                    nc.scalar.activation(rec[:, :, 0:HEADS], rec[:, :, 0:HEADS], ACT.Exp).then_inc(ex_done, 1)

                @block.sync
                def _(e):
                    e.wait_ge(d, mark["mx"])
                    e.dma_start(mx_d[:, :].rearrange("(p t) c -> p t c", t=T), mx[:, :, :]).then_inc(mx_out, 16)
                    e.wait_ge(d, mark["zero"])
                    e.dma_start(start_d[0:E_GAT, :].rearrange("(p t) c -> p t c", t=T), fill[:, :, :]).then_inc(zeroed, 16)
                    e.wait_ge(d, mark["node8"])
                    e.dma_start(node_d[:, :].rearrange("(t p) c -> p t c", p=P), node8[:, :, :]).then_inc(node_out, 16)
                    e.wait_ge(started, 16 * NT)
                    e.dma_start(fill[:, :, :], start_d[0:E_GAT, :].rearrange("(p t) c -> p t c", t=T)).then_inc(fill_in, 16)
                    for q in range(PARTS):
                        part = slice(q * T // PARTS, (q + 1) * T // PARTS)
                        e.wait_ge(d, mark["run", q])
                        e.dma_start(run20_d[:, :].rearrange("(p t) c -> p t c", t=T)[:, part, :], rec[:, part, :]).then_inc(run_out, 16)

                @block.gpsimd
                def _(e):
                    e.wait_ge(mx_out, 16)
                    for n in range(NT):
                        e.indirect_dma_start(out=mx_end[:, n, :], out_offset=None, in_=mx_d[:, :],
                                             in_offset=bass.IndirectOffsetOnAxis(ap=gat_last_i[:, n:n + 1], axis=0)).then_inc(ends_in, 16)
                    e.wait_ge(d, mark["node8"])
                    e.wait_ge(zeroed, 16)
                    for n in range(NT):
                        e.indirect_dma_start(out=start_d[:, :], out_offset=bass.IndirectOffsetOnAxis(ap=gat_start_i[:, n:n + 1], axis=0),
                                             in_=node8[:, n, :], in_offset=None).then_inc(started, 16)
                    e.wait_ge(node_out, 16)
                    e.indirect_dma_start(out=init[:, :], out_offset=None, in_=node_d[:, :],
                                         in_offset=bass.IndirectOffsetOnAxis(ap=first_node[:, 0:1], axis=0)).then_inc(init_in, 16)
                    e.wait_ge(run_out, 16 * PARTS)
                    for n in range(NT):
                        e.indirect_dma_start(out=tot[:, n, :], out_offset=None, in_=run20_d[:, :],
                                             in_offset=bass.IndirectOffsetOnAxis(ap=gat_last_i[:, n:n + 1], axis=0)).then_inc(run_in, 16)
                    e.wait_ge(run_in, 16 * NT)

        def gat_cross():
            C = 7
            CHUNKS = NT // C
            assert CHUNKS * C == NT
            with phase() as sc:
                rows = [sb(f"x_rows{k}", [P, 2, C * P], F32, sc) for k in range(2)]
                below, cross = ([sb(f"x_{n}{k}", [P, C * P], F32, sc) for k in range(2)] for n in ("below", "cross"))
                ps = [sc.enter_context(nc.psum_tensor(f"x_ps{k}", [P, 512], F32)) for k in range(2)]
                step, crossed = sem("x_step"), sem("x_crossed")
                rows_in = [sem(f"x_rows_in{k}") for k in range(2)]
                PER = 4
                with nc.Block() as block:
                    @block.sync
                    def _(e):
                        for c in range(CHUNKS):
                            k = c % 2
                            if c >= 2:
                                e.wait_ge(step, (c - 2) * PER + 2)
                            e.dma_start(rows[k][:, :, :], bounds_gat[:, c * C * P:(c + 1) * C * P].unsqueeze(0).to_broadcast([P, 2, C * P])).then_inc(rows_in[k], 16)

                    @block.vector
                    def _(e):
                        v = nc.vector
                        for c in range(CHUNKS):
                            k = c % 2
                            own = tot[:, c * C:(c + 1) * C, :]
                            st = Steps(e, step, c, PER)
                            e.wait_ge(rows_in[k], 16 * (c // 2 + 1))
                            if c >= 2:
                                e.wait_ge(crossed, c - 1)
                            st(v.tensor_scalar(below[k][:, :], rows[k][:, 0, :], split_gat[:, :], None, ALU.is_lt))
                            st.wait()
                            st(v.scalar_tensor_tensor(out=cross[k][:, :], in0=rows[k][:, 1, :], scalar=split_gat[:, :],
                                                      in1=below[k][:, :], op0=ALU.is_gt, op1=ALU.mult))
                            st(v.tensor_tensor(own, own, gat_has[:, c * C:(c + 1) * C].unsqueeze(2).to_broadcast([P, C, REC]), ALU.mult))
                            st.wait()
                            e.wait_ge(crossed, c + 1)
                            st(v.tensor_tensor(own, own, ps[k][:, 0:C * REC].rearrange("p (n c) -> p n c", c=REC), ALU.add))
                        e.wait_ge(step, PER * CHUNKS)

                    @block.tensor
                    def _(e):
                        for c in range(CHUNKS):
                            k = c % 2
                            e.wait_ge(step, c * PER + 2)
                            if c >= 2:
                                e.wait_ge(step, (c - 1) * PER)
                            for n in range(C):
                                m = nc.tensor.matmul(ps[k][:, n * REC:(n + 1) * REC], cross[k][:, n * P:(n + 1) * P], carry[:, 0:REC],
                                                     start=True, stop=True)
                            m.then_inc(crossed, 1)

        def gat_gates():
            with phase() as sc:
                exs, den, sq4 = (sb(f"q_{n}", [P, NT, HEADS], F32, sc) for n in ("exs", "den", "sq4"))
                num, sq = (sb(f"q_{n}", [P, NT, C16], F32, sc) for n in ("num", "sq"))
                score, cmp, place, pick = (sb(f"q_{n}", [P, NT, EXPERTS], F32, sc) for n in ("score", "cmp", "place", "pick"))
                mean, var, rs, best = (sb(f"q_{n}", [P, NT], F32, sc) for n in ("mean", "var", "rs", "best"))
                vec = {n: sb(f"q_v_{n}", [P, C16], F32, sc) for n in ("b_gat", "ln_gamma", "ln_beta")}
                vec_in, d, es_done, rooted, e2_done = (sem(f"q_{n}") for n in ("vec_in", "d", "es_done", "rooted", "e2_done"))
                mark = {}
                w16, w4 = [P, NT, C16], [P, NT, EXPERTS]
                with nc.Block() as block:
                    @block.sync
                    def _(e):
                        for n in vec:
                            e.dma_start(vec[n][:, :], a[f"L0_ffn_{n}"].unsqueeze(0).to_broadcast([P, C16])).then_inc(vec_in, 16)
                        e.wait_ge(vec_in, 48)

                    @block.vector
                    def _(e):
                        v = nc.vector
                        st = Steps(e, d, 0, 999)

                        def do(instruction):
                            st(instruction)
                            st.wait()

                        do(v.tensor_tensor(exs[:, :, :], a_src[:, :, :], a_dst[:, :, :], ALU.add))
                        do(v.scalar_tensor_tensor(out=exs[:, :, :], in0=exs[:, :, :], scalar=0.2, in1=exs[:, :, :], op0=ALU.mult, op1=ALU.max))
                        do(v.tensor_tensor(exs[:, :, :], exs[:, :, :], node8[:, :, HEADS:2 * HEADS], ALU.subtract))
                        mark["exs"] = st.k
                        e.wait_ge(es_done, 1)
                        do(v.tensor_tensor(den[:, :, :], tot[:, :, 0:HEADS], exs[:, :, :], ALU.add))
                        do(v.tensor_scalar(den[:, :, :], den[:, :, :], 1e-16, None, ALU.add))
                        do(v.reciprocal(den[:, :, :], den[:, :, :]))
                        for h in range(HEADS):
                            c = slice(EXPERTS * h, EXPERTS * (h + 1))
                            do(v.tensor_tensor(num[:, :, c], proj[:, :, c], exs[:, :, h:h + 1].to_broadcast(w4), ALU.mult))
                            do(v.tensor_tensor(num[:, :, c], num[:, :, c], tot[:, :, HEADS + EXPERTS * h:HEADS + EXPERTS * (h + 1)], ALU.add))
                            do(v.tensor_tensor(num[:, :, c], num[:, :, c], den[:, :, h:h + 1].to_broadcast(w4), ALU.mult))
                        e.wait_ge(vec_in, 48)
                        do(v.tensor_tensor(num[:, :, :], num[:, :, :], vec["b_gat"][:, :].unsqueeze(1).to_broadcast(w16), ALU.add))
                        do(v.reduce_sum(mean[:, :], num[:, :, :], REDUCE_LAST))
                        do(v.tensor_scalar(mean[:, :], mean[:, :], 1.0 / C16, None, ALU.mult))
                        do(v.tensor_tensor(num[:, :, :], num[:, :, :], spread(mean[:, :], w16), ALU.subtract))
                        do(v.tensor_tensor(sq[:, :, :], num[:, :, :], num[:, :, :], ALU.mult))
                        do(v.reduce_sum(var[:, :], sq[:, :, :], REDUCE_LAST))
                        do(v.tensor_scalar(var[:, :], var[:, :], 1.0 / C16, EPS, ALU.mult, ALU.add))
                        mark["var"] = st.k
                        e.wait_ge(rooted, 1)
                        do(v.tensor_tensor(num[:, :, :], num[:, :, :], spread(rs[:, :], w16), ALU.mult))
                        do(v.tensor_tensor(num[:, :, :], num[:, :, :], vec["ln_gamma"][:, :].unsqueeze(1).to_broadcast(w16), ALU.mult))
                        do(v.tensor_tensor(num[:, :, :], num[:, :, :], vec["ln_beta"][:, :].unsqueeze(1).to_broadcast(w16), ALU.add))
                        do(v.tensor_tensor(score[:, :, :], num[:, :, 0:4], num[:, :, 4:8], ALU.add))
                        do(v.tensor_tensor(score[:, :, :], score[:, :, :], num[:, :, 8:12], ALU.add))
                        do(v.tensor_tensor(score[:, :, :], score[:, :, :], num[:, :, 12:16], ALU.add))
                        do(v.tensor_scalar(score[:, :, :], score[:, :, :], 1.0 / HEADS, None, ALU.mult))
                        do(v.memset(place[:, :, :], 0.0))
                        for j in range(EXPERTS):
                            other = score[:, :, j:j + 1]
                            if j:
                                do(v.tensor_tensor(cmp[:, :, 0:j], other.to_broadcast([P, NT, j]), score[:, :, 0:j], ALU.is_gt))
                                do(v.tensor_tensor(place[:, :, 0:j], place[:, :, 0:j], cmp[:, :, 0:j], ALU.add))
                            m = EXPERTS - 1 - j
                            if m:
                                do(v.tensor_tensor(cmp[:, :, j + 1:EXPERTS], other.to_broadcast([P, NT, m]), score[:, :, j + 1:EXPERTS], ALU.is_ge))
                                do(v.tensor_tensor(place[:, :, j + 1:EXPERTS], place[:, :, j + 1:EXPERTS], cmp[:, :, j + 1:EXPERTS], ALU.add))
                        do(v.tensor_scalar(pick[:, :, :], place[:, :, :], 2.0, None, ALU.is_lt))
                        do(v.reduce_max(best[:, :], score[:, :, :], REDUCE_LAST))
                        do(v.tensor_tensor(score[:, :, :], score[:, :, :], spread(best[:, :], w4), ALU.subtract))
                        mark["score"] = st.k
                        e.wait_ge(e2_done, 1)
                        do(v.tensor_tensor(score[:, :, :], score[:, :, :], pick[:, :, :], ALU.mult))
                        do(v.reduce_sum(best[:, :], score[:, :, :], REDUCE_LAST))
                        do(v.reciprocal(best[:, :], best[:, :]))
                        do(v.tensor_tensor(gates[:, :, :], score[:, :, :], spread(best[:, :], w4), ALU.mult))

                    @block.scalar
                    def _(e):
                        e.wait_ge(d, mark["exs"])
                        nc.scalar.activation(exs[:, :, :], exs[:, :, :], ACT.Exp).then_inc(es_done, 1)
                        e.wait_ge(d, mark["score"])
                        nc.scalar.activation(score[:, :, :], score[:, :, :], ACT.Exp).then_inc(e2_done, 1)

                    @block.gpsimd
                    def _(e):
                        e.wait_ge(d, mark["var"])
                        e.tensor_tensor(rs[:, :], var[:, :], minus_half[:, :].to_broadcast([P, NT]), ALU.pow).then_inc(rooted, 1)

        def experts_and_gather(srt, rec):
            FC = FF // P
            with phase() as sc:
                fetch, file = gat_gather(srt, rec, sc)
                w1 = sb("f_w1", [P, EXPERTS, 2, FF], F32, sc)
                w2 = sb("f_w2", [P, EXPERTS, FC, D], F32, sc)
                b1 = sb("f_b1", [P, EXPERTS, FC], F32, sc)
                b2 = sb("f_b2", [1, EXPERTS, D], F32, sc)
                xf = [sb(f"f_xf{k}", [P, 2, D], F32, sc) for k in range(2)]
                y = sb("f_y", [P, 2, EXPERTS, D], F32, sc)
                xT = sb("f_xT", [P, 2, 2 * P], F32, sc)
                hid = [sb(f"f_hid{j}", [P, FC, 2 * P], F32, sc) for j in range(2)]
                psT = sc.enter_context(nc.psum_tensor("f_psT", [P, 512], F32))
                psU = [sc.enter_context(nc.psum_tensor(f"f_psU{j}", [P, 512], F32)) for j in range(3)]
                psY = [sc.enter_context(nc.psum_tensor(f"f_psY{j}", [P, 2, D], F32)) for j in range(2)]
                w_in, b_in, turned, xT_ready, up, hidden, down, copied, held, y_kept = (
                    sem(f"f_{n}") for n in ("w_in", "b_in", "turned", "xT_ready", "up", "hidden", "down", "copied", "held", "y_kept"))
                tile_in = [sem(f"f_tile_in{k}") for k in range(2)]
                PAIRS = -(-NT // 2)
                UP, DOWN = EXPERTS * FC, EXPERTS

                def over_pairs(eng, body):
                    body(0, 0, 2)
                    body(0, 1, 2)
                    with eng.Fori(1, PAIRS // 2) as i:
                        for k in range(2):
                            body(i, k, 2)
                    body(PAIRS // 2, 0, 1)
                assert PAIRS % 2 == 1 and NT % 2 == 1

                with nc.Block() as block:
                    block.gpsimd(fetch)
                    block.vector(file)

                    @block.sync
                    def _(e):
                        for x in range(EXPERTS):
                            e.dma_start(w1[:, x, :, :], a["L0_ffn_W1"][x].rearrange("(c p) f -> p c f", p=P)).then_inc(w_in, 16)
                            e.dma_start(w2[:, x, :, :], a["L0_ffn_W2"][x].rearrange("(c p) d -> p c d", p=P)).then_inc(w_in, 16)
                        with nc.allow_non_contiguous_dma(reason="2048 words, once"):
                            e.dma_start(b1[:, :, :], a["L0_ffn_b1"].rearrange("q (c p) -> p q c", p=P)).then_inc(b_in, 16)
                        e.dma_start(b2[:, :, :], a["L0_ffn_b2"].unsqueeze(0)).then_inc(b_in, 16)

                        def load(i, k, m):
                            q = 2 * i + k
                            if later(i):
                                e.wait_ge(turned, q - 1)
                                e.sem_inc(held, 1)
                            e.dma_start(xf[k][:, 0:m, :], xf_d[bass.ds(q * 2 * P, m * P), :].rearrange("(m p) c -> p m c", p=P)).then_inc(tile_in[k], 16)
                        over_pairs(e, load)

                    @block.tensor
                    def _(e):
                        e.wait_ge(w_in, 32 * EXPERTS)
                        e.wait_ge(b_in, 32)

                        def body(i, k, m):
                            q = 2 * i + k
                            cols = m * P
                            e.wait_ge(tile_in[k], 16 * (i + 1))
                            if later(i) or k:
                                e.wait_ge(xT_ready, q)
                            for j in range(m):
                                for c in range(2):
                                    t = nc.tensor.transpose(psT[:, c * 2 * P + j * P:c * 2 * P + (j + 1) * P], xf[k][:, j, c * P:(c + 1) * P], ident[:, :])
                            t.then_inc(turned, 1)
                            e.wait_ge(xT_ready, q + 1)

                            def going_up(x):
                                for f in range(FC):
                                    u = FC * x + f
                                    if u >= 3:
                                        e.wait_ge(hidden, q * UP + u - 2)
                                    elif later(i) or k:
                                        e.wait_ge(hidden, q * UP)
                                    for c in range(2):
                                        t = nc.tensor.matmul(psU[u % 3][:, 0:cols], w1[:, x, c, f * P:(f + 1) * P], xT[:, c, 0:cols],
                                                             start=(c == 0), stop=(c == 1))
                                    t.then_inc(up, 1)

                            def going_down(x):
                                e.wait_ge(hidden, q * UP + FC * (x + 1))
                                if later(i) or k or x >= 2:
                                    e.wait_ge(copied, q * DOWN + x - 1)
                                for j in range(m):
                                    nc.tensor.matmul(psY[x % 2][:, j, :], ones[0:1, :], b2[0:1, x, :], start=True, stop=False)
                                    for f in range(FC):
                                        t = nc.tensor.matmul(psY[x % 2][:, j, :], hid[x % 2][:, f, j * P:(j + 1) * P], w2[:, x, f, :],
                                                             start=False, stop=(f == FC - 1))
                                t.then_inc(down, 1)
                            going_up(0)
                            for x in range(1, EXPERTS):
                                going_up(x)
                                going_down(x - 1)
                            going_down(EXPERTS - 1)
                        over_pairs(e, body)

                    @block.scalar
                    def _(e):
                        e.wait_ge(b_in, 32)

                        def body(i, k, m):
                            q = 2 * i + k
                            cols = m * P
                            e.wait_ge(turned, q + 1)
                            if later(i) or k:
                                e.wait_ge(up, q * UP)
                            nc.scalar.activation(xT[:, :, 0:cols], psT[:, :].rearrange("p (c n) -> p c n", c=2)[:, :, 0:cols], ACT.Copy).then_inc(xT_ready, 1)

                            def gelus(x):
                                if later(i) or k or x >= 2:
                                    e.wait_ge(down, q * DOWN + x - 1)
                                for f in range(FC):
                                    u = FC * x + f
                                    e.wait_ge(up, q * UP + u + 1)
                                    nc.scalar.activation(hid[x % 2][:, f, 0:cols], psU[u % 3][:, 0:cols], ACT.Gelu,
                                                         bias=b1[:, x, f:f + 1]).then_inc(hidden, 1)

                            def copy_out(x):
                                e.wait_ge(down, q * DOWN + x + 1)
                                if x == 0 and (later(i) or k):
                                    e.wait_ge(y_kept, 16 * q)
                                nc.scalar.activation(y[:, 0:m, x, :], psY[x % 2][:, 0:m, :], ACT.Copy).then_inc(copied, 1)
                            gelus(0)
                            gelus(1)
                            for x in range(2, EXPERTS):
                                copy_out(x - 2)
                                gelus(x)
                            copy_out(EXPERTS - 2)
                            copy_out(EXPERTS - 1)
                            e.wait_ge(copied, (q + 1) * DOWN)
                            e.sem_inc(held, 1)
                            e.dma_start(y_d[bass.ds(q * 2 * P, m * P), :, :].rearrange("(m p) x c -> p m x c", p=P) if m > 1 else
                                        y_d[bass.ds(q * 2 * P, P), :, :], y[:, 0:m, :, :] if m > 1 else y[:, 0, :, :]).then_inc(y_kept, 16)
                        over_pairs(e, body)
                        e.wait_ge(y_kept, 16 * PAIRS)

        def combine():
            SLOTS = 4

            def over_slots(eng, body):
                for k in range(SLOTS):
                    body(0, k)
                with eng.Fori(1, NT // SLOTS) as i:
                    for k in range(SLOTS):
                        body(i, k)
                for k in range(NT % SLOTS):
                    body(NT // SLOTS, k)

            with phase() as sc:
                y = [sb(f"o_y{k}", [P, EXPERTS, D], F32, sc) for k in range(SLOTS)]
                acc = [sb(f"o_acc{k}", [P, D], F32, sc) for k in range(SLOTS)]
                step, held = sem("o_step"), sem("o_held")
                tile_in = [sem(f"o_tile_in{k}") for k in range(SLOTS)]
                out_kept = [sem(f"o_out_kept{k}") for k in range(SLOTS)]
                with nc.Block() as block:
                    @block.sync
                    def _(e):
                        def body(i, k):
                            n = SLOTS * i + k
                            if later(i):
                                e.wait_ge(step, (n - SLOTS + 1) * EXPERTS)
                                e.sem_inc(held, 1)
                                e.wait_ge(out_kept[k], 16 * i)
                                e.sem_inc(held, 1)
                            e.dma_start(y[k][:, :, :], y_d[bass.ds(n * P, P), :, :]).then_inc(tile_in[k], 16)
                            e.dma_start(acc[k][:, :], x2_d[bass.ds(n * P, P), :]).then_inc(tile_in[k], 16)
                        over_slots(e, body)

                    @block.vector
                    def _(e):
                        def body(i, k):
                            n = SLOTS * i + k
                            st = Steps(e, step, n, EXPERTS)
                            e.wait_ge(tile_in[k], 32 * (i + 1))
                            for x in range(EXPERTS):
                                st.wait()
                                st(nc.vector.scalar_tensor_tensor(out=acc[k][:, :], in0=y[k][:, x, :], scalar=gates[:, bass.ds(n, 1), x],
                                                                  in1=acc[k][:, :], op0=ALU.mult, op1=ALU.add))
                        over_slots(e, body)

                    @block.scalar
                    def _(e):
                        def body(i, k):
                            n = SLOTS * i + k
                            rows = P if not isinstance(n, int) or n < NT - 1 else N - n * P
                            e.wait_ge(step, (n + 1) * EXPERTS)
                            e.sem_inc(held, 1)
                            e.dma_start(out[bass.ds(n * P, rows), :], acc[k][0:rows, :]).then_inc(out_kept[k], 16)
                        over_slots(e, body)
                        for k in range(SLOTS):
                            e.wait_ge(out_kept[k], 16 * -(-(NT - k) // SLOTS))

        with phase() as gs:
            tot = sb("tot", [P, NT, REC], F32, gs)
            node8 = sb("node8", [P, NT, 2 * HEADS], F32, gs)
            srt = sb("srt", [P, T_GAT, 2], I32, gs)
            with phase() as g2:
                gat_records(g2, srt)
            with phase() as g3:
                rec = sb("rec", [P, T_GAT, REC], F32, g3)
                experts_and_gather(srt, rec)
                gat_softmax(srt, rec, g3)
            gat_cross()
            gat_gates()
        combine()


def kernel(**inputs):
    import numpy as _np
    import concourse.bacc as _bacc
    from concourse import mybir as _mybir
    from concourse.bass_utils import run_bass_kernel_spmd as _run

    nc = _bacc.Bacc("TRN2", target_bir_lowering=False, num_devices=1)
    arrays, args = {}, {}
    for name, value in inputs.items():
        v = _np.ascontiguousarray(value)
        arrays[f"in_{name}"] = v
        args[name] = nc.dram_tensor(f"in_{name}", v.shape, _mybir.dt.from_np(v.dtype), kind="ExternalInput").ap()
    out = nc.dram_tensor("out_0", (N, D), F32, kind="ExternalOutput").ap()
    build(nc, args, out)
    r = _run(nc, [arrays], core_ids=[0])
    return r.results[0]["out_0"]
```
